# Optimizing a Trainium2 kernel written in Bass

```python
import numpy as np
import jax
import jax.numpy as jnp

def _softmax(x, axis=-1):
    return jax.nn.softmax(x, axis=axis)

def _gelu(x):
    return jax.nn.gelu(x, approximate=True)

def _silu(x):
    return jax.nn.silu(x)

def _sigmoid(x):
    return jax.nn.sigmoid(x)

def _layernorm(x, axis=-1, eps=1e-05):
    m = jnp.mean(x, axis=axis, keepdims=True)
    v = jnp.var(x, axis=axis, keepdims=True)
    return (x - m) / jnp.sqrt(v + eps)

def _scatter_add(tgt, idx, src, axis=0):
    return tgt.at[idx].add(src)

def _segment_sum(src, seg, n):
    return jax.ops.segment_sum(src, seg, n)
kernel_name = 'mk_adj_ffn_d4_adj_r2_285742'

def setup_inputs(seed: int=0):
    np.random.seed(seed)
    _w = jnp.asarray

    def _rec_inputs():
        import jax
        import jax.numpy as jnp
        _gk = jax.random.key(seed)
        x = -0.0005207 + 1.001 * jax.random.normal(jax.random.fold_in(_gk, 1), (4096, 128), jnp.float32)
        _w = (1.0 + jnp.arange(4096, dtype=jnp.float32)) ** (-0.5)
        _w = _w / _w.mean()
        _pij = jnp.clip(0.000488281 * _w[:, None] * _w[None, :], 0.0, 1.0)
        _a = jax.random.uniform(jax.random.fold_in(_gk, 2), (4096, 4096)) < _pij
        adj = _a.astype(jnp.int32)
        return (x, adj)
    x, adj = _rec_inputs()

    def _L0_gnn_setup():
        import jax, jax.numpy as jnp
        import numpy as np
        ALPHA = 0.2
        NEG_FILL = -9000000000000000.0
        key = jax.random.key(seed)
        k_h, k_adj, k_W, k_a = jax.random.split(key, 4)
        N, D_IN, D_OUT = (4096, 128, 128)
        h = jax.random.normal(k_h, (N, D_IN), dtype=jnp.float32)
        adj = jax.random.randint(k_adj, (N, N), 0, 2, dtype=jnp.int32)
        W = jax.random.normal(k_W, (D_IN, D_OUT), dtype=jnp.float32) * (1.414 * np.sqrt(2.0 / (D_IN + D_OUT)))
        a = jax.random.normal(k_a, (2 * D_OUT, 1), dtype=jnp.float32) * (1.414 * np.sqrt(2.0 / (2 * D_OUT + 1)))
        return {'h': h, 'adj': adj, 'W': W, 'a': a}
    _L0_gnn_all = _L0_gnn_setup()
    _L0_gnn_in = {k: v for k, v in _L0_gnn_all.items() if k in ('W', 'a')}
    del _L0_gnn_all

    def _L0_ffn_setup():
        import jax, jax.numpy as jnp
        import numpy as np
        B, T, C = (64, 192, 128)
        NH, NKV = (4, 2)
        HD = C // NH
        NREP = NH // NKV
        NE, TOPK = (8, 2)
        HID = int(8 / 3 * C)
        EPS_RMS = 1e-06

        def _rope_tables(t_len):
            inv_freq = 1.0 / 10000.0 ** (np.arange(0, HD, 2, dtype=np.float32) / HD)
            t = np.arange(t_len, dtype=np.float32)
            freqs = np.outer(t, inv_freq)
            emb = np.concatenate([freqs, freqs], axis=-1)
            return (jnp.asarray(np.cos(emb)), jnp.asarray(np.sin(emb)))

        def _rotate_half(x):
            h = x.shape[-1] // 2
            return jnp.concatenate([-x[..., h:], x[..., :h]], axis=-1)

        def _rmsnorm(v, w):
            return v * jax.lax.rsqrt(jnp.mean(v * v, axis=-1, keepdims=True) + EPS_RMS) * w
        key = jax.random.key(seed)
        ks = jax.random.split(key, 10)
        s = lambda k, shape: jax.random.normal(k, shape, jnp.float32) * 0.02
        return {'x': jax.random.normal(ks[0], (B, T, C), jnp.float32), 'ln1_w': jnp.ones((C,), jnp.float32), 'ln2_w': jnp.ones((C,), jnp.float32), 'wq': s(ks[1], (NH * HD, C)), 'wk': s(ks[2], (NKV * HD, C)), 'wv': s(ks[3], (NKV * HD, C)), 'wo': s(ks[4], (C, C)), 'router_w': s(ks[5], (NE, C)), 'w1': s(ks[6], (NE, HID, C)), 'w2': s(ks[7], (NE, C, HID)), 'w3': s(ks[8], (NE, HID, C))}
    _L0_ffn_all = _L0_ffn_setup()
    _L0_ffn_in = {k: v for k, v in _L0_ffn_all.items() if k in ('ln1_w', 'ln2_w', 'wq', 'wk', 'wv', 'wo', 'router_w', 'w1', 'w2', 'w3')}
    del _L0_ffn_all

    def _L1_gnn_setup():
        import jax, jax.numpy as jnp
        import numpy as np
        N, F_IN, F_OUT = (4096, 128, 128)
        ALPHA = 0.2
        NEG = -9000000000000000.0
        key = jax.random.key(seed)
        k1, k2, k3, k4, k5 = jax.random.split(key, 5)
        h = jax.random.normal(k1, (N, F_IN), dtype=jnp.float32)
        adj = jax.random.randint(k2, (N, N), 0, 2, dtype=jnp.int32)
        W_w = jax.random.normal(k3, (F_IN, F_OUT), dtype=jnp.float32) / np.sqrt(F_IN)
        W_b = jax.random.normal(k4, (F_OUT,), dtype=jnp.float32) * 0.01
        a = jax.random.normal(k5, (2 * F_OUT, 1), dtype=jnp.float32) / np.sqrt(2 * F_OUT)
        return {'h': h, 'adj': adj, 'W_w': W_w, 'W_b': W_b, 'a': a}
    _L1_gnn_all = _L1_gnn_setup()
    _L1_gnn_in = {k: v for k, v in _L1_gnn_all.items() if k in ('W_w', 'W_b', 'a')}
    del _L1_gnn_all

    def _L1_ffn_setup():
        import jax, jax.numpy as jnp
        import numpy as np
        E, D, H, TOP_K = (6, 128, 128, 2)
        ROUTER_H = D // 2
        key = jax.random.key(seed)
        ks = jax.random.split(key, 12)
        s = 1.0 / np.sqrt(D)
        sh = 1.0 / np.sqrt(H)
        sr = 1.0 / np.sqrt(ROUTER_H)
        return {'features': jax.random.normal(ks[0], (8, 2048, D), dtype=jnp.float32), 'router_w1': jax.random.uniform(ks[1], (D, ROUTER_H), jnp.float32, -s, s), 'router_b1': jnp.zeros((ROUTER_H,), jnp.float32), 'router_w2': jax.random.uniform(ks[2], (ROUTER_H, E), jnp.float32, -sr, sr), 'router_b2': jnp.zeros((E,), jnp.float32), 'expert_w1': jax.random.uniform(ks[3], (E, D, H), jnp.float32, -s, s), 'expert_b1': jnp.zeros((E, H), jnp.float32), 'expert_w2': jax.random.uniform(ks[4], (E, H, H), jnp.float32, -sh, sh), 'expert_b2': jnp.zeros((E, H), jnp.float32), 'expert_w3': jax.random.uniform(ks[5], (E, H, D), jnp.float32, -sh, sh), 'expert_b3': jnp.zeros((E, D), jnp.float32)}
    _L1_ffn_all = _L1_ffn_setup()
    _L1_ffn_in = {k: v for k, v in _L1_ffn_all.items() if k in ('router_w1', 'router_b1', 'router_w2', 'router_b2', 'expert_w1', 'expert_b1', 'expert_w2', 'expert_b2', 'expert_w3', 'expert_b3')}
    del _L1_ffn_all

    def _L2_gnn_setup():
        import jax, jax.numpy as jnp
        import numpy as np
        N, D_IN, D_OUT = (5000, 128, 128)
        key = jax.random.key(seed)
        k1, k2, k3, k4 = jax.random.split(key, 4)

        def xavier(k, shape, gain=1.414):
            fan_in, fan_out = (shape[0], shape[1])
            bound = gain * np.sqrt(6.0 / (fan_in + fan_out))
            return jax.random.uniform(k, shape, jnp.float32, -bound, bound)
        return {'input': jax.random.normal(k1, (N, D_IN), jnp.float32), 'adj': jax.random.randint(k2, (N, N), 0, 2, jnp.int32), 'M': N, 'W': xavier(k3, (D_IN, D_OUT)), 'b': jnp.zeros((D_OUT,), jnp.float32), 'a': xavier(k4, (D_OUT, 1))}
    _L2_gnn_all = _L2_gnn_setup()
    _L2_gnn_in = {k: v for k, v in _L2_gnn_all.items() if k in ('W', 'b', 'a')}
    del _L2_gnn_all

    def _L2_ffn_setup():
        import jax, jax.numpy as jnp
        import numpy as np
        D_MODEL = 128
        EXPERT_DIM = 256
        NUM_EXPERTS = 8
        TOP_K = 2
        SEQ_LEN = 1024
        BATCH = 2
        key = jax.random.key(seed)
        ks = jax.random.split(key, 8)
        s = 0.02
        x = jax.random.normal(ks[0], (SEQ_LEN, BATCH, D_MODEL), dtype=jnp.float32)
        Wg = jax.random.normal(ks[1], (D_MODEL, NUM_EXPERTS), dtype=jnp.float32) * s
        bg = jax.random.normal(ks[2], (NUM_EXPERTS,), dtype=jnp.float32) * s
        bias = jnp.zeros((NUM_EXPERTS,), dtype=jnp.float32)
        W1 = jax.random.normal(ks[3], (NUM_EXPERTS, D_MODEL, EXPERT_DIM), dtype=jnp.float32) * s
        b1 = jax.random.normal(ks[4], (NUM_EXPERTS, EXPERT_DIM), dtype=jnp.float32) * s
        W2 = jax.random.normal(ks[5], (NUM_EXPERTS, EXPERT_DIM, D_MODEL), dtype=jnp.float32) * s
        b2 = jax.random.normal(ks[6], (NUM_EXPERTS, D_MODEL), dtype=jnp.float32) * s
        return {'x': x, 'Wg': Wg, 'bg': bg, 'bias': bias, 'W1': W1, 'b1': b1, 'W2': W2, 'b2': b2}
    _L2_ffn_all = _L2_ffn_setup()
    _L2_ffn_in = {k: v for k, v in _L2_ffn_all.items() if k in ('Wg', 'bg', 'bias', 'W1', 'b1', 'W2', 'b2')}
    del _L2_ffn_all

    def _L3_gnn_setup():
        import jax, jax.numpy as jnp
        import numpy as np
        N = 4096
        D_IN = 128
        D_OUT = 128
        NEG_INF = -9000000000000000.0
        key = jax.random.key(seed)
        k1, k2, k3, k4 = jax.random.split(key, 4)
        node_features = jax.random.normal(k1, (N, D_IN), dtype=jnp.float32)
        adjacency_matrix = jax.random.randint(k2, (N, N), 0, 2, dtype=jnp.int32)
        W = jax.random.normal(k3, (D_OUT, D_IN), dtype=jnp.float32) / np.sqrt(D_IN)
        b_W = jnp.zeros((D_OUT,), dtype=jnp.float32)
        a_vec = jax.random.normal(k4, (2 * D_OUT,), dtype=jnp.float32) / np.sqrt(2 * D_OUT)
        b_a = jnp.zeros((1,), dtype=jnp.float32)
        return {'node_features': node_features, 'adjacency_matrix': adjacency_matrix, 'W': W, 'b_W': b_W, 'a_vec': a_vec, 'b_a': b_a}
    _L3_gnn_all = _L3_gnn_setup()
    _L3_gnn_in = {k: v for k, v in _L3_gnn_all.items() if k in ('W', 'b_W', 'a_vec', 'b_a')}
    del _L3_gnn_all

    def _L3_ffn_setup():
        import jax, jax.numpy as jnp
        import numpy as np
        B, S, D, E, H, K = (4, 2048, 128, 8, 256, 2)
        key = jax.random.key(seed)
        ks = jax.random.split(key, 6)
        x = jax.random.normal(ks[0], (B, S, D), jnp.float32)
        Wg = jax.random.normal(ks[1], (D, E), jnp.float32) * 0.02
        bg = jnp.zeros((E,), jnp.float32)
        W1 = jax.random.normal(ks[2], (E, D, H), jnp.float32) * 0.02
        b1 = jnp.zeros((E, H), jnp.float32)
        W2 = jax.random.normal(ks[3], (E, H, D), jnp.float32) * 0.02
        b2 = jnp.zeros((E, D), jnp.float32)
        return {'x': x, 'Wg': Wg, 'bg': bg, 'W1': W1, 'b1': b1, 'W2': W2, 'b2': b2}
    _L3_ffn_all = _L3_ffn_setup()
    _L3_ffn_in = {k: v for k, v in _L3_ffn_all.items() if k in ('Wg', 'bg', 'W1', 'b1', 'W2', 'b2')}
    del _L3_ffn_all
    return {'x': x, 'adj': adj, 'L0_gnn_W': _L0_gnn_in['W'], 'L0_gnn_a': _L0_gnn_in['a'], 'L0_ffn_ln1_w': _L0_ffn_in['ln1_w'], 'L0_ffn_ln2_w': _L0_ffn_in['ln2_w'], 'L0_ffn_wq': _L0_ffn_in['wq'], 'L0_ffn_wk': _L0_ffn_in['wk'], 'L0_ffn_wv': _L0_ffn_in['wv'], 'L0_ffn_wo': _L0_ffn_in['wo'], 'L0_ffn_router_w': _L0_ffn_in['router_w'], 'L0_ffn_w1': _L0_ffn_in['w1'], 'L0_ffn_w2': _L0_ffn_in['w2'], 'L0_ffn_w3': _L0_ffn_in['w3'], 'L1_gnn_W_w': _L1_gnn_in['W_w'], 'L1_gnn_W_b': _L1_gnn_in['W_b'], 'L1_gnn_a': _L1_gnn_in['a'], 'L1_ffn_router_w1': _L1_ffn_in['router_w1'], 'L1_ffn_router_b1': _L1_ffn_in['router_b1'], 'L1_ffn_router_w2': _L1_ffn_in['router_w2'], 'L1_ffn_router_b2': _L1_ffn_in['router_b2'], 'L1_ffn_expert_w1': _L1_ffn_in['expert_w1'], 'L1_ffn_expert_b1': _L1_ffn_in['expert_b1'], 'L1_ffn_expert_w2': _L1_ffn_in['expert_w2'], 'L1_ffn_expert_b2': _L1_ffn_in['expert_b2'], 'L1_ffn_expert_w3': _L1_ffn_in['expert_w3'], 'L1_ffn_expert_b3': _L1_ffn_in['expert_b3'], 'L2_gnn_W': _L2_gnn_in['W'], 'L2_gnn_b': _L2_gnn_in['b'], 'L2_gnn_a': _L2_gnn_in['a'], 'L2_ffn_Wg': _L2_ffn_in['Wg'], 'L2_ffn_bg': _L2_ffn_in['bg'], 'L2_ffn_bias': _L2_ffn_in['bias'], 'L2_ffn_W1': _L2_ffn_in['W1'], 'L2_ffn_b1': _L2_ffn_in['b1'], 'L2_ffn_W2': _L2_ffn_in['W2'], 'L2_ffn_b2': _L2_ffn_in['b2'], 'L3_gnn_W': _L3_gnn_in['W'], 'L3_gnn_b_W': _L3_gnn_in['b_W'], 'L3_gnn_a_vec': _L3_gnn_in['a_vec'], 'L3_gnn_b_a': _L3_gnn_in['b_a'], 'L3_ffn_Wg': _L3_ffn_in['Wg'], 'L3_ffn_bg': _L3_ffn_in['bg'], 'L3_ffn_W1': _L3_ffn_in['W1'], 'L3_ffn_b1': _L3_ffn_in['b1'], 'L3_ffn_W2': _L3_ffn_in['W2'], 'L3_ffn_b2': _L3_ffn_in['b2']}

def reference(x, adj, L0_gnn_W, L0_gnn_a, L0_ffn_ln1_w, L0_ffn_ln2_w, L0_ffn_wq, L0_ffn_wk, L0_ffn_wv, L0_ffn_wo, L0_ffn_router_w, L0_ffn_w1, L0_ffn_w2, L0_ffn_w3, L1_gnn_W_w, L1_gnn_W_b, L1_gnn_a, L1_ffn_router_w1, L1_ffn_router_b1, L1_ffn_router_w2, L1_ffn_router_b2, L1_ffn_expert_w1, L1_ffn_expert_b1, L1_ffn_expert_w2, L1_ffn_expert_b2, L1_ffn_expert_w3, L1_ffn_expert_b3, L2_gnn_W, L2_gnn_b, L2_gnn_a, L2_ffn_Wg, L2_ffn_bg, L2_ffn_bias, L2_ffn_W1, L2_ffn_b1, L2_ffn_W2, L2_ffn_b2, L3_gnn_W, L3_gnn_b_W, L3_gnn_a_vec, L3_gnn_b_a, L3_ffn_Wg, L3_ffn_bg, L3_ffn_W1, L3_ffn_b1, L3_ffn_W2, L3_ffn_b2):
    import jax
    import jax.numpy as jnp

    def _L0_gnn_ref(h, adj, W, a):
        import jax, jax.numpy as jnp
        import numpy as np
        ALPHA = 0.2
        NEG_FILL = -9000000000000000.0
        d_out = W.shape[1]
        Wh = h @ W
        Wh1 = Wh @ a[:d_out]
        Wh2 = Wh @ a[d_out:]
        e = Wh1 + Wh2.T
        e = jnp.where(e > 0, e, ALPHA * e)
        scores = jnp.where(adj > 0, e, NEG_FILL)
        attention = jax.nn.softmax(scores, axis=1)
        h_prime = attention @ Wh
        return jax.nn.elu(h_prime)

    def _L0_ffn_ref(x, ln1_w, ln2_w, wq, wk, wv, wo, router_w, w1, w2, w3):
        import jax, jax.numpy as jnp
        import numpy as np
        B, T, C = (64, 192, 128)
        NH, NKV = (4, 2)
        HD = C // NH
        NREP = NH // NKV
        NE, TOPK = (8, 2)
        HID = int(8 / 3 * C)
        EPS_RMS = 1e-06

        def _rope_tables(t_len):
            inv_freq = 1.0 / 10000.0 ** (np.arange(0, HD, 2, dtype=np.float32) / HD)
            t = np.arange(t_len, dtype=np.float32)
            freqs = np.outer(t, inv_freq)
            emb = np.concatenate([freqs, freqs], axis=-1)
            return (jnp.asarray(np.cos(emb)), jnp.asarray(np.sin(emb)))

        def _rotate_half(x):
            h = x.shape[-1] // 2
            return jnp.concatenate([-x[..., h:], x[..., :h]], axis=-1)

        def _rmsnorm(v, w):
            return v * jax.lax.rsqrt(jnp.mean(v * v, axis=-1, keepdims=True) + EPS_RMS) * w
        Bx, Tx, Cx = x.shape
        h = _rmsnorm(x, ln1_w)
        q = (h @ wq.T).reshape(Bx, Tx, NH, HD).transpose(0, 2, 1, 3)
        k = (h @ wk.T).reshape(Bx, Tx, NKV, HD).transpose(0, 2, 1, 3)
        v = (h @ wv.T).reshape(Bx, Tx, NKV, HD).transpose(0, 2, 1, 3)
        cos, sin = _rope_tables(Tx)
        cos, sin = (cos[None, None], sin[None, None])
        q = q * cos + _rotate_half(q) * sin
        k = k * cos + _rotate_half(k) * sin
        k = jnp.repeat(k, NREP, axis=1)
        v = jnp.repeat(v, NREP, axis=1)
        scores = jnp.einsum('bhtd,bhsd->bhts', q, k) / jnp.sqrt(jnp.float32(HD))
        causal = jnp.tril(jnp.ones((Tx, Tx), dtype=bool))
        scores = jnp.where(causal[None, None], scores, jnp.float32(-1e+30))
        att = jax.nn.softmax(scores, axis=-1)
        y = jnp.einsum('bhts,bhsd->bhtd', att, v).transpose(0, 2, 1, 3).reshape(Bx, Tx, Cx)
        x = x + y @ wo.T
        flat = _rmsnorm(x, ln2_w).reshape(-1, Cx)
        probs = jax.nn.softmax(flat @ router_w.T, axis=-1)
        tp, ti = jax.lax.top_k(probs, TOPK)
        tp = tp / (jnp.sum(tp, axis=-1, keepdims=True) + 1e-09)
        weights = jnp.sum(tp[..., None] * jax.nn.one_hot(ti, NE, dtype=flat.dtype), axis=1)
        out = jnp.zeros_like(flat)
        for e in range(NE):
            hh = jax.nn.silu(flat @ w1[e].T) * (flat @ w3[e].T)
            out = out + weights[:, e:e + 1] * (hh @ w2[e].T)
        return x + out.reshape(Bx, Tx, Cx)

    def _L1_gnn_ref(h, adj, W_w, W_b, a):
        import jax, jax.numpy as jnp
        import numpy as np
        N, F_IN, F_OUT = (4096, 128, 128)
        ALPHA = 0.2
        NEG = -9000000000000000.0
        Wh = h @ W_w + W_b
        a1 = a[:F_OUT, 0]
        a2 = a[F_OUT:, 0]
        e = jax.nn.leaky_relu((Wh @ a1)[:, None] + (Wh @ a2)[None, :], negative_slope=ALPHA)
        attention = jnp.where(adj > 0, e, NEG)
        attention = jax.nn.softmax(attention, axis=1)
        h_prime = attention @ Wh
        return h_prime

    def _L1_ffn_ref(features, router_w1, router_b1, router_w2, router_b2, expert_w1, expert_b1, expert_w2, expert_b2, expert_w3, expert_b3):
        import jax, jax.numpy as jnp
        import numpy as np
        E, D, H, TOP_K = (6, 128, 128, 2)
        ROUTER_H = D // 2
        rh = jax.nn.relu(features @ router_w1 + router_b1)
        expert_logits = jax.nn.softmax(rh @ router_w2 + router_b2, axis=-1)
        top_w, top_i = jax.lax.top_k(expert_logits, TOP_K)
        routing_weights = jax.nn.softmax(top_w, axis=-1)
        h1 = jax.nn.relu(jnp.einsum('bsd,edh->bseh', features, expert_w1) + expert_b1)
        h2 = jax.nn.relu(jnp.einsum('bseh,ehf->bsef', h1, expert_w2) + expert_b2)
        expert_out = jnp.einsum('bsef,efo->bseo', h2, expert_w3) + expert_b3
        sel = jnp.take_along_axis(expert_out, top_i[:, :, :, None], axis=2)
        combined = jnp.sum(sel * routing_weights[..., None], axis=2)
        return combined

    def _L2_gnn_ref(input, adj, M, W, b, a):
        import jax, jax.numpy as jnp
        import numpy as np
        N, D_IN, D_OUT = (5000, 128, 128)
        h = jnp.tanh(input @ W + b)
        inp = input @ W
        e = (h @ a)[:, 0]
        valid = jnp.sum(h, axis=1) != 0
        mask = (adj[:M] > 0) & valid[None, :]
        neg = jnp.asarray(-1e+30, h.dtype)
        scores = jnp.where(mask, e[None, :], neg)
        m = jnp.max(scores, axis=1, keepdims=True)
        w = jnp.where(mask, jnp.exp(scores - m), 0.0)
        denom = jnp.sum(w, axis=1, keepdims=True)
        att = w / jnp.maximum(denom, 1e-30)
        return att @ inp

    def _L2_ffn_ref(x, Wg, bg, bias, W1, b1, W2, b2):
        import jax, jax.numpy as jnp
        import numpy as np
        D_MODEL = 128
        EXPERT_DIM = 256
        NUM_EXPERTS = 8
        TOP_K = 2
        SEQ_LEN = 1024
        BATCH = 2
        x_flat = x.reshape(-1, D_MODEL)
        gate_logits = x_flat @ Wg + bg + bias
        topk_vals, topk_idx = jax.lax.top_k(gate_logits, TOP_K)
        topk_w = jax.nn.softmax(topk_vals, axis=-1)
        combine = (jax.nn.one_hot(topk_idx, NUM_EXPERTS, dtype=x.dtype) * topk_w[..., None]).sum(axis=1)
        h = jax.nn.relu(jnp.einsum('td,edh->teh', x_flat, W1) + b1)
        y = jnp.einsum('teh,ehd->ted', h, W2) + b2
        out = jnp.einsum('ted,te->td', y, combine)
        return out.reshape(x.shape)

    def _L3_gnn_ref(node_features, adjacency_matrix, W, b_W, a_vec, b_a):
        import jax, jax.numpy as jnp
        import numpy as np
        N = 4096
        D_IN = 128
        D_OUT = 128
        NEG_INF = -9000000000000000.0
        h = node_features @ W.T + b_W
        a1, a2 = (a_vec[:D_OUT], a_vec[D_OUT:])
        e = (h @ a1)[:, None] + (h @ a2)[None, :] + b_a[0]
        e = jnp.where(e > 0, e, 0.2 * e)
        scores = jnp.where(adjacency_matrix > 0, e, jnp.float32(NEG_INF))
        attention = jax.nn.softmax(scores, axis=1)
        h_prime = attention @ h
        return h_prime

    def _L3_ffn_ref(x, Wg, bg, W1, b1, W2, b2):
        import jax, jax.numpy as jnp
        import numpy as np
        B, S, D, E, H, K = (4, 2048, 128, 8, 256, 2)
        Bv, Sv, Dv = x.shape
        gate_scores = x @ Wg + bg
        _, idx = jax.lax.top_k(gate_scores, K)
        mask = jax.nn.one_hot(idx, E, dtype=x.dtype).sum(axis=-2)
        xf = x.reshape(-1, Dv)
        mf = mask.reshape(-1, E)
        h = jax.nn.gelu(jnp.einsum('td,edh->teh', xf, W1) + b1[None], approximate=False)
        y = jnp.einsum('teh,ehd->ted', h, W2) + b2[None]
        out = jnp.einsum('ted,te->td', y, mf)
        return out.reshape(Bv, Sv, Dv)
    x = x + _L0_gnn_ref(_layernorm(x, axis=-1), adj, L0_gnn_W, L0_gnn_a)
    x = x + _L0_ffn_ref(_layernorm(x, axis=-1)[None], L0_ffn_ln1_w, L0_ffn_ln2_w, L0_ffn_wq, L0_ffn_wk, L0_ffn_wv, L0_ffn_wo, L0_ffn_router_w, L0_ffn_w1, L0_ffn_w2, L0_ffn_w3)[0]
    x = x + _L1_gnn_ref(_layernorm(x, axis=-1), adj, L1_gnn_W_w, L1_gnn_W_b, L1_gnn_a)
    x = x + _L1_ffn_ref(_layernorm(x, axis=-1)[None], L1_ffn_router_w1, L1_ffn_router_b1, L1_ffn_router_w2, L1_ffn_router_b2, L1_ffn_expert_w1, L1_ffn_expert_b1, L1_ffn_expert_w2, L1_ffn_expert_b2, L1_ffn_expert_w3, L1_ffn_expert_b3)[0]
    x = x + _L2_gnn_ref(_layernorm(x, axis=-1), adj, 4096, L2_gnn_W, L2_gnn_b, L2_gnn_a)
    x = x + _L2_ffn_ref(_layernorm(x, axis=-1)[None], L2_ffn_Wg, L2_ffn_bg, L2_ffn_bias, L2_ffn_W1, L2_ffn_b1, L2_ffn_W2, L2_ffn_b2)[0]
    x = x + _L3_gnn_ref(_layernorm(x, axis=-1), adj, L3_gnn_W, L3_gnn_b_W, L3_gnn_a_vec, L3_gnn_b_a)
    x = x + _L3_ffn_ref(_layernorm(x, axis=-1)[None], L3_ffn_Wg, L3_ffn_bg, L3_ffn_W1, L3_ffn_b1, L3_ffn_W2, L3_ffn_b2)[0]
    return x

_drawn_inputs = setup_inputs


def setup_inputs(seed=0):
    import zlib

    import numpy as np

    out = dict(_drawn_inputs(seed))
    spreads = {'L0_ffn_ln1_w': (1.0, 0.6),
     'L0_ffn_ln2_w': (1.0, 0.6),
     'L1_ffn_router_b1': (0.0, 0.421),
     'L1_ffn_router_b2': (0.0, 0.517),
     'L1_ffn_expert_b1': (0.0, 2.0),
     'L1_ffn_expert_b2': (0.0, 2.0),
     'L1_ffn_expert_b3': (0.0, 1.162),
     'L2_gnn_b': (0.0, 2.0),
     'L2_ffn_bias': (0.0, 0.8),
     'L3_gnn_b_W': (0.0, 0.76),
     'L3_ffn_bg': (0.0, 0.1),
     'L3_ffn_b1': (0.0, 0.8),
     'L3_ffn_b2': (0.0, 0.8)}
    factors = {'L0_ffn_wq': 8.0,
     'L0_ffn_wk': 8.0,
     'L0_ffn_wv': 8.0,
     'L0_ffn_wo': 8.0,
     'L0_ffn_router_w': 8.0,
     'L0_ffn_w1': 8.0,
     'L0_ffn_w2': 8.0,
     'L0_ffn_w3': 8.0,
     'L1_gnn_W_b': 40.621,
     'L1_ffn_expert_w1': 3.119,
     'L1_ffn_expert_w2': 2.687,
     'L2_ffn_Wg': 5.197,
     'L2_ffn_bg': 22.907,
     'L2_ffn_W1': 5.768,
     'L2_ffn_b1': 38.796,
     'L2_ffn_W2': 4.844,
     'L2_ffn_b2': 40.574,
     'L3_ffn_W1': 3.721,
     'L3_ffn_W2': 3.422,
     'L1_gnn_a': 4.149,
     'L3_gnn_a_vec': 4.947}
    for name, (base, spread) in spreads.items():
        noise = np.random.default_rng([zlib.crc32(name.encode()), seed]).standard_normal(out[name].shape)
        drawn = base * np.exp(spread * noise) if base else spread * noise
        out[name] = jnp.asarray(drawn.astype(out[name].dtype))
    for name, factor in factors.items():
        out[name] = (out[name] * factor).astype(out[name].dtype)
    return out
```

```python
from contextlib import ExitStack, contextmanager

import numpy as np

import concourse.bass as bass
from concourse import mybir

ALU = mybir.AluOpType
ACT = mybir.ActivationFunctionType
AX = mybir.AxisListType
F32 = mybir.dt.float32
BF16 = mybir.dt.bfloat16
U8 = mybir.dt.uint8
I32 = mybir.dt.int32
RMAX = bass.bass_isa.ReduceOp.max

P = 128
N = 4096
D = 128
T = N // P
G = 4
NG = T // G
GW = G * P
IC = 1024
NI = N // IC
NB = IC // P
VW = D + 1
ROW_MAX = 70.0
EPS = 1e-5
WORK = 19800
BANKS = 8


class Workspace:

    def __init__(self, tensor, width):
        self.tensor, self.width, self.used = tensor, width, 0

    def cut(self, shape, dt=F32, align=1):
        size = {F32: 4, I32: 4, BF16: 2, U8: 1}[dt]
        n = int(np.prod(shape[1:]))
        columns = -(-n * size // 4)
        start = -(-self.used // align) * align
        assert start + columns <= self.width, (shape, start, self.width)
        self.used = start + columns
        flat = self.tensor[0:shape[0], start:start + columns]
        if dt != F32:
            flat = flat.bitcast(dt)[:, 0:n]
        names = [f"d{i}" for i in range(len(shape) - 1)]
        if len(names) > 1:
            flat = flat.rearrange(f"p ({' '.join(names)}) -> p {' '.join(names)}", **dict(zip(names, shape[1:])))
        return flat


@contextmanager
def stage(k):
    marks, before = (k.work.used, k.banks.used), k.nc.snapshot_sems()
    yield
    k.work.used, k.banks.used = marks
    taken = k.nc.allocated_since(before)
    if taken:
        k.nc.clear_and_free_semaphores(taken)
        k.nc.all_engine_barrier()


class Kernel:

    def __init__(self, nc, dram):
        self.nc, self.dram = nc, dram


def is_later(count):
    return not isinstance(count, int) or count > 0


def wait_apart(engine, sem, value, passed):
    engine.wait_ge(sem, value).then_inc(passed, 1)




def layer_norm_stats(k, name):
    nc, x = k.nc, k.x
    with stage(k), ExitStack() as ctx:
        sb = lambda shape, dt=F32: k.work.cut(shape, dt)
        sem = lambda n: nc.alloc_semaphore(f"{name}_{n}")
        stats = sb([P, T, 6])
        mean2, diff, m2 = sb([P, T]), sb([P, T]), sb([P, T])
        var, std = k.var, sb([P, T])
        tiles_done, step_done, var_ready, std_ready = (
            sem("tiles_done"), sem("step_done"), sem("var_ready"), sem("std_ready"))
        block = ctx.enter_context(nc.Block())

        @block.vector
        def _(dve):
            with dve.Fori(0, T // 4) as i:
                for u in range(4):
                    at = bass.ds(i * 4 + u, 1)
                    nc.vector.bn_stats(stats[:, at, :], x[:, at, :]).then_inc(tiles_done, 1)
            dve.wait_ge(tiles_done, T)
            even_mean, even_m2, odd_mean, odd_m2 = (stats[:, :, n] for n in (1, 2, 4, 5))
            nc.vector.tensor_tensor(mean2[:], even_mean, odd_mean, ALU.add)
            nc.vector.tensor_tensor(m2[:], even_m2, odd_m2, ALU.add)
            nc.vector.tensor_tensor(diff[:], even_mean, odd_mean, ALU.subtract).then_inc(step_done, 1)
            dve.wait_ge(step_done, 1)
            nc.vector.scalar_tensor_tensor(out=diff[:], in0=diff[:], scalar=0.25, in1=diff[:],
                                           op0=ALU.mult, op1=ALU.mult).then_inc(step_done, 1)
            dve.wait_ge(step_done, 2)
            nc.vector.scalar_tensor_tensor(out=var[:], in0=m2[:], scalar=1.0 / D, in1=diff[:],
                                           op0=ALU.mult, op1=ALU.add).then_inc(step_done, 1)
            dve.wait_ge(step_done, 3)
            nc.vector.tensor_scalar(m2[:], var[:], EPS, None, ALU.add).then_inc(var_ready, 1)
            dve.wait_ge(std_ready, 1)
            nc.vector.reciprocal(k.rstd[:], std[:]).then_inc(step_done, 1)
            dve.wait_ge(step_done, 4)
            nc.vector.scalar_tensor_tensor(out=k.shift[:], in0=mean2[:], scalar=-0.5, in1=k.rstd[:],
                                           op0=ALU.mult, op1=ALU.mult)

        @block.scalar
        def _(act):
            act.wait_ge(var_ready, 1)
            nc.scalar.activation(std[:], m2[:], ACT.Sqrt).then_inc(std_ready, 1)




def gnn_layer(k, name, kind, load_adj=False):
    nc, d = k.nc, k.dram
    layer_norm_stats(k, f"{name}_ln")
    with stage(k), ExitStack() as ctx:
        sb = lambda shape, dt=F32: k.work.cut(shape, dt)
        t = {
            "V": sb([P, T, VW]),
            "a_row": sb([P, N]) if kind != "tanh" else None,
            "b_col": sb([P, T]),
            "b_exp": sb([P, T]),
            "all_sum": sb([P, D]),
        }
        gnn_project(k, name, kind, t)
        gnn_attend(k, name, kind, t, load_adj)


def gnn_project(k, name, kind, t):
    nc, x = k.nc, k.x
    V, a_row, b_col, b_exp = t["V"], t["a_row"], t["b_col"], t["b_exp"]
    tanh = kind == "tanh"
    bias = k.dram.get(f"{name}_b_row")
    with stage(k), ExitStack() as ctx:
        sb = lambda shape, dt=F32: k.work.cut(shape, dt)
        sem = lambda n: nc.alloc_semaphore(f"{name}_{n}")
        ps = lambda shape: k.banks.cut(shape, align=512)
        W, WT = sb([P, D]), sb([P, D])
        a2 = sb([P, 2])
        wa = sb([P, 2])
        wa_wide = sb([P, P])
        b_row, b_wide, bc = sb([P, D]), sb([P, P]), sb([P, 1])
        ba = sb([P, 1])
        aw_row = sb([P, D])
        const2 = sb([P, 2])
        xn = [sb([P, G, D]) for u in range(2)]
        xT = [sb([P, GW]) for u in range(2)]
        h = [sb([P, G, D]) for u in range(2)] if tanh else None
        h_sum = sb([P, T]) if tanh else None
        b_top, b_all = sb([P, 1]), sb([P, 1])
        v_sum = sb([P, D])
        xT_ps = [ps([P, GW]) for u in range(2)]
        v_ps = [ps([P, G, D]) for u in range(2)]
        a_ps = [ps([P, GW]) for u in range(2)]
        s_ps = ps([P, 512])
        b_ps, wa_ps, c_ps, sum_ps = s_ps[:, 0:T], s_ps[:, 64:66], s_ps[:, 68:70], s_ps[:, 128:128 + D]

        weights_in, ones_set = sem("weights_in"), sem("ones_set")
        wa_done, wa_ready, const_ready, wide_ready = (sem(n) for n in ("wa_done", "wa_ready", "const_ready", "wide_ready"))
        xn_ready, tr_done, xT_ready = sem("xn_ready"), sem("tr_done"), sem("xT_ready")
        v_done, v_taken, a_taken = sem("v_done"), sem("v_taken"), sem("a_taken")
        h_ready, h_tanh, h_summed, h_scaled, h_taken = (
            sem(n) for n in ("h_ready", "h_tanh", "h_summed", "h_scaled", "h_taken"))
        chain, top_ready, top_all, shifted, exp_ready = (
            sem(n) for n in ("chain", "top_ready", "top_all", "shifted", "exp_ready"))
        vsum_ready, sum_done = sem("vsum_ready"), sem("sum_done")
        block = ctx.enter_context(nc.Block())
        dr = k.dram
        loads = [(W[:], dr[f"{name}_W"])]
        if tanh:
            loads += [(aw_row[:], dr[f"{name}_a_row"].partition_broadcast(P))]
        else:
            loads += [(WT[:], dr[f"{name}_WT"]), (a2[:], dr[f"{name}_a2"])]
        if bias is not None:
            loads += [(b_row[:], bias.partition_broadcast(P))]
            if not tanh:
                loads += [(bc[:], dr[f"{name}_b_col"])]
        has_ba = f"{name}_ba" in dr
        if has_ba:
            loads += [(ba[:], dr[f"{name}_ba"].partition_broadcast(P))]

        @block.sync
        def _(sp):
            for out, src in loads:
                sp.dma_start(out, src).then_inc(weights_in, 16)

        @block.gpsimd
        def _(pool):
            nc.gpsimd.memset(V[:, :, D:VW], 1.0).then_inc(ones_set, 1)
            pool.wait_ge(top_ready, 1)
            nc.gpsimd.partition_all_reduce(b_all[:], b_top[:], P, RMAX).then_inc(top_all, 1)

        @block.tensor
        def _(pe):
            def transposes(g, u):
                pe.wait_ge(xn_ready, g + 1)
                if is_later(g - 1):
                    pe.wait_ge(xT_ready, g - 1)
                for j in range(G):
                    last = nc.tensor.transpose(xT_ps[u][:, j * P:(j + 1) * P], xn[u][:, j, :], k.ident[:])
                last.then_inc(tr_done, 1)

            def project(g, u):
                pe.wait_ge(xT_ready, g + 1)
                if is_later(g - 1):
                    pe.wait_ge(v_taken, g - 1)
                    if not tanh:
                        pe.wait_ge(a_taken, g - 1)
                for j in range(G):
                    block_T = xT[u][:, j * P:(j + 1) * P]
                    last = nc.tensor.matmul(v_ps[u][:, j, :], block_T, W[:], start=True, stop=True)
                    if not tanh:
                        nc.tensor.matmul(b_ps[:, bass.ds(g * G + j, 1)], block_T, wa[:, 1:2], start=True, stop=True)
                if not tanh:
                    last = nc.tensor.matmul(a_ps[u][:], wa_wide[:], xT[u][:], start=True, stop=True)
                last.then_inc(v_done, 1)

            pe.wait_ge(weights_in, 16 * len(loads))
            if not tanh:
                nc.tensor.matmul(wa_ps, WT[:], a2[:], start=True, stop=True).then_inc(wa_done, 1)
                if bias is not None:
                    pe.wait_ge(wide_ready, 1)
                    nc.tensor.matmul(c_ps, b_wide[:], a2[:], start=True, stop=True).then_inc(wa_done, 1)
                pe.wait_ge(wa_ready, 1)
                pe.wait_ge(const_ready, 1)
            for u in range(2):
                transposes(u, u)
            for u in range(2):
                transposes(2 + u, u)
            for u in range(2):
                project(u, u)
            with pe.Fori(1, NG // 2 - 1) as i:
                for u in range(2):
                    transposes(i * 2 + (2 + u), u)
                for u in range(2):
                    project(i * 2 + u, u)
            for u in range(2):
                project(NG - 2 + u, u)
            if not tanh:
                pe.wait_ge(vsum_ready, 1)
                nc.tensor.matmul(sum_ps, k.ones[:], v_sum[:], start=True, stop=True).then_inc(sum_done, 1)

        @block.scalar
        def _(act):
            def copy_T(g, u):
                act.wait_ge(tr_done, g + 1)
                if is_later(g - 1):
                    act.wait_ge(v_done, g - 1)
                nc.scalar.activation(xT[u][:], xT_ps[u][:], ACT.Copy).then_inc(xT_ready, 1)

            def take(g, u):
                if tanh:
                    act.wait_ge(h_ready, g + 1)
                    nc.scalar.activation(h[u][:], h[u][:], ACT.Tanh).then_inc(h_tanh, 1)
                else:
                    act.wait_ge(v_done, g + 1)
                    nc.scalar.activation(a_row[:, bass.ds(g * GW, GW)], a_ps[u][:], ACT.Identity,
                                         bias=const2[:, 0:1]).then_inc(a_taken, 1)

            for u in range(2):
                copy_T(u, u)
            for u in range(2):
                copy_T(2 + u, u)
            if not tanh:
                act.wait_ge(const_ready, 1)
            for u in range(2):
                take(u, u)
            with act.Fori(1, NG // 2 - 1) as i:
                for u in range(2):
                    copy_T(i * 2 + (2 + u), u)
                for u in range(2):
                    take(i * 2 + u, u)
            for u in range(2):
                take(NG - 2 + u, u)
            act.wait_ge(shifted, 1)
            nc.scalar.activation(b_exp[:], b_col[:], ACT.Exp, scale=1.0 if tanh else 0.2).then_inc(exp_ready, 1)

        @block.vector
        def _(dve):
            links = [0]

            def link(ins):
                links[0] += 1
                ins.then_inc(chain, 1)
                dve.wait_ge(chain, links[0])

            def normalise(g, u):
                if is_later(g - 1):
                    dve.wait_ge(tr_done, g - 1)
                for j in range(G):
                    at = bass.ds(g * G + j, 1)
                    last = nc.vector.tensor_scalar(xn[u][:, j:j + 1, :], x[:, at, :], k.rstd[:, at], k.shift[:, at],
                                                   ALU.mult, ALU.add)
                last.then_inc(xn_ready, 1)

            def take(g, u):
                dve.wait_ge(v_done, g + 1)
                at = bass.ds(g * G, G)
                if tanh:
                    if is_later(g - 1):
                        dve.wait_ge(h_taken, g - 1)
                    nc.vector.tensor_tensor(h[u][:], v_ps[u][:], b_row[:, None, :].to_broadcast([P, G, D]),
                                            ALU.add).then_inc(h_ready, 1)
                    nc.vector.tensor_copy(V[:, at, 0:D], v_ps[u][:]).then_inc(v_taken, 1)
                elif bias is not None:
                    nc.vector.tensor_tensor(V[:, at, 0:D], v_ps[u][:], b_row[:, None, :].to_broadcast([P, G, D]),
                                            ALU.add).then_inc(v_taken, 1)
                else:
                    nc.vector.tensor_copy(V[:, at, 0:D], v_ps[u][:]).then_inc(v_taken, 1)

            def reduce_h(g, u):
                at = bass.ds(g * G, G)
                dve.wait_ge(h_tanh, g + 1)
                nc.vector.tensor_reduce(h_sum[:, at], h[u][:], AX.X, ALU.add).then_inc(h_summed, 1)
                dve.wait_ge(h_summed, g + 1)
                nc.vector.tensor_tensor(h[u][:], h[u][:], aw_row[:, None, :].to_broadcast([P, G, D]),
                                        ALU.mult).then_inc(h_scaled, 1)
                dve.wait_ge(h_scaled, g + 1)
                nc.vector.tensor_reduce(b_col[:, at], h[u][:], AX.X, ALU.add).then_inc(h_taken, 1)

            dve.wait_ge(weights_in, 16 * len(loads))
            if not tanh:
                if bias is not None:
                    nc.vector.tensor_copy(b_wide[:], bc[:, 0:1].to_broadcast([P, P])).then_inc(wide_ready, 1)
                dve.wait_ge(wa_done, 1 if bias is None else 2)
                link(nc.vector.tensor_copy(wa[:], wa_ps))
                nc.vector.tensor_copy(wa_wide[:], wa[:, 0:1].to_broadcast([P, P])).then_inc(wa_ready, 1)
                if bias is not None:
                    if has_ba:
                        link(nc.vector.tensor_copy(const2[:], c_ps))
                        nc.vector.tensor_tensor(const2[:, 0:1], const2[:, 0:1], ba[:], ALU.add).then_inc(const_ready, 1)
                    else:
                        nc.vector.tensor_copy(const2[:], c_ps).then_inc(const_ready, 1)
                else:
                    nc.vector.memset(const2[:], 0.0).then_inc(const_ready, 1)
            for u in range(2):
                normalise(u, u)
            for u in range(2):
                normalise(2 + u, u)
            for u in range(2):
                take(u, u)
            if tanh:
                for u in range(2):
                    reduce_h(u, u)
            with dve.Fori(1, NG // 2 - 1) as i:
                for u in range(2):
                    normalise(i * 2 + (2 + u), u)
                for u in range(2):
                    take(i * 2 + u, u)
                if tanh:
                    for u in range(2):
                        reduce_h(i * 2 + u, u)
            for u in range(2):
                take(NG - 2 + u, u)
            if tanh:
                for u in range(2):
                    reduce_h(NG - 2 + u, u)
                dve.wait_ge(h_taken, NG)
            else:
                dve.wait_ge(v_taken, NG)
                link(nc.vector.tensor_scalar(b_col[:], b_ps, const2[:, 1:2], None, ALU.add))
                nc.vector.tensor_reduce(v_sum[:], V[:, :, 0:D].rearrange("p t d -> p d t"), AX.X, ALU.add).then_inc(vsum_ready, 1)
            nc.vector.tensor_reduce(b_top[:], b_col[:], AX.X, ALU.max).then_inc(top_ready, 1)
            dve.wait_ge(top_all, 1)
            nc.vector.tensor_scalar(b_col[:], b_col[:], b_all[:], None, ALU.subtract).then_inc(shifted, 1)
            if not tanh:
                dve.wait_ge(a_taken, NG)
                link(nc.vector.tensor_scalar(a_row[:], a_row[:], b_all[:], 0.8, ALU.add, ALU.mult))
                nc.vector.tensor_scalar(a_row[:], a_row[:], ROW_MAX, None, ALU.min)
                dve.wait_ge(sum_done, 1)
                nc.vector.tensor_copy(t["all_sum"][:], sum_ps)
            else:
                dve.wait_ge(exp_ready, 1)
                link(nc.vector.tensor_scalar(h_sum[:], h_sum[:], 0.0, None, ALU.not_equal))
                link(nc.vector.tensor_tensor(b_exp[:], b_exp[:], h_sum[:], ALU.mult))
                dve.wait_ge(ones_set, 1)
                dve.wait_ge(v_taken, NG)
                with dve.Fori(0, T // 4) as i:
                    for u in range(4):
                        at = bass.ds(i * 4 + u, 1)
                        nc.vector.tensor_scalar(V[:, at, :], V[:, at, :], b_exp[:, at], None, ALU.mult)


def gnn_attend(k, name, kind, t, load_adj):
    nc, x, mask = k.nc, k.x, k.mask
    V, a_row, b_col, b_exp, all_sum = t["V"], t["a_row"], t["b_col"], t["b_exp"], t["all_sum"]
    tanh, elu = kind == "tanh", kind == "elu"
    RING = 2
    with stage(k), ExitStack() as ctx:
        sb = lambda shape, dt=F32: k.work.cut(shape, dt)
        sem = lambda n: nc.alloc_semaphore(f"{name}_m_{n}")
        p = [sb([P, IC]) for u in range(2)]
        e = [sb([P, IC]) for u in range(2)] if not tanh else None
        num = sb([P, NB, VW])
        den, lone, inv, lone_inv = (sb([P, NB]) for _ in range(4))
        low = sb([P, NB, D]) if elu else None
        adj = [sb([P, IC], I32) for u in range(RING)] if load_adj else None
        acc = k.banks.cut([P, NB, 256], align=512)
        e_ready, p_ready, p_used, acc_taken = (sem(n) for n in ("e_ready", "p_ready", "p_used", "acc_taken"))
        chain, low_ready, low_exp, x_added = (sem(n) for n in ("chain", "low_ready", "low_exp", "x_added"))
        adj_in = [sem(f"adj_in{u}") for u in range(RING)]
        mask_ready, act_passed = sem("mask_ready"), sem("act_passed")
        block = ctx.enter_context(nc.Block())

        if load_adj:
            @block.sync
            def _(sp):
                def load(s, jt, ic, u):
                    if is_later(s - (RING - 1)):
                        sp.wait_ge(mask_ready, s - (RING - 1))
                    sp.dma_start(adj[u][:], k.dram["adjT"][bass.ds(jt * P, P), bass.ds(ic * IC, IC)]).then_inc(adj_in[u], 16)

                for u in range(2):
                    load(u, u, 0, u)
                with sp.Fori(1, T // 2) as i:
                    for u in range(2):
                        load(i * 2 + u, i * 2 + u, 0, u)
                with sp.Fori(1, NI) as ic:
                    with sp.Fori(0, T // 2) as i:
                        for u in range(2):
                            load(ic * T + i * 2 + u, i * 2 + u, ic, u)

        @block.scalar
        def _(act):
            def exps(ic, i, u):
                s = ic * T + i * 2 + u
                if is_later(s - 1):
                    wait_apart(act, p_ready, s - 1, act_passed)
                nc.scalar.activation(e[u][:], a_row[:, bass.ds(ic * IC, IC)], ACT.Exp,
                                     bias=b_col[:, bass.ds(i * 2 + u, 1)]).then_inc(e_ready, 1)

            def take(ic):
                act.wait_ge(p_used, ic * T + T)
                if is_later(ic):
                    act.wait_ge(x_added, ic)
                nc.scalar.activation(num[:], acc[:, :, 0:VW], ACT.Copy).then_inc(acc_taken, 1)

            def low_half(ic):
                if elu:
                    act.wait_ge(low_ready, ic + 1)
                    nc.scalar.activation(low[:], low[:], ACT.Exp).then_inc(low_exp, 1)

            if tanh:
                take(0)
                with act.Fori(1, NI) as ic:
                    take(ic)
            else:
                for u in range(2):
                    exps(0, 0, u)
                with act.Fori(1, T // 2) as i:
                    for u in range(2):
                        exps(0, i, u)
                with act.Fori(1, NI) as ic:
                    for u in range(2):
                        exps(ic, 0, u)
                    take(ic - 1)
                    low_half(ic - 1)
                    with act.Fori(1, T // 2) as i:
                        for u in range(2):
                            exps(ic, i, u)
                take(NI - 1)
                low_half(NI - 1)

        @block.vector
        def _(dve):
            def weights(ic, i, u):
                s = ic * T + i * 2 + u
                at, cols = bass.ds(i * 2 + u, 1), bass.ds(ic * IC, IC)
                if load_adj:
                    dve.wait_ge(adj_in[u], (ic * (T // 2) + i) * 16 + 16)
                    nc.vector.tensor_scalar(mask[:, at, cols], adj[u][:, None, :], 0.0, None, ALU.is_gt).then_inc(mask_ready, 1)
                    dve.wait_ge(mask_ready, s + 1)
                if is_later(s - 1):
                    dve.wait_ge(p_used, s - 1)
                if tanh:
                    nc.vector.tensor_copy(p[u][:, None, :], mask[:, at, cols]).then_inc(p_ready, 1)
                else:
                    dve.wait_ge(e_ready, s + 1)
                    nc.vector.scalar_tensor_tensor(out=p[u][:, None, :], in0=e[u][:, None, :], scalar=b_exp[:, at],
                                                   in1=mask[:, at, cols], op0=ALU.max, op1=ALU.mult).then_inc(p_ready, 1)

            def finish(ic, links):
                dve.wait_ge(acc_taken, ic + 1)
                tiles = bass.ds(ic * NB, NB)

                def link(n, ins):
                    ins.then_inc(chain, 1)
                    dve.wait_ge(chain, links + n)
                if tanh:
                    link(1, nc.vector.tensor_scalar(den[:], num[:, :, D], 1e-37, None, ALU.max))
                    link(2, nc.vector.reciprocal(inv[:], den[:]))
                    link(3, nc.vector.tensor_tensor(num[:, :, 0:D], num[:, :, 0:D],
                                                    inv[:, :, None].to_broadcast([P, NB, D]), ALU.mult))
                else:
                    link(1, nc.vector.tensor_scalar(lone[:], num[:, :, D], 0.0, None, ALU.is_equal))
                    link(2, nc.vector.scalar_tensor_tensor(out=den[:], in0=lone[:], scalar=float(N), in1=num[:, :, D],
                                                           op0=ALU.mult, op1=ALU.add))
                    for b in range(NB):
                        last = nc.vector.scalar_tensor_tensor(out=num[:, b, 0:D], in0=all_sum[:], scalar=lone[:, b:b + 1],
                                                              in1=num[:, b, 0:D], op0=ALU.mult, op1=ALU.add)
                    link(3, nc.vector.reciprocal(inv[:], den[:]))
                    link(4, nc.vector.tensor_tensor(num[:, :, 0:D], num[:, :, 0:D],
                                                    inv[:, :, None].to_broadcast([P, NB, D]), ALU.mult))
                if elu:
                    nc.vector.tensor_scalar(low[:], num[:, :, 0:D], 0.0, None, ALU.min).then_inc(low_ready, 1)
                    link(5, nc.vector.tensor_scalar(num[:, :, 0:D], num[:, :, 0:D], 0.0, -1.0, ALU.max, ALU.add))
                    dve.wait_ge(low_exp, ic + 1)
                    link(6, nc.vector.tensor_tensor(num[:, :, 0:D], num[:, :, 0:D], low[:], ALU.add))
                nc.vector.tensor_tensor(x[:, tiles, :], x[:, tiles, :], num[:, :, 0:D], ALU.add).then_inc(x_added, 1)

            n_links = 3 if tanh else 6 if elu else 4
            for u in range(2):
                weights(0, 0, u)
            with dve.Fori(1, T // 2) as i:
                for u in range(2):
                    weights(0, i, u)
            with dve.Fori(1, NI) as ic:
                for i in range(1):
                    for u in range(2):
                        weights(ic, i, u)
                finish(ic - 1, (ic - 1) * n_links)
                with dve.Fori(1, T // 2) as i:
                    for u in range(2):
                        weights(ic, i, u)
            finish(NI - 1, (NI - 1) * n_links)

        @block.tensor
        def _(pe):
            def step(ic, i, u, first=False, last=False):
                s = ic * T + i * 2 + u
                pe.wait_ge(p_ready, s + 1)
                for b in range(NB):
                    ins = nc.tensor.matmul(acc[:, b, 0:VW], p[u][:, b * P:(b + 1) * P], V[:, bass.ds(i * 2 + u, 1), :],
                                           start=first and b % 2 == 0, stop=last, skip_group_check=True)
                ins.then_inc(p_used, 1)
                return ins

            def chunk(ic):
                if is_later(ic):
                    pe.wait_ge(acc_taken, ic)
                step(ic, 0, 0, first=True)
                step(ic, 0, 1)
                with pe.Fori(1, T // 2 - 1) as i:
                    step(ic, i, 0)
                    step(ic, i, 1)
                step(ic, T // 2 - 1, 0)
                step(ic, T // 2 - 1, 1, last=True)

            chunk(0)
            with pe.Fori(1, NI) as ic:
                chunk(ic)




def ffn_spec(s):
    return {
        0: dict(E=8, hidden=[128, 128, 85], kind="gated", router="softmax_norm"),
        1: dict(E=6, hidden=[128], kind="deep", router="softmax_twice"),
        2: dict(E=8, hidden=[128, 128], kind="relu", router="softmax"),
        3: dict(E=8, hidden=[128, 128], kind="gelu", router="mask"),
    }[s]


def ffn_layer(k, s):
    nc, name, spec = k.nc, f"L{s}f", ffn_spec(s)
    layer_norm_stats(k, f"{name}_ln")
    with stage(k), ExitStack() as ctx:
        sb = lambda shape, dt=F32: k.work.cut(shape, dt)
        t = {"xT": sb([P, N]), "logits": sb([P, T, spec["E"]]),
             "gates": sb([P, T, spec["E"]])}
        ffn_transpose(k, name, spec, t)
        ffn_route(k, name, spec, t)
        ffn_experts(k, name, spec, t)


def ffn_transpose(k, name, spec, t, src=None):
    nc, x, E = k.nc, k.x if src is None else src, spec["E"]
    deep, gated = spec["kind"] == "deep", spec["kind"] == "gated"
    RH = D // 2
    with stage(k), ExitStack() as ctx:
        sb = lambda shape, dt=F32: k.work.cut(shape, dt)
        sem = lambda n: nc.alloc_semaphore(f"{name}_t_{n}")
        ps = lambda shape: k.banks.cut(shape, align=512)
        r_w = sb([RH if deep else P, E])
        r_b = sb([P, E]) if not gated else None
        ln2 = sb([P, 1]) if gated else None
        r_w1, r_b1 = (sb([P, RH]), sb([RH, 1])) if deep else (None, None)
        r_b2 = sb([P, E]) if spec["router"] == "softmax" else None
        xn = [sb([P, G, D]) for u in range(2)]
        xs = [sb([P, GW]) for u in range(2)]
        rh = [sb([RH, GW]) for u in range(2)] if deep else None
        xT_ps = [ps([P, GW]) for u in range(2)]
        rh_ps = [ps([RH, GW]) for u in range(2)] if deep else None
        lg_ps = ps([P, 512])
        weights_in, xn_ready, tr_done, xs_ready, xT_ready = (
            sem(n) for n in ("weights_in", "xn_ready", "tr_done", "xs_ready", "xT_ready"))
        rh_done, rh_ready, lg_done, bias_ready = (sem(n) for n in ("rh_done", "rh_ready", "lg_done", "bias_ready"))
        block = ctx.enter_context(nc.Block())
        dr = k.dram
        loads = [(r_w[:], dr[f"{name}_r_w"])]
        loads += [(ln2[:], dr[f"{name}_ln2"])] if gated else [(r_b[:], dr[f"{name}_r_b"].partition_broadcast(P))]
        if deep:
            loads += [(r_w1[:], dr[f"{name}_r_w1"]), (r_b1[:], dr[f"{name}_r_b1"])]
        if r_b2 is not None:
            loads += [(r_b2[:], dr[f"{name}_r_b2"].partition_broadcast(P))]

        @block.sync
        def _(sp):
            for out, src in loads:
                sp.dma_start(out, src).then_inc(weights_in, 16)

        @block.vector
        def _(dve):
            def normalise(g, u):
                if is_later(g - 1):
                    dve.wait_ge(tr_done, g - 1)
                for j in range(G):
                    at = bass.ds(g * G + j, 1)
                    last = nc.vector.tensor_scalar(xn[u][:, j:j + 1, :], x[:, at, :], k.rstd[:, at], k.shift[:, at],
                                                   ALU.mult, ALU.add)
                last.then_inc(xn_ready, 1)

            def keep(g, u):
                dve.wait_ge(xs_ready, g + 1)
                nc.vector.tensor_copy(t["xT"][:, bass.ds(g * GW, GW)], xs[u][:]).then_inc(xT_ready, 1)

            for u in range(2):
                normalise(u, u)
            with dve.Fori(0, NG // 2 - 1) as i:
                for u in range(2):
                    normalise(i * 2 + (2 + u), u)
                for u in range(2):
                    keep(i * 2 + u, u)
            for u in range(2):
                keep(NG - 2 + u, u)
            dve.wait_ge(lg_done, NG)
            dve.wait_ge(weights_in, 16 * len(loads))
            if r_b2 is not None:
                nc.vector.tensor_tensor(r_b[:], r_b[:], r_b2[:], ALU.add).then_inc(bias_ready, 1)
                dve.wait_ge(bias_ready, 1)
            all_logits = lg_ps[:, 0:T * E].rearrange("p (t e) -> p t e", e=E)
            if gated:
                nc.vector.tensor_copy(t["logits"][:], all_logits)
            else:
                nc.vector.tensor_tensor(t["logits"][:], all_logits, r_b[:, None, :].to_broadcast([P, T, E]), ALU.add)

        @block.scalar
        def _(act):
            def copy_T(g, u):
                act.wait_ge(tr_done, g + 1)
                if is_later(g - 1):
                    act.wait_ge(rh_done if deep else lg_done, g - 1)
                    act.wait_ge(xT_ready, g - 1)
                nc.scalar.activation(xs[u][:], xT_ps[u][:], ACT.Copy, scale=ln2[:] if gated else 1.0).then_inc(xs_ready, 1)

            def relu(g, u):
                act.wait_ge(rh_done, g + 1)
                if is_later(g - 1):
                    act.wait_ge(lg_done, g - 1)
                nc.scalar.activation(rh[u][:], rh_ps[u][:], ACT.Relu, bias=r_b1[:]).then_inc(rh_ready, 1)

            act.wait_ge(weights_in, 16 * len(loads))
            for u in range(2):
                copy_T(u, u)
            for u in range(2):
                copy_T(2 + u, u)
            if deep:
                for u in range(2):
                    relu(u, u)
            with act.Fori(1, NG // 2 - 1) as i:
                for u in range(2):
                    copy_T(i * 2 + (2 + u), u)
                if deep:
                    for u in range(2):
                        relu(i * 2 + u, u)
            if deep:
                for u in range(2):
                    relu(NG - 2 + u, u)

        @block.tensor
        def _(pe):
            def transposes(g, u):
                pe.wait_ge(xn_ready, g + 1)
                if is_later(g - 1):
                    pe.wait_ge(xs_ready, g - 1)
                for j in range(G):
                    last = nc.tensor.transpose(xT_ps[u][:, j * P:(j + 1) * P], xn[u][:, j, :], k.ident[:])
                last.then_inc(tr_done, 1)

            def hidden(g, u):
                if deep:
                    pe.wait_ge(xs_ready, g + 1)
                    if is_later(g - 1):
                        pe.wait_ge(rh_ready, g - 1)
                    nc.tensor.matmul(rh_ps[u][:], r_w1[:], xs[u][:], start=True, stop=True).then_inc(rh_done, 1)

            def logits(g, u):
                if deep:
                    pe.wait_ge(rh_ready, g + 1)
                else:
                    pe.wait_ge(xs_ready, g + 1)
                src = rh[u] if deep else xs[u]
                for j in range(G):
                    last = nc.tensor.matmul(lg_ps[:, bass.ds((g * G + j) * E, E)], src[:, j * P:(j + 1) * P], r_w[:],
                                            start=True, stop=True)
                last.then_inc(lg_done, 1)

            def route(i):
                for u in range(2):
                    hidden(i * 2 + u, u)
                for u in range(2):
                    logits(i * 2 + u, u)

            pe.wait_ge(weights_in, 16 * len(loads))
            for u in range(2):
                transposes(u, u)
            for u in range(2):
                transposes(2 + u, u)
            route(0)
            with pe.Fori(1, NG // 2 - 1) as i:
                for u in range(2):
                    transposes(i * 2 + (2 + u), u)
                route(i)
            route(NG // 2 - 1)


def ffn_route(k, name, spec, t):
    nc, E, router = k.nc, spec["E"], spec["router"]
    logits, gates = t["logits"], t["gates"]
    with stage(k), ExitStack() as ctx:
        sb = lambda shape, dt=F32: k.work.cut(shape, dt)
        sem = lambda n: nc.alloc_semaphore(f"{name}_r_{n}")
        first = sb([P, E])
        sel = [sb([P, T, E]) for n in range(2)]
        rank, score = sb([P, T, E]), sb([P, T, E])
        top = [sb([P, T]) for n in range(2)]
        top_rank, one, two = sb([P, T]), sb([P, T]), sb([P, T])
        total = sb([P, T])
        chain, to_exp, exp_done = sem("chain"), sem("to_exp"), sem("exp_done")
        block = ctx.enter_context(nc.Block())
        wide = lambda a: a[:, :, None].to_broadcast([P, T, E])
        softmax = router in ("softmax_norm", "softmax_twice")

        @block.scalar
        def _(act):
            if softmax:
                act.wait_ge(to_exp, 1)
                nc.scalar.activation(score[:], score[:], ACT.Exp).then_inc(exp_done, 1)
            if router in ("softmax", "softmax_twice"):
                act.wait_ge(to_exp, 2 if softmax else 1)
                nc.scalar.activation(two[:], two[:], ACT.Exp).then_inc(exp_done, 1)

        @block.vector
        def _(dve):
            links = [0]

            def link(ins):
                links[0] += 1
                ins.then_inc(chain, 1)
                dve.wait_ge(chain, links[0])

            def tt(out, a, b, op):
                link(nc.vector.tensor_tensor(out, a, b, op))

            def reduce(out, a, op):
                link(nc.vector.tensor_reduce(out, a, AX.X, op))

            for e in range(E):
                nc.vector.memset(first[:, e:e + 1], float(E - e))
            if softmax:
                reduce(top[0][:], logits[:], ALU.max)
                nc.vector.tensor_tensor(score[:], logits[:], wide(top[0]), ALU.subtract).then_inc(to_exp, 1)
                dve.wait_ge(exp_done, 1)
                reduce(total[:], score[:], ALU.add)
                link(nc.vector.reciprocal(total[:], total[:]))
                tt(score[:], score[:], wide(total), ALU.mult)
            else:
                link(nc.vector.tensor_copy(score[:], logits[:]))
            for n in range(2):
                reduce(top[n][:], score[:], ALU.max)
                tt(rank[:], score[:], wide(top[n]), ALU.is_equal)
                tt(rank[:], rank[:], first[:, None, :].to_broadcast([P, T, E]), ALU.mult)
                reduce(top_rank[:], rank[:], ALU.max)
                tt(sel[n][:], rank[:], wide(top_rank), ALU.is_equal)
                if n == 0:
                    link(nc.vector.scalar_tensor_tensor(out=score[:], in0=sel[0][:], scalar=-1e30, in1=score[:],
                                                        op0=ALU.mult, op1=ALU.add))
            if router in ("mask", "softmax_norm"):
                tt(gates[:], sel[0][:], sel[1][:], ALU.add)
            if router == "softmax_norm":
                tt(one[:], top[0][:], top[1][:], ALU.add)
                link(nc.vector.tensor_scalar(one[:], one[:], 1e-9, None, ALU.add))
                link(nc.vector.reciprocal(one[:], one[:]))
                tt(two[:], top[1][:], one[:], ALU.mult)
                tt(one[:], top[0][:], one[:], ALU.mult)
            elif router != "mask":
                nc.vector.tensor_tensor(two[:], top[1][:], top[0][:], ALU.subtract).then_inc(to_exp, 1)
                dve.wait_ge(exp_done, 2 if softmax else 1)
                link(nc.vector.tensor_scalar(one[:], two[:], 1.0, None, ALU.add))
                link(nc.vector.reciprocal(one[:], one[:]))
                tt(two[:], two[:], one[:], ALU.mult)
            if router != "mask":
                tt(sel[0][:], sel[0][:], wide(one), ALU.mult)
                tt(sel[1][:], sel[1][:], wide(two), ALU.mult)
                tt(gates[:], sel[0][:], sel[1][:], ALU.add)


def ffn_experts(k, name, spec, t):
    nc, x, E, kind, hidden = k.nc, k.x, spec["E"], spec["kind"], spec["hidden"]
    xT, gates = t["xT"], t["gates"]
    M = len(hidden)
    H = sum(hidden)
    units = [(e, m) for e in range(E) for m in range(M)]
    U = len(units)
    gated, deep = kind == "gated", kind == "deep"
    HS = 3 if gated else 2
    bias = not gated
    with stage(k), ExitStack() as ctx:
        sb = lambda shape, dt=F32: k.work.cut(shape, dt)
        sem = lambda n: nc.alloc_semaphore(f"{name}_e_{n}")
        ps = lambda shape: k.banks.cut(shape, align=512)
        w_in = sb([P, E, H])
        w_up = sb([P, E, H]) if gated else None
        w_mid = sb([P, E, D]) if deep else None
        w_out = sb([P, E, M, D])
        b_in = sb([P, E, M]) if bias else None
        b_mid = sb([P, E]) if deep else None
        b_out = sb([P, E, D]) if bias else None
        act_out = [sb([P, GW]) for u in range(2)] if gated or deep else None
        hid = [sb([P, GW]) for u in range(HS)]
        in_ps = [ps([P, GW]) for u in range(HS)]
        up_ps = [ps([P, GW]) for u in range(HS)] if gated else None
        mid_ps = [ps([P, GW]) for u in range(2)] if deep else None
        y_ps = [ps([P, G, D]) for u in range(2)]
        weights_in = sem("weights_in")
        in_done, in_taken, mid_done = sem("in_done"), sem("in_taken"), sem("mid_done")
        hid_ready, out_done, y_taken, x_chain = sem("hid_ready"), sem("out_done"), sem("y_taken"), sem("x_chain")
        block = ctx.enter_context(nc.Block())
        dr = k.dram
        loads = [(w_in[:], dr[f"{name}_w_in"]), (w_out[:], dr[f"{name}_w_out"])]
        if gated:
            loads += [(w_up[:], dr[f"{name}_w_up"])]
        if deep:
            loads += [(w_mid[:], dr[f"{name}_w_mid"]), (b_mid[:], dr[f"{name}_b_mid"])]
        if bias:
            loads += [(b_in[:], dr[f"{name}_b_in"]), (b_out[:], dr[f"{name}_b_out"].partition_broadcast(P))]

        @block.sync
        def _(sp):
            for out, src in loads:
                sp.dma_start(out, src).then_inc(weights_in, 16)

        @block.tensor
        def _(pe):
            def first_product(c, n):
                e, m = units[n]
                lo, w = sum(hidden[:m]), hidden[m]
                at = c * U + n
                u = n % HS
                if deep:
                    pe.wait_ge(in_taken, at + 1)
                else:
                    pe.wait_ge(hid_ready, at + 1)
                cols = xT[:, bass.ds(c * GW, GW)]
                ins = nc.tensor.matmul(in_ps[u][0:w, :], w_in[:, e, lo:lo + w], cols, start=True, stop=True)
                if gated:
                    ins = nc.tensor.matmul(up_ps[u][0:w, :], w_up[:, e, lo:lo + w], cols, start=True, stop=True)
                ins.then_inc(in_done, 1)

            def mid_product(c, n):
                e, at, u = units[n][0], c * U + n, n % 2
                pe.wait_ge(in_taken, at + 3)
                pe.wait_ge(hid_ready, at + 1)
                nc.tensor.matmul(mid_ps[u][:], w_mid[:, e, :], act_out[u][:], start=True, stop=True).then_inc(mid_done, 1)

            def out_product(c, n):
                e, m = units[n]
                w, at, u = hidden[m], c * U + n, n % HS
                pe.wait_ge(hid_ready, at + HS + 1)
                if m == 0:
                    pe.wait_ge(y_taken, c * E + e + 1)
                for b in range(G):
                    ins = nc.tensor.matmul(y_ps[e % 2][:, b, :], hid[u][0:w, b * P:(b + 1) * P], w_out[0:w, e, m, :],
                                           start=m == 0 and b == 0, stop=m == M - 1, skip_group_check=True)
                ins.then_inc(out_done, 1)

            def unit(c, n, last=False):
                ahead = 2 if deep or gated else 1
                for step, product in ((ahead, first_product),) + (((1, mid_product),) if deep else ()):
                    if n + step < U:
                        product(c, n + step)
                    elif not last:
                        product(c + 1, n + step - U)
                out_product(c, n)

            pe.sem_inc(out_done, HS)
            pe.wait_ge(weights_in, 16 * len(loads))
            first_product(0, 0)
            if deep or gated:
                first_product(0, 1)
            if deep:
                mid_product(0, 0)
            with pe.Fori(0, NG - 1) as c:
                for n in range(U):
                    unit(c, n)
            for n in range(U):
                unit(NG - 1, n, last=True)

        @block.scalar
        def _(act):
            def unit(c, n):
                e, m = units[n]
                w, at, u = hidden[m], c * U + n, n % HS
                act.wait_ge(in_done, at + 1)
                if gated:
                    act.wait_ge(hid_ready, at + HS - 1)
                    nc.scalar.activation(act_out[n % 2][0:w, :], in_ps[u][0:w, :], ACT.Silu).then_inc(in_taken, 1)
                elif deep:
                    act.wait_ge(mid_done, at + 1)
                    nc.scalar.activation(act_out[u][:], in_ps[u][:], ACT.Relu, bias=b_in[:, e, m:m + 1]).then_inc(in_taken, 1)
                else:
                    act.wait_ge(out_done, at + 1)
                    nc.scalar.activation(hid[u][0:w, :], in_ps[u][0:w, :], ACT.Gelu if kind == "gelu" else ACT.Relu,
                                         bias=b_in[:, e, m:m + 1]).then_inc(hid_ready, 1)

            def mid_unit(c, n):
                e, at, u = units[n][0], c * U + n, n % HS
                act.wait_ge(mid_done, at + 3)
                act.wait_ge(out_done, at + 1)
                nc.scalar.activation(hid[u][:], mid_ps[u][:], ACT.Relu, bias=b_mid[:, e:e + 1]).then_inc(hid_ready, 1)

            if not gated:
                act.sem_inc(hid_ready, HS)
            if deep:
                act.sem_inc(in_taken, 2)
            act.wait_ge(weights_in, 16 * len(loads))
            if deep:
                unit(0, 0)
                with act.Fori(0, NG - 1) as c:
                    for n in range(U):
                        unit(c, n + 1) if n + 1 < U else unit(c + 1, 0)
                        mid_unit(c, n)
                for n in range(U):
                    if n + 1 < U:
                        unit(NG - 1, n + 1)
                    mid_unit(NG - 1, n)
            else:
                with act.Fori(0, NG) as c:
                    for n in range(U):
                        unit(c, n)

        @block.vector
        def _(dve):
            def product(c, n):
                e, m = units[n]
                w, at, u = hidden[m], c * U + n, n % HS
                dve.wait_ge(in_taken, at + 1)
                dve.wait_ge(out_done, at + 1)
                nc.vector.tensor_tensor(hid[u][0:w, :], act_out[n % 2][0:w, :], up_ps[u][0:w, :], ALU.mult).then_inc(hid_ready, 1)

            n_chain = 2 if bias else 1

            def add(c, e):
                done = (c * E + e) * n_chain
                dve.wait_ge(out_done, (c * E + e) * M + M + HS)
                for b in range(G):
                    at = bass.ds(c * G + b, 1)
                    ins = nc.vector.scalar_tensor_tensor(out=x[:, at, :], in0=y_ps[e % 2][:, b:b + 1, :], scalar=gates[:, at, e:e + 1],
                                                         in1=x[:, at, :], op0=ALU.mult, op1=ALU.add)
                ins.then_inc(y_taken, 1)
                dve.wait_ge(y_taken, c * E + e + 3)
                if bias:
                    for b in range(G):
                        at = bass.ds(c * G + b, 1)
                        ins = nc.vector.scalar_tensor_tensor(out=x[:, at, :], in0=b_out[:, e:e + 1, :], scalar=gates[:, at, e:e + 1],
                                                             in1=x[:, at, :], op0=ALU.mult, op1=ALU.add)
                    ins.then_inc(x_chain, 1)
                    dve.wait_ge(x_chain, c * E + e + 1)

            dve.sem_inc(y_taken, 2)
            if gated:
                dve.sem_inc(hid_ready, HS)
            if deep:
                dve.sem_inc(mid_done, 2)
            dve.wait_ge(weights_in, 16 * len(loads))
            with dve.Fori(0, NG) as c:
                for n, (e, m) in enumerate(units):
                    if gated:
                        product(c, n)
                        if m == 0 and e > 0:
                            add(c, e - 1)
                    else:
                        if m == M - 1:
                            add(c, e)
                if gated:
                    add(c, E - 1)




def ffn0_layer(k):
    nc, name, spec = k.nc, "L0f", ffn_spec(0)
    layer_norm_stats(k, f"{name}_ln")
    with stage(k), ExitStack() as ctx:
        sb = lambda shape, dt=F32: k.work.cut(shape, dt)
        dram_r = nc.dram_tensor("r_scratch", (N, D), F32, kind="Internal").ap()
        causal_attention(k, dram_r)
        t = {"xT": sb([P, N]), "logits": sb([P, T, spec["E"]]),
             "gates": sb([P, T, spec["E"]])}
        with stage(k):
            r = sb([P, T, D])
            rms_norm_scale(k, r, dram_r)
            ffn_transpose(k, name, spec, t, src=r)
        ffn_route(k, name, spec, t)
        ffn_experts(k, name, spec, t)


def rms_norm_scale(k, r, dram_r):
    nc = k.nc
    with stage(k), ExitStack() as ctx:
        sem = lambda n: nc.alloc_semaphore(f"rms_{n}")
        square = [k.work.cut([P, G, D]) for u in range(2)]
        r_in = [sem(f"r_in{g}") for g in range(NG)]
        squared, reduced, sum_ready, root_ready = sem("squared"), sem("reduced"), sem("sum_ready"), sem("root_ready")
        block = ctx.enter_context(nc.Block())

        @block.sync
        def _(sp):
            for g in range(NG):
                sp.dma_start(r[:, g * G:(g + 1) * G, :],
                             dram_r[g * GW:(g + 1) * GW, :].rearrange("(t p) d -> p t d", p=P)).then_inc(r_in[g], 16)

        @block.scalar
        def _(act):
            for g in range(NG):
                act.wait_ge(r_in[g], 16)
                if g >= 2:
                    act.wait_ge(reduced, g - 1)
                nc.scalar.activation(square[g % 2][:], r[:, g * G:(g + 1) * G, :], ACT.Square).then_inc(squared, 1)
            act.wait_ge(sum_ready, 1)
            nc.scalar.activation(k.rstd[:], k.rstd[:], ACT.Sqrt).then_inc(root_ready, 1)

        @block.vector
        def _(dve):
            nc.vector.memset(k.shift[:], 0.0)
            for g in range(NG):
                dve.wait_ge(squared, g + 1)
                nc.vector.tensor_reduce(k.rstd[:, g * G:(g + 1) * G], square[g % 2][:], AX.X, ALU.add).then_inc(reduced, 1)
            dve.wait_ge(reduced, NG)
            nc.vector.tensor_scalar(k.rstd[:], k.rstd[:], 1.0 / D, 1e-6, ALU.mult, ALU.add).then_inc(sum_ready, 1)
            dve.wait_ge(root_ready, 1)
            nc.vector.reciprocal(k.rstd[:], k.rstd[:])


NH, NKV, HD = 4, 2, 32
HV = HD + 1
PARTS = 3


def causal_attention(k, dram_r):
    nc, x, d = k.nc, k.x, k.dram
    scale = 1.0 / float(np.sqrt(np.float32(HD)))
    with stage(k), ExitStack() as ctx:
        sb = lambda shape, dt=F32: k.work.cut(shape, dt)
        sem = lambda n: nc.alloc_semaphore(f"at_{n}")
        ps = lambda shape: k.banks.cut(shape, align=512)
        KW = NKV * HD
        q_parts = nc.dram_tensor("q_parts", (PARTS, P, GW), BF16, kind="Internal").ap()
        k_parts = nc.dram_tensor("k_parts", (PARTS, KW, GW), BF16, kind="Internal").ap()
        w_q, w_qr = sb([P, D]), sb([P, D])
        w_k, w_kr, w_v = sb([P, KW]), sb([P, KW]), sb([P, KW])
        w_o, ln1, tri = sb([P, D]), sb([P, 1]), sb([P, P])
        rms, h_scale, h_shift = sb([P, T]), sb([P, T]), sb([P, T])
        ka, kb = sb([P, NKV, N], BF16), sb([2 * HD + 1, NKV, N], BF16)
        qa, qb = sb([P, NH, GW], BF16), sb([2 * HD + 1, NH, GW], BF16)
        v = sb([P, T, NKV, HV])
        cos, sin = sb([P, GW]), sb([P, GW])
        xs = sb([P, GW])
        full = sb([P, GW])
        rest = sb([P, GW])
        qp, kp = sb([P, PARTS, GW], BF16), sb([KW, PARTS, GW], BF16)
        tops = sb([P, G, NH, NG + 1])
        tri_s = sb([P, 2, P])
        top = sb([P, G * NH])
        top_row = sb([G * NH, P], BF16)
        p = [sb([P, 2, GW]) for u in range(2)]
        inv = sb([P, NKV, 2, G])
        y = full[:].rearrange("p (b h e) -> p b h e", b=G, h=NH)
        r = rest[:].rearrange("p (b d) -> p b d", b=G)
        xn = full[:].rearrange("p (b d) -> p b d", b=G)
        s_ps = [ps([P, 2, GW]) for u in range(2)]
        acc = ps([P, NKV, 512])
        pa_ps, pb_ps = ps([P, GW]), ps([P, GW])
        acc_v = [acc[:, kv, 0:2 * G * HV].rearrange("p (h b e) -> p h b e", h=2, e=HV) for kv in range(NKV)]

        weights_in, cos_in, sin_in = sem("weights_in"), sem("cos_in"), sem("sin_in")
        scaled, rms_ready, ones_set, chain = sem("scaled"), sem("rms_ready"), sem("ones_set"), sem("chain")
        xn_ready, tr_done, xs_ready, proj_done = sem("xn_ready"), sem("tr_done"), sem("xs_ready"), sem("proj_done")
        rotated, high_ready, rest_ready, mid_ready, parts_ready = (
            sem(n) for n in ("rotated", "high_ready", "rest_ready", "mid_ready", "parts_ready"))
        parts_out, parts_in, kb_copied = sem("parts_out"), sem("parts_in"), sem("kb_copied")
        s1_done, s1_taken, tri_added, top_ready = sem("s1_done"), sem("s1_taken"), sem("tri_added"), sem("top_ready")
        top_done, top_copied, top_in = sem("top_done"), sem("top_copied"), sem("top_in")
        s2_done, p_ready, p_masked, p_used = sem("s2_done"), sem("p_ready"), sem("p_masked"), sem("p_used")
        y_ready, y_tr_done, yT_ready, o_done, o_taken = (
            sem(n) for n in ("y_ready", "y_tr_done", "yT_ready", "o_done", "o_taken"))
        pe_passed = sem("pe_passed")
        r_ready, r_out, acc_taken = sem("r_ready"), sem("r_out"), sem("acc_taken")
        block = ctx.enter_context(nc.Block())
        loads = [(w_q[:], d["at_w_q"]), (w_qr[:], d["at_w_qr"]), (w_k[:], d["at_w_k"]), (w_kr[:], d["at_w_kr"]),
                 (w_v[:], d["at_w_v"]), (w_o[:], d["at_w_o"]), (ln1[:], d["at_ln1"]), (tri[:], d["at_tri"])]

        def first_units(c):
            return G * NKV * c * (c + 1) // 2

        def second_units(c):
            return NKV * G * c * (c + 1) // 2

        @block.sync
        def _(sp):
            for out, src in loads:
                sp.dma_start(out, src).then_inc(weights_in, 16)
            for c in range(NG):
                cols = slice(c * GW, (c + 1) * GW)
                if c:
                    sp.wait_ge(rotated, 4 * c)
                sp.dma_start(cos[:], d["at_cos"][:, cols]).then_inc(cos_in, 16)
                sp.dma_start(sin[:], d["at_sin"][:, cols]).then_inc(sin_in, 16)
                sp.wait_ge(parts_ready, 2 * c + 2)
                sp.dma_start(q_parts.rearrange("n p t -> p n t"), qp[:]).then_inc(parts_out, 16)
                sp.dma_start(k_parts.rearrange("n p t -> p n t"), kp[:]).then_inc(parts_out, 16)
                sp.wait_ge(parts_out, 32 * c + 32)
                if c:
                    sp.wait_ge(s2_done, second_units(c))
                for row, part in enumerate((0, 0, 0, 1)):
                    sp.dma_start(qa[row * HD:(row + 1) * HD, :, :],
                                 q_parts[part].rearrange("(h r) t -> r h t", r=HD)).then_inc(parts_in, 16)
                for row, part in enumerate((2, 1)):
                    sp.dma_start(qb[row * HD:(row + 1) * HD, :, :],
                                 q_parts[part].rearrange("(h r) t -> r h t", r=HD)).then_inc(parts_in, 16)
                for row, part in enumerate((0, 1, 2, 0)):
                    sp.dma_start(ka[row * HD:(row + 1) * HD, :, cols],
                                 k_parts[part].rearrange("(h r) t -> r h t", r=HD)).then_inc(parts_in, 16)
                for row, part in enumerate((0, 1)):
                    sp.dma_start(kb[row * HD:(row + 1) * HD, :, cols],
                                 k_parts[part].rearrange("(h r) t -> r h t", r=HD)).then_inc(parts_in, 16)
                sp.wait_ge(top_copied, c + 1)
                sp.dma_start(qb[2 * HD:2 * HD + 1, :, :], top_row[:]).then_inc(top_in, 16)
                sp.wait_ge(r_ready, c + 1)
                sp.dma_start(dram_r[cols, :].rearrange("(t p) d -> p t d", p=P), r).then_inc(r_out, 16)
            sp.wait_ge(r_out, 16 * NG)

        @block.gpsimd
        def _(pool):
            nc.gpsimd.memset(v[:, :, :, HD:HV], 1.0).then_inc(ones_set, 1)
            for c in range(NG):
                for j in range(G):
                    for u in range(NKV):
                        pool.wait_ge(p_ready, second_units(c) + NKV * (G * c + j) + u + 1)
                        tile = p[u][:, :, j * P:(j + 1) * P]
                        nc.gpsimd.affine_select(out=tile, in_=tile, compare_op=ALU.is_ge, fill=0.0, base=0,
                                                pattern=[[0, 2], [1, P]], channel_multiplier=-1).then_inc(p_masked, 1)

        @block.tensor
        def _(pe):
            def first_scores(c, sc, b, kv, width):
                unit = b * NKV + kv
                at = first_units(c) + sc * (G * NKV) + unit
                if is_later(at - 1):
                    wait_apart(pe, s1_taken, at - 1, pe_passed)
                for h in range(2):
                    ins = nc.tensor.matmul(s_ps[unit % 2][:, h, 0:width], qa[0:HD, kv * 2 + h, b * P:(b + 1) * P],
                                           ka[0:HD, kv, bass.ds(sc * GW, width)], start=True, stop=True)
                ins.then_inc(s1_done, 1)

            def scores(c, j, kv, lo=0):
                at = second_units(c) + NKV * j + kv
                if is_later(at - 1):
                    pe.wait_ge(p_ready, at - 1)
                for h in range(2):
                    keys, head, out = bass.ds(j * P, P), kv * 2 + h, s_ps[kv][:, h, lo:GW]
                    nc.tensor.matmul(out, ka[:, kv, keys], qa[:, head, lo:GW], start=True, stop=False)
                    ins = nc.tensor.matmul(out, kb[:, kv, keys], qb[:, head, lo:GW], start=False, stop=True)
                ins.then_inc(s2_done, 1)

            def values(c, j, kv, first=False, diagonal=None):
                at = second_units(c) + NKV * j + kv
                if diagonal is None:
                    pe.wait_ge(p_ready, at + 1)
                else:
                    pe.wait_ge(p_masked, NKV * (G * c + diagonal) + kv + 1)
                for h in range(2):
                    for b in range(diagonal or 0, G):
                        ins = nc.tensor.matmul(acc_v[kv][:, h, b, :], p[kv][:, h, b * P:(b + 1) * P], v[:, bass.ds(j, 1), kv, :],
                                               start=first and h == 0 and b == 0, stop=diagonal == b, skip_group_check=True)
                ins.then_inc(p_used, 1)

            pe.wait_ge(weights_in, 16 * len(loads))
            pe.wait_ge(ones_set, 2)
            for c in range(NG):
                pe.wait_ge(xn_ready, c + 1)
                for j in range(G):
                    ins = nc.tensor.transpose(pa_ps[:, j * P:(j + 1) * P], xn[:, j, :], k.ident[:])
                ins.then_inc(tr_done, 1)
                pe.wait_ge(xs_ready, c + 1)
                if c:
                    pe.wait_ge(p_ready, second_units(c))
                nc.tensor.matmul(s_ps[0][:, 0, :], w_q[:], xs[:], start=True, stop=True)
                nc.tensor.matmul(s_ps[0][:, 1, :], w_qr[:], xs[:], start=True, stop=True)
                nc.tensor.matmul(s_ps[1][0:KW, 0, :], w_k[:], xs[:], start=True, stop=True)
                nc.tensor.matmul(s_ps[1][0:KW, 1, :], w_kr[:], xs[:], start=True, stop=True)
                for j in range(G):
                    ins = nc.tensor.matmul(pb_ps[:, j * KW:(j + 1) * KW], xs[:, j * P:(j + 1) * P], w_v[:], start=True, stop=True)
                ins.then_inc(proj_done, 1)
                pe.wait_ge(parts_in, 16 * 12 * (c + 1))
                if c:
                    with pe.Fori(0, c) as sc:
                        for b in range(G):
                            for kv in range(NKV):
                                first_scores(c, sc, b, kv, GW)
                for b in range(G):
                    for kv in range(NKV):
                        first_scores(c, c, b, kv, (b + 1) * P)
                pe.wait_ge(top_ready, c + 1)
                nc.tensor.transpose(pa_ps[0:G * NH, 0:P], top[:], k.ident[:]).then_inc(top_done, 1)
                pe.wait_ge(top_in, 16 * (c + 1))
                pe.wait_ge(s1_taken, first_units(c + 1))
                if c:
                    pe.wait_ge(acc_taken, c)
                scores(c, 0, 0)
                if c:
                    for kv in range(NKV):
                        scores(c, 0 + (kv == 1), 1 - kv)
                        values(c, 0, kv, first=True)
                    with pe.Fori(1, G * c) as j:
                        scores(c, j, 1)
                        values(c, j, 0)
                        scores(c, j + 1, 0)
                        values(c, j, 1)
                for j in range(G):
                    tile = G * c + j
                    scores(c, tile, 1, j * P)
                    values(c, tile, 0, first=tile == 0, diagonal=j)
                    if j + 1 < G:
                        scores(c, tile + 1, 0, (j + 1) * P)
                    values(c, tile, 1, first=tile == 0, diagonal=j)
                pe.wait_ge(y_ready, c + 1)
                for b in range(G):
                    ins = nc.tensor.transpose(pa_ps[:, b * P:(b + 1) * P], y[:, b, :, :].rearrange("p h e -> p (h e)"), k.ident[:])
                ins.then_inc(y_tr_done, 1)
                pe.wait_ge(yT_ready, c + 1)
                for b in range(G):
                    ins = nc.tensor.matmul(pb_ps[:, b * P:(b + 1) * P], xs[:, b * P:(b + 1) * P], w_o[:], start=True, stop=True)
                ins.then_inc(o_done, 1)

        @block.scalar
        def _(act):
            act.wait_ge(scaled, 1)
            nc.scalar.activation(rms[:], rms[:], ACT.Sqrt).then_inc(rms_ready, 1)
            act.wait_ge(weights_in, 16 * len(loads))
            for c in range(NG):
                act.wait_ge(tr_done, c + 1)
                nc.scalar.activation(xs[:], pa_ps[:], ACT.Copy, scale=ln1[:]).then_inc(xs_ready, 1)
                for n, (w, parts) in enumerate(((P, qp), (KW, kp))):
                    act.wait_ge(rotated, 4 * c + 2 * n + 2)
                    if c:
                        act.wait_ge(parts_out, 32 * c)
                    nc.scalar.activation(parts[:, 0, :], full[0:w, :], ACT.Copy).then_inc(high_ready, 1)
                    act.wait_ge(rest_ready, 2 * c + n + 1)
                    nc.scalar.activation(parts[:, 1, :], rest[0:w, :], ACT.Copy).then_inc(mid_ready, 1)
                act.wait_ge(top_done, c + 1)
                if c:
                    act.wait_ge(top_in, 16 * c)
                nc.scalar.activation(top_row[:], pa_ps[0:G * NH, 0:P], ACT.Copy, scale=-1.0).then_inc(top_copied, 1)

                def exps(j, kv, lo=0):
                    at = second_units(c) + NKV * j + kv
                    act.wait_ge(s2_done, at + 1)
                    if is_later(at - 1):
                        act.wait_ge(p_used, at - 1)
                    nc.scalar.activation(p[kv][:, :, lo:GW], s_ps[kv][:, :, lo:GW], ACT.Exp).then_inc(p_ready, 1)

                if c:
                    with act.Fori(0, G * c) as j:
                        for kv in range(NKV):
                            exps(j, kv)
                for j in range(G):
                    for kv in range(NKV):
                        exps(G * c + j, kv, j * P)
                act.wait_ge(y_tr_done, c + 1)
                nc.scalar.activation(xs[:], pa_ps[:], ACT.Copy).then_inc(yT_ready, 1)

        @block.vector
        def _(dve):
            links = [0]

            def link(ins):
                links[0] += 1
                ins.then_inc(chain, 1)
                dve.wait_ge(chain, links[0])

            nc.vector.memset(kb[2 * HD:2 * HD + 1, :, :], 1.0).then_inc(ones_set, 1)
            link(nc.vector.tensor_tensor(rms[:], k.rstd[:], k.rstd[:], ALU.mult))
            link(nc.vector.tensor_tensor(rms[:], rms[:], k.var[:], ALU.mult))
            nc.vector.tensor_scalar(rms[:], rms[:], 1e-6, None, ALU.add).then_inc(scaled, 1)
            dve.wait_ge(rms_ready, 1)
            link(nc.vector.reciprocal(rms[:], rms[:]))
            nc.vector.tensor_tensor(h_scale[:], k.rstd[:], rms[:], ALU.mult)
            link(nc.vector.tensor_tensor(h_shift[:], k.shift[:], rms[:], ALU.mult))
            dve.wait_ge(weights_in, 16 * len(loads))
            for c in range(NG):
                for j in range(G):
                    at = c * G + j
                    ins = nc.vector.tensor_scalar(xn[:, j, :], x[:, at, :], h_scale[:, at:at + 1], h_shift[:, at:at + 1],
                                                  ALU.mult, ALU.add)
                ins.then_inc(xn_ready, 1)
                dve.wait_ge(proj_done, c + 1)
                dve.wait_ge(cos_in, 16 * (c + 1))
                dve.wait_ge(sin_in, 16 * (c + 1))
                if c:
                    dve.wait_ge(parts_out, 32 * c)
                if c:
                    dve.wait_ge(r_out, 16 * c)
                for n, (w, parts, mul) in enumerate(((P, qp, scale), (KW, kp, 1.0))):
                    if n:
                        dve.wait_ge(parts_ready, 2 * c + 1)
                    nc.vector.scalar_tensor_tensor(out=full[0:w, :], in0=s_ps[n][0:w, 0, :], scalar=mul, in1=cos[0:w, :],
                                                   op0=ALU.mult, op1=ALU.mult)
                    nc.vector.scalar_tensor_tensor(out=rest[0:w, :], in0=s_ps[n][0:w, 1, :], scalar=mul, in1=sin[0:w, :],
                                                   op0=ALU.mult, op1=ALU.mult).then_inc(rotated, 1)
                    dve.wait_ge(rotated, 4 * c + 2 * n + 1)
                    nc.vector.tensor_tensor(full[0:w, :], full[0:w, :], rest[0:w, :], ALU.add).then_inc(rotated, 1)
                    dve.wait_ge(high_ready, 2 * c + n + 1)
                    dve.wait_ge(rotated, 4 * c + 2 * n + 2)
                    nc.vector.tensor_tensor(rest[0:w, :], full[0:w, :], parts[:, 0, :], ALU.subtract).then_inc(rest_ready, 1)
                    dve.wait_ge(rest_ready, 2 * c + n + 1)
                    dve.wait_ge(mid_ready, 2 * c + n + 1)
                    nc.vector.tensor_tensor(parts[:, 2, :], rest[0:w, :], parts[:, 1, :], ALU.subtract).then_inc(parts_ready, 1)
                nc.vector.tensor_copy(v[:, c * G:(c + 1) * G, :, 0:HD],
                                      pb_ps[:, 0:G * KW].rearrange("p (t h e) -> p t h e", t=G, e=HD))
                link(nc.vector.memset(tops[:], -1e30))

                def greatest(sc, b, kv, width):
                    unit = b * NKV + kv
                    at = first_units(c) + sc * (G * NKV) + unit
                    dve.wait_ge(s1_done, at + 1)
                    out = tops[:, b, kv * 2:kv * 2 + 2, bass.ds(sc, 1)]
                    return nc.vector.tensor_reduce(out, s_ps[unit % 2][:, :, 0:width], AX.X, ALU.max)

                if c:
                    with dve.Fori(0, c) as sc:
                        for b in range(G):
                            for kv in range(NKV):
                                greatest(sc, b, kv, GW).then_inc(s1_taken, 1)
                for b in range(G):
                    for kv in range(NKV):
                        unit = b * NKV + kv
                        dve.wait_ge(s1_done, first_units(c) + c * G * NKV + unit + 1)
                        if unit:
                            dve.wait_ge(s1_taken, first_units(c) + c * G * NKV + unit)
                        nc.vector.tensor_tensor(tri_s[:], s_ps[unit % 2][:, :, b * P:(b + 1) * P],
                                                tri[:, None, :].to_broadcast([P, 2, P]), ALU.add).then_inc(tri_added, 1)
                        if b:
                            greatest(c, b, kv, b * P)
                        dve.wait_ge(tri_added, c * G * NKV + unit + 1)
                        nc.vector.tensor_reduce(tops[:, b, kv * 2:kv * 2 + 2, NG:NG + 1], tri_s[:], AX.X, ALU.max).then_inc(s1_taken, 1)
                dve.wait_ge(s1_taken, first_units(c + 1))
                nc.vector.tensor_reduce(top[:].rearrange("p (h b) -> p b h", h=NH), tops[:], AX.X, ALU.max).then_inc(top_ready, 1)
                dve.wait_ge(p_used, second_units(c + 1))
                for kv in range(NKV):
                    ins = nc.vector.reciprocal(inv[:, kv, :, :], acc_v[kv][:, :, :, HD])
                link(ins)
                for kv in range(NKV):
                    for h in range(2):
                        ins = nc.vector.tensor_tensor(y[:, :, kv * 2 + h, :], acc_v[kv][:, h, :, 0:HD],
                                                      inv[:, kv, h, :, None].to_broadcast([P, G, HD]), ALU.mult)
                ins.then_inc(y_ready, 1)
                dve.wait_ge(y_ready, c + 1)
                dve.sem_inc(acc_taken, 1)
                for j in range(G):
                    at = c * G + j
                    ins = nc.vector.tensor_scalar(r[:, j, :], x[:, at, :], k.rstd[:, at:at + 1], k.shift[:, at:at + 1],
                                                  ALU.mult, ALU.add)
                link(ins)
                dve.wait_ge(o_done, c + 1)
                nc.vector.tensor_tensor(r, r, pb_ps[:].rearrange("p (b d) -> p b d", b=G), ALU.add).then_inc(r_ready, 1)
                dve.wait_ge(r_ready, c + 1)
                xc = x[:, c * G:(c + 1) * G, :]
                link(nc.vector.tensor_tensor(xc, xc, r, ALU.add))




def load_all(k):
    nc = k.nc
    with ExitStack() as ctx:
        x_in = ctx.enter_context(nc.semaphore("x_in"))
        block = ctx.enter_context(nc.Block())

        @block.sync
        def _(sp):
            sp.dma_start(k.x[:], k.dram["x"].rearrange("(t p) d -> p t d", p=P)).then_inc(x_in, 16)
            sp.dma_start(k.ident[:], k.dram["ident"]).then_inc(x_in, 16)
            sp.wait_ge(x_in, 32)

        @block.vector
        def _(dve):
            nc.vector.memset(k.ones[:], 1.0)


def store_all(k):
    nc = k.nc
    with ExitStack() as ctx:
        x_out = ctx.enter_context(nc.semaphore("x_out"))
        block = ctx.enter_context(nc.Block())

        @block.sync
        def _(sp):
            sp.dma_start(k.out.rearrange("(t p) d -> p t d", p=P), k.x[:]).then_inc(x_out, 16)
            sp.wait_ge(x_out, 16)


def program(nc, dram, out, first=0, last=8):
    with ExitStack() as ctx:
        k = Kernel(nc, dram)
        k.out = out
        sb = lambda n, shape, dt=F32: ctx.enter_context(nc.sbuf_tensor(n, shape, dt))
        k.mask = sb("mask", [P, T, N], U8)
        k.x = sb("x_sb", [P, T, D])
        k.ident, k.ones = sb("ident_sb", [P, P]), sb("ones_sb", [P, P])
        k.rstd, k.shift, k.var = sb("rstd", [P, T]), sb("shift", [P, T]), sb("var", [P, T])
        k.work = Workspace(sb("work", [P, WORK]), WORK)
        k.banks = Workspace(ctx.enter_context(nc.psum_tensor("banks", [P, BANKS * 512], F32)), BANKS * 512)
        load_all(k)
        loaded = False
        for s in range(first, last):
            if s in (0, 2, 4, 6):
                gnn_layer(k, f"L{s // 2}g", {0: "elu", 2: "leaky", 4: "tanh", 6: "leaky"}[s], load_adj=not loaded)
                loaded = True
            elif s == 1:
                ffn0_layer(k)
            else:
                ffn_layer(k, s // 2)
        store_all(k)


def lay_out(w):
    c = np.ascontiguousarray
    a = {"x": w["x"], "adjT": c(w["adj"].T), "ident": np.eye(P, dtype=np.float32)}
    for n, W, vec in ((0, w["L0_gnn_W"], w["L0_gnn_a"]), (1, w["L1_gnn_W_w"], w["L1_gnn_a"]),
                      (3, w["L3_gnn_W"].T, w["L3_gnn_a_vec"])):
        a[f"L{n}g_W"], a[f"L{n}g_WT"] = c(W), c(W.T)
        a[f"L{n}g_a2"] = c(vec.reshape(2, D).T)
    a["L2g_W"], a["L2g_a_row"] = w["L2_gnn_W"], c(w["L2_gnn_a"].reshape(D))
    for n, b in ((1, w["L1_gnn_W_b"]), (2, w["L2_gnn_b"]), (3, w["L3_gnn_b_W"])):
        a[f"L{n}g_b_row"] = b
    for n, b in ((1, w["L1_gnn_W_b"]), (3, w["L3_gnn_b_W"])):
        a[f"L{n}g_b_col"] = c(b.reshape(D, 1))
    a["L3g_ba"] = w["L3_gnn_b_a"]
    def inward(W):
        return c(W.transpose(1, 0, 2))

    def outward(W):
        e, h, d = W.shape
        tiles = -(-h // P)
        return c(np.pad(W, ((0, 0), (0, tiles * P - h), (0, 0))).reshape(e, tiles, P, d).transpose(2, 0, 1, 3))

    def by_hidden(b):
        return c(b.reshape(b.shape[0], -1, P).transpose(2, 0, 1))

    a["L0f_w_in"], a["L0f_w_up"] = (c(w[f"L0_ffn_{n}"].transpose(2, 0, 1)) for n in ("w1", "w3"))
    a["L0f_w_out"] = outward(w["L0_ffn_w2"].transpose(0, 2, 1))
    a["L0f_r_w"], a["L0f_ln2"] = c(w["L0_ffn_router_w"].T), c(w["L0_ffn_ln2_w"].reshape(D, 1))
    halves = np.concatenate([np.arange(HD // 2, HD), np.arange(HD // 2)])

    def rotated(W):
        return c(W.reshape(-1, HD, D)[:, halves].reshape(-1, D).T)

    for n, W in (("q", w["L0_ffn_wq"]), ("k", w["L0_ffn_wk"])):
        a[f"at_w_{n}"], a[f"at_w_{n}r"] = c(W.T), rotated(W)
    a["at_w_v"], a["at_w_o"] = c(w["L0_ffn_wv"].T), c(w["L0_ffn_wo"].T)
    a["at_ln1"] = c(w["L0_ffn_ln1_w"].reshape(D, 1))
    inv_freq = 1.0 / 10000.0 ** (np.arange(0, HD, 2, dtype=np.float32) / HD)
    angle = np.outer(np.arange(N, dtype=np.float32), inv_freq)
    angle = np.concatenate([angle, angle], axis=-1)
    sign = np.where(np.arange(HD) < HD // 2, -1.0, 1.0).astype(np.float32)
    a["at_cos"] = c(np.tile(np.cos(angle).T, (NH, 1)).astype(np.float32))
    a["at_sin"] = c(np.tile((np.sin(angle) * sign).T, (NH, 1)).astype(np.float32))
    a["at_tri"] = np.where(np.arange(P)[None, :] <= np.arange(P)[:, None], 0.0, -1e30).astype(np.float32)
    a["L1f_w_in"], a["L1f_w_mid"] = inward(w["L1_ffn_expert_w1"]), inward(w["L1_ffn_expert_w2"])
    a["L1f_w_out"] = outward(w["L1_ffn_expert_w3"])
    a["L1f_b_in"], a["L1f_b_mid"] = by_hidden(w["L1_ffn_expert_b1"]), c(w["L1_ffn_expert_b2"].T)
    a["L1f_b_out"] = w["L1_ffn_expert_b3"]
    a["L1f_r_w"], a["L1f_r_b"] = w["L1_ffn_router_w2"], w["L1_ffn_router_b2"]
    a["L1f_r_w1"], a["L1f_r_b1"] = w["L1_ffn_router_w1"], c(w["L1_ffn_router_b1"].reshape(-1, 1))
    for n in (2, 3):
        a[f"L{n}f_w_in"], a[f"L{n}f_w_out"] = inward(w[f"L{n}_ffn_W1"]), outward(w[f"L{n}_ffn_W2"])
        a[f"L{n}f_b_in"], a[f"L{n}f_b_out"] = by_hidden(w[f"L{n}_ffn_b1"]), w[f"L{n}_ffn_b2"]
        a[f"L{n}f_r_w"], a[f"L{n}f_r_b"] = w[f"L{n}_ffn_Wg"], w[f"L{n}_ffn_bg"]
    a["L2f_r_b2"] = w["L2_ffn_bias"]
    return a


def kernel(**inputs):
    import concourse.bacc as bacc
    from concourse.bass_utils import run_bass_kernel_spmd
    nc = bacc.Bacc("TRN2", target_bir_lowering=False, num_devices=1, dynamic_dma_scratch_size=1024)
    arrays, dram = {}, {}
    for name, a in lay_out({n: np.asarray(v) for n, v in inputs.items()}).items():
        arrays[f"in_{name}_dram"] = a
        dram[name] = nc.dram_tensor(f"in_{name}_dram", a.shape, mybir.dt.from_np(a.dtype), kind="ExternalInput").ap()
    out = nc.dram_tensor("out_0_dram", (N, D), F32, kind="ExternalOutput").ap()
    program(nc, dram, out)
    return run_bass_kernel_spmd(nc, [arrays], core_ids=[0]).results[0]["out_0_dram"]
```

```python
from contextlib import ExitStack, contextmanager

import numpy as np

import concourse.bass as bass
from concourse import mybir

ALU = mybir.AluOpType
ACT = mybir.ActivationFunctionType
AX = mybir.AxisListType
F32 = mybir.dt.float32
BF16 = mybir.dt.bfloat16
U8 = mybir.dt.uint8
I32 = mybir.dt.int32
RMAX = bass.bass_isa.ReduceOp.max

P = 128
N = 4096
D = 128
T = N // P
G = 4
NG = T // G
GW = G * P
IC = 1024
NI = N // IC
NB = IC // P
VW = D + 1
ROW_MAX = 70.0
EPS = 1e-5
WORK = 19638
BANKS = 8


class Workspace:

    def __init__(self, tensor, width):
        self.tensor, self.width, self.used = tensor, width, 0

    def cut(self, shape, dt=F32, align=1):
        size = {F32: 4, I32: 4, BF16: 2, U8: 1}[dt]
        n = int(np.prod(shape[1:]))
        columns = -(-n * size // 4)
        start = -(-self.used // align) * align
        assert start + columns <= self.width, (shape, start, self.width)
        self.used = start + columns
        flat = self.tensor[0:shape[0], start:start + columns]
        if dt != F32:
            flat = flat.bitcast(dt)[:, 0:n]
        names = [f"d{i}" for i in range(len(shape) - 1)]
        if len(names) > 1:
            flat = flat.rearrange(f"p ({' '.join(names)}) -> p {' '.join(names)}", **dict(zip(names, shape[1:])))
        return flat


@contextmanager
def stage(k):
    marks, before = (k.work.used, k.banks.used), k.nc.snapshot_sems()
    yield
    k.work.used, k.banks.used = marks
    taken = k.nc.allocated_since(before)
    if taken:
        k.nc.clear_and_free_semaphores(taken)
        k.nc.all_engine_barrier()


class Kernel:

    def __init__(self, nc, dram):
        self.nc, self.dram = nc, dram


def is_later(count):
    return not isinstance(count, int) or count > 0


def wait_apart(engine, sem, value, passed):
    engine.wait_ge(sem, value).then_inc(passed, 1)




def tile_stats(k, at):
    return k.nc.vector.bn_stats(k.stats[:, at, :], k.x[:, at, :])


class LayerNorm:

    def __init__(self, k, name):
        self.k = k
        self.mean2, self.diff, self.m2, self.std = (k.work.cut([P, T]) for _ in range(4))
        self.step_done, self.var_ready, self.std_ready = (
            k.nc.alloc_semaphore(f"{name}_ln_{n}") for n in ("step_done", "var_ready", "std_ready"))

    def vector_part(self, dve):
        k, nc, mean2, diff, m2, step_done = self.k, self.k.nc, self.mean2, self.diff, self.m2, self.step_done
        even_mean, even_m2, odd_mean, odd_m2 = (k.stats[:, :, n] for n in (1, 2, 4, 5))
        nc.vector.tensor_tensor(mean2[:], even_mean, odd_mean, ALU.add)
        nc.vector.tensor_tensor(m2[:], even_m2, odd_m2, ALU.add)
        nc.vector.tensor_tensor(diff[:], even_mean, odd_mean, ALU.subtract).then_inc(step_done, 1)
        dve.wait_ge(step_done, 1)
        nc.vector.scalar_tensor_tensor(out=diff[:], in0=diff[:], scalar=0.25, in1=diff[:],
                                       op0=ALU.mult, op1=ALU.mult).then_inc(step_done, 1)
        dve.wait_ge(step_done, 2)
        nc.vector.scalar_tensor_tensor(out=k.var[:], in0=m2[:], scalar=1.0 / D, in1=diff[:],
                                       op0=ALU.mult, op1=ALU.add).then_inc(step_done, 1)
        dve.wait_ge(step_done, 3)
        nc.vector.tensor_scalar(m2[:], k.var[:], EPS, None, ALU.add).then_inc(self.var_ready, 1)
        dve.wait_ge(self.std_ready, 1)
        nc.vector.reciprocal(k.rstd[:], self.std[:]).then_inc(step_done, 1)
        dve.wait_ge(step_done, 4)
        nc.vector.scalar_tensor_tensor(out=k.shift[:], in0=mean2[:], scalar=-0.5, in1=k.rstd[:],
                                       op0=ALU.mult, op1=ALU.mult).then_inc(step_done, 1)
        dve.wait_ge(step_done, 5)

    def scalar_part(self, act):
        act.wait_ge(self.var_ready, 1)
        self.k.nc.scalar.activation(self.std[:], self.m2[:], ACT.Sqrt).then_inc(self.std_ready, 1)




def gnn_layer(k, name, kind, load_adj=False):
    nc, d = k.nc, k.dram
    with stage(k), ExitStack() as ctx:
        sb = lambda shape, dt=F32: k.work.cut(shape, dt)
        t = {
            "V": sb([P, T, VW]),
            "a_row": sb([P, N]) if kind != "tanh" else None,
            "b_col": sb([P, T]),
            "b_exp": sb([P, T]),
            "all_sum": sb([P, D]),
        }
        gnn_project(k, name, kind, t)
        gnn_attend(k, name, kind, t, load_adj)


def gnn_project(k, name, kind, t):
    nc, x = k.nc, k.x
    V, a_row, b_col, b_exp = t["V"], t["a_row"], t["b_col"], t["b_exp"]
    tanh = kind == "tanh"
    bias = k.dram.get(f"{name}_b_row")
    with stage(k), ExitStack() as ctx:
        sb = lambda shape, dt=F32: k.work.cut(shape, dt)
        sem = lambda n: nc.alloc_semaphore(f"{name}_{n}")
        ps = lambda shape: k.banks.cut(shape, align=512)
        W, WT = sb([P, D]), sb([P, D])
        a2 = sb([P, 2])
        wa = sb([P, 2])
        wa_wide = sb([P, P])
        b_row, b_wide, bc = sb([P, D]), sb([P, P]), sb([P, 1])
        ba = sb([P, 1])
        aw_row = sb([P, D])
        const2 = sb([P, 2])
        xn = [sb([P, G, D]) for u in range(2)]
        xT = [sb([P, GW]) for u in range(2)]
        h = [sb([P, G, D]) for u in range(2)] if tanh else None
        h_sum = sb([P, T]) if tanh else None
        b_top, b_all = sb([P, 1]), sb([P, 1])
        v_sum = sb([P, D])
        xT_ps = [ps([P, GW]) for u in range(2)]
        v_ps = [ps([P, G, D]) for u in range(2)]
        a_ps = [ps([P, GW]) for u in range(2)]
        s_ps = ps([P, 512])
        b_ps, wa_ps, c_ps, sum_ps = s_ps[:, 0:T], s_ps[:, 64:66], s_ps[:, 68:70], s_ps[:, 128:128 + D]

        weights_in, ones_set = sem("weights_in"), sem("ones_set")
        wa_done, wa_ready, const_ready, wide_ready = (sem(n) for n in ("wa_done", "wa_ready", "const_ready", "wide_ready"))
        xn_ready, tr_done, xT_ready = sem("xn_ready"), sem("tr_done"), sem("xT_ready")
        v_done, v_taken, a_taken = sem("v_done"), sem("v_taken"), sem("a_taken")
        h_ready, h_tanh, h_summed, h_scaled, h_taken = (
            sem(n) for n in ("h_ready", "h_tanh", "h_summed", "h_scaled", "h_taken"))
        chain, top_ready, top_all, shifted, exp_ready = (
            sem(n) for n in ("chain", "top_ready", "top_all", "shifted", "exp_ready"))
        vsum_ready, sum_done = sem("vsum_ready"), sem("sum_done")
        block = ctx.enter_context(nc.Block())
        ln = LayerNorm(k, name)
        dr = k.dram
        loads = [(W[:], dr[f"{name}_W"])]
        if tanh:
            loads += [(aw_row[:], dr[f"{name}_a_row"].partition_broadcast(P))]
        else:
            loads += [(WT[:], dr[f"{name}_WT"]), (a2[:], dr[f"{name}_a2"])]
        if bias is not None:
            loads += [(b_row[:], bias.partition_broadcast(P))]
            if not tanh:
                loads += [(bc[:], dr[f"{name}_b_col"])]
        has_ba = f"{name}_ba" in dr
        if has_ba:
            loads += [(ba[:], dr[f"{name}_ba"].partition_broadcast(P))]

        @block.sync
        def _(sp):
            for out, src in loads:
                sp.dma_start(out, src).then_inc(weights_in, 16)

        @block.gpsimd
        def _(pool):
            nc.gpsimd.memset(V[:, :, D:VW], 1.0).then_inc(ones_set, 1)
            pool.wait_ge(top_ready, 1)
            nc.gpsimd.partition_all_reduce(b_all[:], b_top[:], P, RMAX).then_inc(top_all, 1)

        @block.tensor
        def _(pe):
            def transposes(g, u):
                pe.wait_ge(xn_ready, g + 1)
                if is_later(g - 1):
                    pe.wait_ge(xT_ready, g - 1)
                for j in range(G):
                    last = nc.tensor.transpose(xT_ps[u][:, j * P:(j + 1) * P], xn[u][:, j, :], k.ident[:])
                last.then_inc(tr_done, 1)

            def project(g, u):
                pe.wait_ge(xT_ready, g + 1)
                if is_later(g - 1):
                    pe.wait_ge(v_taken, g - 1)
                    if not tanh:
                        pe.wait_ge(a_taken, g - 1)
                for j in range(G):
                    block_T = xT[u][:, j * P:(j + 1) * P]
                    last = nc.tensor.matmul(v_ps[u][:, j, :], block_T, W[:], start=True, stop=True)
                    if not tanh:
                        nc.tensor.matmul(b_ps[:, bass.ds(g * G + j, 1)], block_T, wa[:, 1:2], start=True, stop=True)
                if not tanh:
                    last = nc.tensor.matmul(a_ps[u][:], wa_wide[:], xT[u][:], start=True, stop=True)
                last.then_inc(v_done, 1)

            for u in range(2):
                transposes(u, u)
            pe.wait_ge(weights_in, 16 * len(loads))
            if not tanh:
                nc.tensor.matmul(wa_ps, WT[:], a2[:], start=True, stop=True).then_inc(wa_done, 1)
                if bias is not None:
                    pe.wait_ge(wide_ready, 1)
                    nc.tensor.matmul(c_ps, b_wide[:], a2[:], start=True, stop=True).then_inc(wa_done, 1)
                pe.wait_ge(wa_ready, 1)
                pe.wait_ge(const_ready, 1)
            for u in range(2):
                transposes(2 + u, u)
            for u in range(2):
                project(u, u)
            with pe.Fori(1, NG // 2 - 1) as i:
                for u in range(2):
                    transposes(i * 2 + (2 + u), u)
                for u in range(2):
                    project(i * 2 + u, u)
            for u in range(2):
                project(NG - 2 + u, u)
            if not tanh:
                pe.wait_ge(vsum_ready, 1)
                nc.tensor.matmul(sum_ps, k.ones[:], v_sum[:], start=True, stop=True).then_inc(sum_done, 1)

        @block.scalar
        def _(act):
            def copy_T(g, u):
                act.wait_ge(tr_done, g + 1)
                if is_later(g - 1):
                    act.wait_ge(v_done, g - 1)
                nc.scalar.activation(xT[u][:], xT_ps[u][:], ACT.Copy).then_inc(xT_ready, 1)

            def take(g, u):
                if tanh:
                    act.wait_ge(h_ready, g + 1)
                    nc.scalar.activation(h[u][:], h[u][:], ACT.Tanh).then_inc(h_tanh, 1)
                else:
                    act.wait_ge(v_done, g + 1)
                    nc.scalar.activation(a_row[:, bass.ds(g * GW, GW)], a_ps[u][:], ACT.Identity,
                                         bias=const2[:, 0:1]).then_inc(a_taken, 1)

            ln.scalar_part(act)
            for u in range(2):
                copy_T(u, u)
            for u in range(2):
                copy_T(2 + u, u)
            if not tanh:
                act.wait_ge(const_ready, 1)
            for u in range(2):
                take(u, u)
            with act.Fori(1, NG // 2 - 1) as i:
                for u in range(2):
                    copy_T(i * 2 + (2 + u), u)
                for u in range(2):
                    take(i * 2 + u, u)
            for u in range(2):
                take(NG - 2 + u, u)
            act.wait_ge(shifted, 1)
            nc.scalar.activation(b_exp[:], b_col[:], ACT.Exp, scale=1.0 if tanh else 0.2).then_inc(exp_ready, 1)

        @block.vector
        def _(dve):
            links = [0]

            def link(ins):
                links[0] += 1
                ins.then_inc(chain, 1)
                dve.wait_ge(chain, links[0])

            def normalise(g, u):
                if is_later(g - 1):
                    dve.wait_ge(tr_done, g - 1)
                for j in range(G):
                    at = bass.ds(g * G + j, 1)
                    last = nc.vector.tensor_scalar(xn[u][:, j:j + 1, :], x[:, at, :], k.rstd[:, at], k.shift[:, at],
                                                   ALU.mult, ALU.add)
                last.then_inc(xn_ready, 1)

            def take(g, u):
                dve.wait_ge(v_done, g + 1)
                at = bass.ds(g * G, G)
                if tanh:
                    if is_later(g - 1):
                        dve.wait_ge(h_taken, g - 1)
                    nc.vector.tensor_tensor(h[u][:], v_ps[u][:], b_row[:, None, :].to_broadcast([P, G, D]),
                                            ALU.add).then_inc(h_ready, 1)
                    nc.vector.tensor_copy(V[:, at, 0:D], v_ps[u][:]).then_inc(v_taken, 1)
                elif bias is not None:
                    nc.vector.tensor_tensor(V[:, at, 0:D], v_ps[u][:], b_row[:, None, :].to_broadcast([P, G, D]),
                                            ALU.add).then_inc(v_taken, 1)
                else:
                    nc.vector.tensor_copy(V[:, at, 0:D], v_ps[u][:]).then_inc(v_taken, 1)

            def reduce_h(g, u):
                at = bass.ds(g * G, G)
                dve.wait_ge(h_tanh, g + 1)
                nc.vector.tensor_reduce(h_sum[:, at], h[u][:], AX.X, ALU.add).then_inc(h_summed, 1)
                dve.wait_ge(h_summed, g + 1)
                nc.vector.tensor_tensor(h[u][:], h[u][:], aw_row[:, None, :].to_broadcast([P, G, D]),
                                        ALU.mult).then_inc(h_scaled, 1)
                dve.wait_ge(h_scaled, g + 1)
                nc.vector.tensor_reduce(b_col[:, at], h[u][:], AX.X, ALU.add).then_inc(h_taken, 1)

            ln.vector_part(dve)
            for u in range(2):
                normalise(u, u)
            dve.wait_ge(weights_in, 16 * len(loads))
            if not tanh:
                if bias is not None:
                    nc.vector.tensor_copy(b_wide[:], bc[:, 0:1].to_broadcast([P, P])).then_inc(wide_ready, 1)
                dve.wait_ge(wa_done, 1 if bias is None else 2)
                link(nc.vector.tensor_copy(wa[:], wa_ps))
                nc.vector.tensor_copy(wa_wide[:], wa[:, 0:1].to_broadcast([P, P])).then_inc(wa_ready, 1)
                if bias is not None:
                    if has_ba:
                        link(nc.vector.tensor_copy(const2[:], c_ps))
                        nc.vector.tensor_tensor(const2[:, 0:1], const2[:, 0:1], ba[:], ALU.add).then_inc(const_ready, 1)
                    else:
                        nc.vector.tensor_copy(const2[:], c_ps).then_inc(const_ready, 1)
                else:
                    nc.vector.memset(const2[:], 0.0).then_inc(const_ready, 1)
            for u in range(2):
                normalise(2 + u, u)
            for u in range(2):
                take(u, u)
            if tanh:
                for u in range(2):
                    reduce_h(u, u)
            with dve.Fori(1, NG // 2 - 1) as i:
                for u in range(2):
                    normalise(i * 2 + (2 + u), u)
                for u in range(2):
                    take(i * 2 + u, u)
                if tanh:
                    for u in range(2):
                        reduce_h(i * 2 + u, u)
            for u in range(2):
                take(NG - 2 + u, u)
            if tanh:
                for u in range(2):
                    reduce_h(NG - 2 + u, u)
                dve.wait_ge(h_taken, NG)
            else:
                dve.wait_ge(v_taken, NG)
                link(nc.vector.tensor_scalar(b_col[:], b_ps, const2[:, 1:2], None, ALU.add))
            nc.vector.tensor_reduce(b_top[:], b_col[:], AX.X, ALU.max).then_inc(top_ready, 1)
            if not tanh:
                nc.vector.tensor_reduce(v_sum[:], V[:, :, 0:D].rearrange("p t d -> p d t"), AX.X, ALU.add).then_inc(vsum_ready, 1)
            dve.wait_ge(top_all, 1)
            nc.vector.tensor_scalar(b_col[:], b_col[:], b_all[:], None, ALU.subtract).then_inc(shifted, 1)
            if not tanh:
                dve.wait_ge(a_taken, NG)
                link(nc.vector.tensor_scalar(a_row[:], a_row[:], b_all[:], 0.8, ALU.add, ALU.mult))
                nc.vector.tensor_scalar(a_row[:], a_row[:], ROW_MAX, None, ALU.min)
                dve.wait_ge(sum_done, 1)
                nc.vector.tensor_copy(t["all_sum"][:], sum_ps)
            else:
                dve.wait_ge(exp_ready, 1)
                link(nc.vector.tensor_scalar(h_sum[:], h_sum[:], 0.0, None, ALU.not_equal))
                link(nc.vector.tensor_tensor(b_exp[:], b_exp[:], h_sum[:], ALU.mult))
                dve.wait_ge(ones_set, 1)
                dve.wait_ge(v_taken, NG)
                with dve.Fori(0, T // 4) as i:
                    for u in range(4):
                        at = bass.ds(i * 4 + u, 1)
                        nc.vector.tensor_scalar(V[:, at, :], V[:, at, :], b_exp[:, at], None, ALU.mult)


def gnn_attend(k, name, kind, t, load_adj):
    nc, x, mask = k.nc, k.x, k.mask
    V, a_row, b_col, b_exp, all_sum = t["V"], t["a_row"], t["b_col"], t["b_exp"], t["all_sum"]
    tanh, elu = kind == "tanh", kind == "elu"
    STEPS = 4
    RING = 4
    with stage(k), ExitStack() as ctx:
        sb = lambda shape, dt=F32: k.work.cut(shape, dt)
        sem = lambda n: nc.alloc_semaphore(f"{name}_m_{n}")
        p = [sb([P, IC]) for u in range(2)]
        e = [sb([P, IC]) for u in range(2)] if not tanh else None
        num = sb([P, NB, VW])
        den, lone, inv, lone_inv = (sb([P, NB]) for _ in range(4))
        low = sb([P, NB, D]) if elu else None
        adj = [sb([P, IC], I32) for u in range(RING)] if load_adj else None
        acc = k.banks.cut([P, NB, 256], align=512)
        e_ready, p_ready, p_used, acc_taken = (sem(n) for n in ("e_ready", "p_ready", "p_used", "acc_taken"))
        chain, low_ready, low_exp, x_added = (sem(n) for n in ("chain", "low_ready", "low_exp", "x_added"))
        adj_in = [sem(f"adj_in{u}") for u in range(RING)]
        mask_ready, act_passed = sem("mask_ready"), sem("act_passed")
        block = ctx.enter_context(nc.Block())

        if load_adj:
            @block.sync
            def _(sp):
                def load(s, jt, ic, u):
                    if is_later(s - (RING - 1)):
                        sp.wait_ge(mask_ready, s - (RING - 1))
                    sp.dma_start(adj[u][:], k.dram["adjT"][bass.ds(jt * P, P), bass.ds(ic * IC, IC)]).then_inc(adj_in[u], 16)

                for u in range(RING):
                    load(u, u, 0, u)
                with sp.Fori(1, T // RING) as i:
                    for u in range(RING):
                        load(i * RING + u, i * RING + u, 0, u)
                with sp.Fori(1, NI) as ic:
                    with sp.Fori(0, T // RING) as i:
                        for u in range(RING):
                            load(ic * T + i * RING + u, i * RING + u, ic, u)

        @block.scalar
        def _(act):
            def exps(ic, i, u):
                s = ic * T + i * STEPS + u
                if is_later(s - 1):
                    wait_apart(act, p_ready, s - 1, act_passed)
                nc.scalar.activation(e[u % 2][:], a_row[:, bass.ds(ic * IC, IC)], ACT.Exp,
                                     bias=b_col[:, bass.ds(i * STEPS + u, 1)]).then_inc(e_ready, 1)

            def take(ic):
                act.wait_ge(p_used, ic * T + T)
                if is_later(ic):
                    act.wait_ge(x_added, ic)
                nc.scalar.activation(num[:], acc[:, :, 0:VW], ACT.Copy).then_inc(acc_taken, 1)

            def low_half(ic):
                if elu:
                    act.wait_ge(low_ready, ic + 1)
                    nc.scalar.activation(low[:], low[:], ACT.Exp).then_inc(low_exp, 1)

            if tanh:
                take(0)
                with act.Fori(1, NI) as ic:
                    take(ic)
            else:
                for u in range(STEPS):
                    exps(0, 0, u)
                with act.Fori(1, T // STEPS) as i:
                    for u in range(STEPS):
                        exps(0, i, u)
                with act.Fori(1, NI) as ic:
                    for u in range(2):
                        exps(ic, 0, u)
                    take(ic - 1)
                    for u in range(2, STEPS):
                        exps(ic, 0, u)
                    for u in range(2):
                        exps(ic, 1, u)
                    low_half(ic - 1)
                    for u in range(2, STEPS):
                        exps(ic, 1, u)
                    with act.Fori(2, T // STEPS) as i:
                        for u in range(STEPS):
                            exps(ic, i, u)
                take(NI - 1)
                low_half(NI - 1)

        @block.vector
        def _(dve):
            def weights(ic, i, u):
                cols = bass.ds(ic * IC, IC)
                if load_adj:
                    for v in (u, u + 1):
                        dve.wait_ge(adj_in[v], (ic * (T // RING) + i) * 16 + 16)
                        nc.vector.tensor_scalar(mask[:, bass.ds(i * STEPS + v, 1), cols], adj[v][:, None, :], 0.0, None,
                                                ALU.is_gt).then_inc(mask_ready, 1)
                for v in (u, u + 1):
                    s, at = ic * T + i * STEPS + v, bass.ds(i * STEPS + v, 1)
                    if load_adj:
                        dve.wait_ge(mask_ready, s + 1)
                    if is_later(s - 1):
                        dve.wait_ge(p_used, s - 1)
                    if tanh:
                        nc.vector.tensor_copy(p[v % 2][:, None, :], mask[:, at, cols]).then_inc(p_ready, 1)
                    else:
                        dve.wait_ge(e_ready, s + 1)
                        nc.vector.scalar_tensor_tensor(out=p[v % 2][:, None, :], in0=e[v % 2][:, None, :],
                                                       scalar=b_exp[:, at], in1=mask[:, at, cols],
                                                       op0=ALU.max, op1=ALU.mult).then_inc(p_ready, 1)

            def link(n, ins):
                ins.then_inc(chain, 1)
                dve.wait_ge(chain, n)

            def finish_denominators(ic, links):
                dve.wait_ge(acc_taken, ic + 1)
                if tanh:
                    link(links + 1, nc.vector.tensor_scalar(den[:], num[:, :, D], 1e-37, None, ALU.max))
                    link(links + 2, nc.vector.reciprocal(inv[:], den[:]))
                else:
                    link(links + 1, nc.vector.tensor_scalar(lone[:], num[:, :, D], 0.0, None, ALU.is_equal))
                    link(links + 2, nc.vector.scalar_tensor_tensor(out=den[:], in0=lone[:], scalar=float(N), in1=num[:, :, D],
                                                                   op0=ALU.mult, op1=ALU.add))
                    for b in range(NB):
                        nc.vector.scalar_tensor_tensor(out=num[:, b, 0:D], in0=all_sum[:], scalar=lone[:, b:b + 1],
                                                       in1=num[:, b, 0:D], op0=ALU.mult, op1=ALU.add)
                    link(links + 3, nc.vector.reciprocal(inv[:], den[:]))

            def finish_quotients(ic, links):
                before = links + (2 if tanh else 3)
                link(before + 1, nc.vector.tensor_tensor(num[:, :, 0:D], num[:, :, 0:D],
                                                         inv[:, :, None].to_broadcast([P, NB, D]), ALU.mult))
                if elu:
                    nc.vector.tensor_scalar(low[:], num[:, :, 0:D], 0.0, None, ALU.min).then_inc(low_ready, 1)
                    link(before + 2, nc.vector.tensor_scalar(num[:, :, 0:D], num[:, :, 0:D], 0.0, -1.0, ALU.max, ALU.add))

            def finish_x(ic, links):
                tiles = bass.ds(ic * NB, NB)
                if elu:
                    dve.wait_ge(low_exp, ic + 1)
                    link(links + 6, nc.vector.tensor_tensor(num[:, :, 0:D], num[:, :, 0:D], low[:], ALU.add))
                nc.vector.tensor_tensor(x[:, tiles, :], x[:, tiles, :], num[:, :, 0:D], ALU.add).then_inc(x_added, 1)
                dve.wait_ge(x_added, ic + 1)
                for b in range(NB):
                    tile_stats(k, bass.ds(ic * NB + b, 1))

            n_links = 3 if tanh else 6 if elu else 4
            for u in range(0, STEPS, 2):
                weights(0, 0, u)
            with dve.Fori(1, T // STEPS) as i:
                for u in range(0, STEPS, 2):
                    weights(0, i, u)
            with dve.Fori(1, NI) as ic:
                last = ic - 1, (ic - 1) * n_links
                weights(ic, 0, 0)
                finish_denominators(*last)
                weights(ic, 0, 2)
                finish_quotients(*last)
                weights(ic, 1, 0)
                finish_x(*last)
                weights(ic, 1, 2)
                with dve.Fori(2, T // STEPS) as i:
                    for u in range(0, STEPS, 2):
                        weights(ic, i, u)
            last = NI - 1, (NI - 1) * n_links
            finish_denominators(*last)
            finish_quotients(*last)
            finish_x(*last)

        @block.tensor
        def _(pe):
            def step(ic, i, u, first=False, last=False):
                s = ic * T + i * 2 + u
                pe.wait_ge(p_ready, s + 1)
                for b in range(NB):
                    ins = nc.tensor.matmul(acc[:, b, 0:VW], p[u][:, b * P:(b + 1) * P], V[:, bass.ds(i * 2 + u, 1), :],
                                           start=first and b % 2 == 0, stop=last, skip_group_check=True)
                ins.then_inc(p_used, 1)
                return ins

            def chunk(ic):
                if is_later(ic):
                    pe.wait_ge(acc_taken, ic)
                step(ic, 0, 0, first=True)
                step(ic, 0, 1)
                with pe.Fori(1, T // 2 - 1) as i:
                    step(ic, i, 0)
                    step(ic, i, 1)
                step(ic, T // 2 - 1, 0)
                step(ic, T // 2 - 1, 1, last=True)

            chunk(0)
            with pe.Fori(1, NI) as ic:
                chunk(ic)




def ffn_spec(s):
    return {
        0: dict(E=8, hidden=[128, 128, 85], kind="gated", router="softmax_norm"),
        1: dict(E=6, hidden=[128], kind="deep", router="softmax_twice"),
        2: dict(E=8, hidden=[128, 128], kind="relu", router="softmax"),
        3: dict(E=8, hidden=[128, 128], kind="gelu", router="mask"),
    }[s]


def ffn_layer(k, s):
    nc, name, spec = k.nc, f"L{s}f", ffn_spec(s)
    with stage(k), ExitStack() as ctx:
        sb = lambda shape, dt=F32: k.work.cut(shape, dt)
        t = {"xT": sb([P, N]), "logits": sb([P, T, spec["E"]]),
             "gates": sb([P, T, spec["E"]])}
        ffn_transpose(k, name, spec, t)
        ffn_route(k, name, spec, t)
        ffn_experts(k, name, spec, t)


def ffn_transpose(k, name, spec, t, src=None):
    nc, x, E = k.nc, k.x if src is None else src, spec["E"]
    deep, gated = spec["kind"] == "deep", spec["kind"] == "gated"
    RH = D // 2
    with stage(k), ExitStack() as ctx:
        sb = lambda shape, dt=F32: k.work.cut(shape, dt)
        sem = lambda n: nc.alloc_semaphore(f"{name}_t_{n}")
        ps = lambda shape: k.banks.cut(shape, align=512)
        r_w = sb([RH if deep else P, E])
        r_b = sb([P, E]) if not gated else None
        ln2 = sb([P, 1]) if gated else None
        r_w1, r_b1 = (sb([P, RH]), sb([RH, 1])) if deep else (None, None)
        r_b2 = sb([P, E]) if spec["router"] == "softmax" else None
        xn = [sb([P, G, D]) for u in range(2)]
        xs = [sb([P, GW]) for u in range(2)]
        rh = [sb([RH, GW]) for u in range(2)] if deep else None
        xT_ps = [ps([P, GW]) for u in range(2)]
        rh_ps = [ps([RH, GW]) for u in range(2)] if deep else None
        lg_ps = ps([P, 512])
        weights_in, xn_ready, tr_done, xs_ready, xT_ready = (
            sem(n) for n in ("weights_in", "xn_ready", "tr_done", "xs_ready", "xT_ready"))
        ln = LayerNorm(k, name) if not gated else None
        rh_done, rh_ready, lg_done, bias_ready = (sem(n) for n in ("rh_done", "rh_ready", "lg_done", "bias_ready"))
        block = ctx.enter_context(nc.Block())
        dr = k.dram
        loads = [(r_w[:], dr[f"{name}_r_w"])]
        loads += [(ln2[:], dr[f"{name}_ln2"])] if gated else [(r_b[:], dr[f"{name}_r_b"].partition_broadcast(P))]
        if deep:
            loads += [(r_w1[:], dr[f"{name}_r_w1"]), (r_b1[:], dr[f"{name}_r_b1"])]
        if r_b2 is not None:
            loads += [(r_b2[:], dr[f"{name}_r_b2"].partition_broadcast(P))]

        @block.sync
        def _(sp):
            for out, src in loads:
                sp.dma_start(out, src).then_inc(weights_in, 16)

        @block.vector
        def _(dve):
            def normalise(g, u):
                if is_later(g - 1):
                    dve.wait_ge(tr_done, g - 1)
                for j in range(G):
                    at = bass.ds(g * G + j, 1)
                    last = nc.vector.tensor_scalar(xn[u][:, j:j + 1, :], x[:, at, :], k.rstd[:, at], k.shift[:, at],
                                                   ALU.mult, ALU.add)
                last.then_inc(xn_ready, 1)

            def keep(g, u):
                dve.wait_ge(xs_ready, g + 1)
                nc.vector.tensor_copy(t["xT"][:, bass.ds(g * GW, GW)], xs[u][:]).then_inc(xT_ready, 1)

            if ln is not None:
                ln.vector_part(dve)
            for u in range(2):
                normalise(u, u)
            with dve.Fori(0, NG // 2 - 1) as i:
                for u in range(2):
                    normalise(i * 2 + (2 + u), u)
                for u in range(2):
                    keep(i * 2 + u, u)
            for u in range(2):
                keep(NG - 2 + u, u)
            dve.wait_ge(lg_done, NG)
            dve.wait_ge(weights_in, 16 * len(loads))
            if r_b2 is not None:
                nc.vector.tensor_tensor(r_b[:], r_b[:], r_b2[:], ALU.add).then_inc(bias_ready, 1)
                dve.wait_ge(bias_ready, 1)
            all_logits = lg_ps[:, 0:T * E].rearrange("p (t e) -> p t e", e=E)
            if gated:
                nc.vector.tensor_copy(t["logits"][:], all_logits)
            else:
                nc.vector.tensor_tensor(t["logits"][:], all_logits, r_b[:, None, :].to_broadcast([P, T, E]), ALU.add)

        @block.scalar
        def _(act):
            def copy_T(g, u):
                act.wait_ge(tr_done, g + 1)
                if is_later(g - 1):
                    act.wait_ge(rh_done if deep else lg_done, g - 1)
                    act.wait_ge(xT_ready, g - 1)
                nc.scalar.activation(xs[u][:], xT_ps[u][:], ACT.Copy, scale=ln2[:] if gated else 1.0).then_inc(xs_ready, 1)

            def relu(g, u):
                act.wait_ge(rh_done, g + 1)
                if is_later(g - 1):
                    act.wait_ge(lg_done, g - 1)
                nc.scalar.activation(rh[u][:], rh_ps[u][:], ACT.Relu, bias=r_b1[:]).then_inc(rh_ready, 1)

            if ln is not None:
                ln.scalar_part(act)
            act.wait_ge(weights_in, 16 * len(loads))
            for u in range(2):
                copy_T(u, u)
            for u in range(2):
                copy_T(2 + u, u)
            if deep:
                for u in range(2):
                    relu(u, u)
            with act.Fori(1, NG // 2 - 1) as i:
                for u in range(2):
                    copy_T(i * 2 + (2 + u), u)
                if deep:
                    for u in range(2):
                        relu(i * 2 + u, u)
            if deep:
                for u in range(2):
                    relu(NG - 2 + u, u)

        @block.tensor
        def _(pe):
            def transposes(g, u):
                pe.wait_ge(xn_ready, g + 1)
                if is_later(g - 1):
                    pe.wait_ge(xs_ready, g - 1)
                for j in range(G):
                    last = nc.tensor.transpose(xT_ps[u][:, j * P:(j + 1) * P], xn[u][:, j, :], k.ident[:])
                last.then_inc(tr_done, 1)

            def hidden(g, u):
                if deep:
                    pe.wait_ge(xs_ready, g + 1)
                    if is_later(g - 1):
                        pe.wait_ge(rh_ready, g - 1)
                    nc.tensor.matmul(rh_ps[u][:], r_w1[:], xs[u][:], start=True, stop=True).then_inc(rh_done, 1)

            def logits(g, u):
                if deep:
                    pe.wait_ge(rh_ready, g + 1)
                else:
                    pe.wait_ge(xs_ready, g + 1)
                src = rh[u] if deep else xs[u]
                for j in range(G):
                    last = nc.tensor.matmul(lg_ps[:, bass.ds((g * G + j) * E, E)], src[:, j * P:(j + 1) * P], r_w[:],
                                            start=True, stop=True)
                last.then_inc(lg_done, 1)

            def route(i):
                for u in range(2):
                    hidden(i * 2 + u, u)
                for u in range(2):
                    logits(i * 2 + u, u)

            pe.wait_ge(weights_in, 16 * len(loads))
            for u in range(2):
                transposes(u, u)
            for u in range(2):
                transposes(2 + u, u)
            route(0)
            with pe.Fori(1, NG // 2 - 1) as i:
                for u in range(2):
                    transposes(i * 2 + (2 + u), u)
                route(i)
            route(NG // 2 - 1)


def ffn_route(k, name, spec, t):
    nc, E, router = k.nc, spec["E"], spec["router"]
    logits, gates = t["logits"], t["gates"]
    with stage(k), ExitStack() as ctx:
        sb = lambda shape, dt=F32: k.work.cut(shape, dt)
        sem = lambda n: nc.alloc_semaphore(f"{name}_r_{n}")
        first = sb([P, E])
        sel = [sb([P, T, E]) for n in range(2)]
        rank, score = sb([P, T, E]), sb([P, T, E])
        top = [sb([P, T]) for n in range(2)]
        top_rank, one, two = sb([P, T]), sb([P, T]), sb([P, T])
        total = sb([P, T])
        chain, to_exp, exp_done = sem("chain"), sem("to_exp"), sem("exp_done")
        block = ctx.enter_context(nc.Block())
        wide = lambda a: a[:, :, None].to_broadcast([P, T, E])
        softmax = router in ("softmax_norm", "softmax_twice")

        @block.scalar
        def _(act):
            if softmax:
                act.wait_ge(to_exp, 1)
                nc.scalar.activation(score[:], score[:], ACT.Exp).then_inc(exp_done, 1)
            if router in ("softmax", "softmax_twice"):
                act.wait_ge(to_exp, 2 if softmax else 1)
                nc.scalar.activation(two[:], two[:], ACT.Exp).then_inc(exp_done, 1)

        @block.vector
        def _(dve):
            links = [0]

            def link(ins):
                links[0] += 1
                ins.then_inc(chain, 1)
                dve.wait_ge(chain, links[0])

            def tt(out, a, b, op):
                link(nc.vector.tensor_tensor(out, a, b, op))

            def reduce(out, a, op):
                link(nc.vector.tensor_reduce(out, a, AX.X, op))

            for e in range(E):
                nc.vector.memset(first[:, e:e + 1], float(E - e))
            if softmax:
                reduce(top[0][:], logits[:], ALU.max)
                nc.vector.tensor_tensor(score[:], logits[:], wide(top[0]), ALU.subtract).then_inc(to_exp, 1)
                dve.wait_ge(exp_done, 1)
                reduce(total[:], score[:], ALU.add)
                link(nc.vector.reciprocal(total[:], total[:]))
                tt(score[:], score[:], wide(total), ALU.mult)
            else:
                link(nc.vector.tensor_copy(score[:], logits[:]))
            for n in range(2):
                reduce(top[n][:], score[:], ALU.max)
                tt(rank[:], score[:], wide(top[n]), ALU.is_equal)
                tt(rank[:], rank[:], first[:, None, :].to_broadcast([P, T, E]), ALU.mult)
                reduce(top_rank[:], rank[:], ALU.max)
                tt(sel[n][:], rank[:], wide(top_rank), ALU.is_equal)
                if n == 0:
                    link(nc.vector.scalar_tensor_tensor(out=score[:], in0=sel[0][:], scalar=-1e30, in1=score[:],
                                                        op0=ALU.mult, op1=ALU.add))
            if router in ("mask", "softmax_norm"):
                tt(gates[:], sel[0][:], sel[1][:], ALU.add)
            if router == "softmax_norm":
                tt(one[:], top[0][:], top[1][:], ALU.add)
                link(nc.vector.tensor_scalar(one[:], one[:], 1e-9, None, ALU.add))
                link(nc.vector.reciprocal(one[:], one[:]))
                tt(two[:], top[1][:], one[:], ALU.mult)
                tt(one[:], top[0][:], one[:], ALU.mult)
            elif router != "mask":
                nc.vector.tensor_tensor(two[:], top[1][:], top[0][:], ALU.subtract).then_inc(to_exp, 1)
                dve.wait_ge(exp_done, 2 if softmax else 1)
                link(nc.vector.tensor_scalar(one[:], two[:], 1.0, None, ALU.add))
                link(nc.vector.reciprocal(one[:], one[:]))
                tt(two[:], two[:], one[:], ALU.mult)
            if router != "mask":
                tt(sel[0][:], sel[0][:], wide(one), ALU.mult)
                tt(sel[1][:], sel[1][:], wide(two), ALU.mult)
                tt(gates[:], sel[0][:], sel[1][:], ALU.add)


def ffn_experts(k, name, spec, t):
    nc, x, E, kind, hidden = k.nc, k.x, spec["E"], spec["kind"], spec["hidden"]
    xT, gates = t["xT"], t["gates"]
    M = len(hidden)
    H = sum(hidden)
    units = [(e, m) for e in range(E) for m in range(M)]
    U = len(units)
    gated, deep = kind == "gated", kind == "deep"
    HS = 3 if gated else 2
    bias = not gated
    with stage(k), ExitStack() as ctx:
        sb = lambda shape, dt=F32: k.work.cut(shape, dt)
        sem = lambda n: nc.alloc_semaphore(f"{name}_e_{n}")
        ps = lambda shape: k.banks.cut(shape, align=512)
        w_in = sb([P, E, H])
        w_up = sb([P, E, H]) if gated else None
        w_mid = sb([P, E, D]) if deep else None
        w_out = sb([P, E, M, D])
        b_in = sb([P, E, M]) if bias else None
        b_mid = sb([P, E]) if deep else None
        b_out = sb([P, E, D]) if bias else None
        act_out = [sb([P, GW]) for u in range(2)] if gated or deep else None
        hid = [sb([P, GW]) for u in range(HS)]
        in_ps = [ps([P, GW]) for u in range(HS)]
        up_ps = [ps([P, GW]) for u in range(HS)] if gated else None
        mid_ps = [ps([P, GW]) for u in range(2)] if deep else None
        y_ps = [ps([P, G, D]) for u in range(2)]
        weights_in = sem("weights_in")
        in_done, in_taken, mid_done = sem("in_done"), sem("in_taken"), sem("mid_done")
        hid_ready, out_done, y_taken, x_chain = sem("hid_ready"), sem("out_done"), sem("y_taken"), sem("x_chain")
        block = ctx.enter_context(nc.Block())
        dr = k.dram
        loads = [(w_in[:], dr[f"{name}_w_in"]), (w_out[:], dr[f"{name}_w_out"])]
        if gated:
            loads += [(w_up[:], dr[f"{name}_w_up"])]
        if deep:
            loads += [(w_mid[:], dr[f"{name}_w_mid"]), (b_mid[:], dr[f"{name}_b_mid"])]
        if bias:
            loads += [(b_in[:], dr[f"{name}_b_in"]), (b_out[:], dr[f"{name}_b_out"].partition_broadcast(P))]

        @block.sync
        def _(sp):
            for out, src in loads:
                sp.dma_start(out, src).then_inc(weights_in, 16)

        @block.tensor
        def _(pe):
            def first_product(c, n):
                e, m = units[n]
                lo, w = sum(hidden[:m]), hidden[m]
                at = c * U + n
                u = n % HS
                if deep:
                    pe.wait_ge(in_taken, at + 1)
                else:
                    pe.wait_ge(hid_ready, at + 1)
                cols = xT[:, bass.ds(c * GW, GW)]
                ins = nc.tensor.matmul(in_ps[u][0:w, :], w_in[:, e, lo:lo + w], cols, start=True, stop=True)
                if gated:
                    ins = nc.tensor.matmul(up_ps[u][0:w, :], w_up[:, e, lo:lo + w], cols, start=True, stop=True)
                ins.then_inc(in_done, 1)

            def mid_product(c, n):
                e, at, u = units[n][0], c * U + n, n % 2
                pe.wait_ge(in_taken, at + 3)
                pe.wait_ge(hid_ready, at + 1)
                nc.tensor.matmul(mid_ps[u][:], w_mid[:, e, :], act_out[u][:], start=True, stop=True).then_inc(mid_done, 1)

            def out_product(c, n):
                e, m = units[n]
                w, at, u = hidden[m], c * U + n, n % HS
                pe.wait_ge(hid_ready, at + HS + 1)
                if m == 0:
                    pe.wait_ge(y_taken, c * E + e + 1)
                for b in range(G):
                    ins = nc.tensor.matmul(y_ps[e % 2][:, b, :], hid[u][0:w, b * P:(b + 1) * P], w_out[0:w, e, m, :],
                                           start=m == 0 and b == 0, stop=m == M - 1, skip_group_check=True)
                ins.then_inc(out_done, 1)

            def unit(c, n, last=False):
                ahead = 2 if deep or gated else 1
                for step, product in ((ahead, first_product),) + (((1, mid_product),) if deep else ()):
                    if n + step < U:
                        product(c, n + step)
                    elif not last:
                        product(c + 1, n + step - U)
                out_product(c, n)

            pe.sem_inc(out_done, HS)
            pe.wait_ge(weights_in, 16 * len(loads))
            first_product(0, 0)
            if deep or gated:
                first_product(0, 1)
            if deep:
                mid_product(0, 0)
            with pe.Fori(0, NG - 1) as c:
                for n in range(U):
                    unit(c, n)
            for n in range(U):
                unit(NG - 1, n, last=True)

        @block.scalar
        def _(act):
            def unit(c, n):
                e, m = units[n]
                w, at, u = hidden[m], c * U + n, n % HS
                act.wait_ge(in_done, at + 1)
                if gated:
                    act.wait_ge(hid_ready, at + HS - 1)
                    nc.scalar.activation(act_out[n % 2][0:w, :], in_ps[u][0:w, :], ACT.Silu).then_inc(in_taken, 1)
                elif deep:
                    act.wait_ge(mid_done, at + 1)
                    nc.scalar.activation(act_out[u][:], in_ps[u][:], ACT.Relu, bias=b_in[:, e, m:m + 1]).then_inc(in_taken, 1)
                else:
                    act.wait_ge(out_done, at + 1)
                    nc.scalar.activation(hid[u][0:w, :], in_ps[u][0:w, :], ACT.Gelu if kind == "gelu" else ACT.Relu,
                                         bias=b_in[:, e, m:m + 1]).then_inc(hid_ready, 1)

            def mid_unit(c, n):
                e, at, u = units[n][0], c * U + n, n % HS
                act.wait_ge(mid_done, at + 3)
                act.wait_ge(out_done, at + 1)
                nc.scalar.activation(hid[u][:], mid_ps[u][:], ACT.Relu, bias=b_mid[:, e:e + 1]).then_inc(hid_ready, 1)

            if not gated:
                act.sem_inc(hid_ready, HS)
            if deep:
                act.sem_inc(in_taken, 2)
            act.wait_ge(weights_in, 16 * len(loads))
            if deep:
                unit(0, 0)
                with act.Fori(0, NG - 1) as c:
                    for n in range(U):
                        unit(c, n + 1) if n + 1 < U else unit(c + 1, 0)
                        mid_unit(c, n)
                for n in range(U):
                    if n + 1 < U:
                        unit(NG - 1, n + 1)
                    mid_unit(NG - 1, n)
            else:
                with act.Fori(0, NG) as c:
                    for n in range(U):
                        unit(c, n)

        @block.vector
        def _(dve):
            def product(c, n):
                e, m = units[n]
                w, at, u = hidden[m], c * U + n, n % HS
                dve.wait_ge(in_taken, at + 1)
                dve.wait_ge(out_done, at + 1)
                nc.vector.tensor_tensor(hid[u][0:w, :], act_out[n % 2][0:w, :], up_ps[u][0:w, :], ALU.mult).then_inc(hid_ready, 1)

            n_chain = 2 if bias else 1

            def add(c, e):
                done = (c * E + e) * n_chain
                dve.wait_ge(out_done, (c * E + e) * M + M + HS)
                for b in range(G):
                    at = bass.ds(c * G + b, 1)
                    ins = nc.vector.scalar_tensor_tensor(out=x[:, at, :], in0=y_ps[e % 2][:, b:b + 1, :], scalar=gates[:, at, e:e + 1],
                                                         in1=x[:, at, :], op0=ALU.mult, op1=ALU.add)
                ins.then_inc(y_taken, 1)
                dve.wait_ge(y_taken, c * E + e + 3)
                if bias:
                    for b in range(G):
                        at = bass.ds(c * G + b, 1)
                        ins = nc.vector.scalar_tensor_tensor(out=x[:, at, :], in0=b_out[:, e:e + 1, :], scalar=gates[:, at, e:e + 1],
                                                             in1=x[:, at, :], op0=ALU.mult, op1=ALU.add)
                    ins.then_inc(x_chain, 1)
                    dve.wait_ge(x_chain, c * E + e + 1)

            dve.sem_inc(y_taken, 2)
            if gated:
                dve.sem_inc(hid_ready, HS)
            if deep:
                dve.sem_inc(mid_done, 2)
            dve.wait_ge(weights_in, 16 * len(loads))
            with dve.Fori(0, NG) as c:
                for n, (e, m) in enumerate(units):
                    if gated:
                        product(c, n)
                        if m == 0 and e > 0:
                            add(c, e - 1)
                    else:
                        if m == M - 1:
                            add(c, e)
                if gated:
                    add(c, E - 1)
                for b in range(G):
                    tile_stats(k, bass.ds(c * G + b, 1))




def ffn0_layer(k):
    nc, name, spec = k.nc, "L0f", ffn_spec(0)
    with stage(k), ExitStack() as ctx:
        sb = lambda shape, dt=F32: k.work.cut(shape, dt)
        dram_r = nc.dram_tensor("r_scratch", (N, D), F32, kind="Internal").ap()
        causal_attention(k, dram_r)
        t = {"xT": sb([P, N]), "logits": sb([P, T, spec["E"]]),
             "gates": sb([P, T, spec["E"]])}
        with stage(k):
            r = sb([P, T, D])
            rms_norm_scale(k, r, dram_r)
            ffn_transpose(k, name, spec, t, src=r)
        ffn_route(k, name, spec, t)
        ffn_experts(k, name, spec, t)


def rms_norm_scale(k, r, dram_r):
    nc = k.nc
    with stage(k), ExitStack() as ctx:
        sem = lambda n: nc.alloc_semaphore(f"rms_{n}")
        square = [k.work.cut([P, G, D]) for u in range(2)]
        r_in = [sem(f"r_in{g}") for g in range(NG)]
        squared, reduced, sum_ready, root_ready = sem("squared"), sem("reduced"), sem("sum_ready"), sem("root_ready")
        block = ctx.enter_context(nc.Block())

        @block.sync
        def _(sp):
            for g in range(NG):
                sp.dma_start(r[:, g * G:(g + 1) * G, :],
                             dram_r[g * GW:(g + 1) * GW, :].rearrange("(t p) d -> p t d", p=P)).then_inc(r_in[g], 16)

        @block.scalar
        def _(act):
            for g in range(NG):
                act.wait_ge(r_in[g], 16)
                if g >= 2:
                    act.wait_ge(reduced, g - 1)
                nc.scalar.activation(square[g % 2][:], r[:, g * G:(g + 1) * G, :], ACT.Square).then_inc(squared, 1)
            act.wait_ge(sum_ready, 1)
            nc.scalar.activation(k.rstd[:], k.rstd[:], ACT.Sqrt).then_inc(root_ready, 1)

        @block.vector
        def _(dve):
            nc.vector.memset(k.shift[:], 0.0)
            for g in range(NG):
                dve.wait_ge(squared, g + 1)
                nc.vector.tensor_reduce(k.rstd[:, g * G:(g + 1) * G], square[g % 2][:], AX.X, ALU.add).then_inc(reduced, 1)
            dve.wait_ge(reduced, NG)
            nc.vector.tensor_scalar(k.rstd[:], k.rstd[:], 1.0 / D, 1e-6, ALU.mult, ALU.add).then_inc(sum_ready, 1)
            dve.wait_ge(root_ready, 1)
            nc.vector.reciprocal(k.rstd[:], k.rstd[:])


NH, NKV, HD = 4, 2, 32
HV = HD + 1
PARTS = 3


def causal_attention(k, dram_r):
    with stage(k):
        kept = {"ka": k.work.cut([P, NKV, N], BF16), "kb": k.work.cut([2 * HD + 1, NKV, N], BF16),
                "v": k.work.cut([P, T, NKV, HV])}
        q_parts = k.nc.dram_tensor("q_parts", (PARTS, P, N), BF16, kind="Internal").ap()
        k_parts = k.nc.dram_tensor("k_parts", (PARTS, NKV * HD, N), BF16, kind="Internal").ap()
        attention_project(k, kept, q_parts, k_parts)
        attention_attend(k, kept, q_parts, dram_r)


def attention_project(k, kept, q_parts, k_parts):
    nc, x, d, ka, kb, v = k.nc, k.x, k.dram, kept["ka"], kept["kb"], kept["v"]
    scale = 1.0 / float(np.sqrt(np.float32(HD)))
    with stage(k), ExitStack() as ctx:
        sb = lambda shape, dt=F32: k.work.cut(shape, dt)
        sem = lambda n: nc.alloc_semaphore(f"ap_{n}")
        ps = lambda shape: k.banks.cut(shape, align=512)
        KW = NKV * HD
        w_q, w_qr = sb([P, D]), sb([P, D])
        w_k, w_kr, w_v = sb([P, KW]), sb([P, KW]), sb([P, KW])
        ln1 = sb([P, 1])
        rms, h_scale, h_shift = sb([P, T]), sb([P, T]), sb([P, T])
        cos, sin = [sb([P, GW]) for u in range(2)], [sb([P, GW]) for u in range(2)]
        xn = sb([P, G, D])
        xs = [sb([P, GW]) for u in range(2)]
        full = [sb([P, GW]), sb([KW, GW])]
        rest = [sb([P, GW]), sb([KW, GW])]
        parts = [sb([P, PARTS, GW], BF16), sb([KW, PARTS, GW], BF16)]
        xT_ps = [ps([P, GW]) for u in range(2)]
        ln = LayerNorm(k, "ap")
        f_ps = [ps([P, 2, GW]), ps([P, 2, GW])]
        v_ps = [ps([P, GW]) for u in range(2)]

        weights_in = sem("weights_in")
        tables_in = [sem(f"tables_in{u}") for u in range(2)]
        scaled, rms_ready, ones_set, chain = sem("scaled"), sem("rms_ready"), sem("ones_set"), sem("chain")
        xn_ready, tr_done, xs_ready = sem("xn_ready"), sem("tr_done"), sem("xs_ready")
        f_done, v_done, v_taken = sem("f_done"), sem("v_done"), sem("v_taken")
        rotated, high_ready, rest_ready, mid_ready, parts_ready = (
            sem(n) for n in ("rotated", "high_ready", "rest_ready", "mid_ready", "parts_ready"))
        parts_out, parts_in = [sem("q_out"), sem("k_out")], sem("parts_in")
        block = ctx.enter_context(nc.Block())
        loads = [(w_q[:], d["at_w_q"]), (w_qr[:], d["at_w_qr"]), (w_k[:], d["at_w_k"]), (w_kr[:], d["at_w_kr"]),
                 (w_v[:], d["at_w_v"]), (ln1[:], d["at_ln1"])]

        def tables(sp, c):
            cols = slice(c * GW, (c + 1) * GW)
            if c >= 2:
                sp.wait_ge(rotated, 4 * (c - 1))
            sp.dma_start(cos[c % 2][:], d["at_cos"][:, cols]).then_inc(tables_in[c % 2], 16)
            sp.dma_start(sin[c % 2][:], d["at_sin"][:, cols]).then_inc(tables_in[c % 2], 16)

        @block.sync
        def _(sp):
            for out, src in loads:
                sp.dma_start(out, src).then_inc(weights_in, 16)
            tables(sp, 0)
            tables(sp, 1)
            for c in range(NG):
                cols = slice(c * GW, (c + 1) * GW)
                sp.wait_ge(parts_ready, 2 * c + 1)
                sp.dma_start(q_parts[:, :, cols].rearrange("n p t -> p n t"), parts[0][:]).then_inc(parts_out[0], 16)
                sp.wait_ge(parts_ready, 2 * c + 2)
                sp.dma_start(k_parts[:, :, cols].rearrange("n p t -> p n t"), parts[1][:]).then_inc(parts_out[1], 16)
                if c + 2 < NG:
                    tables(sp, c + 2)
                if c % 2:
                    cols = slice((c - 1) * GW, (c + 1) * GW)
                    sp.wait_ge(parts_out[1], 16 * c + 16)
                    for row, part in enumerate((0, 1, 2, 0)):
                        sp.dma_start(ka[row * HD:(row + 1) * HD, :, cols],
                                     k_parts[part][:, cols].rearrange("(h r) t -> r h t", r=HD)).then_inc(parts_in, 16)
                    for row, part in enumerate((0, 1)):
                        sp.dma_start(kb[row * HD:(row + 1) * HD, :, cols],
                                     k_parts[part][:, cols].rearrange("(h r) t -> r h t", r=HD)).then_inc(parts_in, 16)
            sp.wait_ge(parts_in, 16 * 6 * NG // 2)
            sp.wait_ge(parts_out[0], 16 * NG)

        @block.gpsimd
        def _(pool):
            nc.gpsimd.memset(v[:, :, :, HD:HV], 1.0)

        @block.tensor
        def _(pe):
            pe.wait_ge(weights_in, 16 * len(loads))
            for c in range(NG + 1):
                if c < NG:
                    pe.wait_ge(xn_ready, c + 1)
                    if c >= 2:
                        pe.wait_ge(xs_ready, c - 1)
                    for j in range(G):
                        ins = nc.tensor.transpose(xT_ps[c % 2][:, j * P:(j + 1) * P], xn[:, j, :], k.ident[:])
                    ins.then_inc(tr_done, 1)
                if c:
                    last, xT = c - 1, xs[(c - 1) % 2]
                    pe.wait_ge(xs_ready, c)
                    for n, (w, width) in enumerate((((w_q, w_qr), P), ((w_k, w_kr), KW))):
                        if last:
                            pe.wait_ge(rotated, 4 * last - 4 + 2 * n + 1)
                        nc.tensor.matmul(f_ps[n][0:width, 0, :], w[0][:], xT[:], start=True, stop=True)
                        nc.tensor.matmul(f_ps[n][0:width, 1, :], w[1][:], xT[:], start=True, stop=True).then_inc(f_done, 1)
                    if last >= 2:
                        pe.wait_ge(v_taken, last - 1)
                    for j in range(G):
                        ins = nc.tensor.matmul(v_ps[last % 2][:, j * KW:(j + 1) * KW], xT[:, j * P:(j + 1) * P], w_v[:],
                                               start=True, stop=True)
                    ins.then_inc(v_done, 1)

        @block.scalar
        def _(act):
            ln.scalar_part(act)
            act.wait_ge(scaled, 1)
            nc.scalar.activation(rms[:], rms[:], ACT.Sqrt).then_inc(rms_ready, 1)
            act.wait_ge(weights_in, 16 * len(loads))
            for c in range(NG + 1):
                if c < NG:
                    act.wait_ge(tr_done, c + 1)
                    if c >= 2:
                        act.wait_ge(v_done, c - 1)
                    nc.scalar.activation(xs[c % 2][:], xT_ps[c % 2][:], ACT.Copy, scale=ln1[:]).then_inc(xs_ready, 1)
                if c:
                    last = c - 1
                    for n in range(2):
                        act.wait_ge(rotated, 4 * last + 2 * n + 2)
                        if last:
                            act.wait_ge(parts_out[n], 16 * last)
                        nc.scalar.activation(parts[n][:, 0, :], full[n][:], ACT.Copy).then_inc(high_ready, 1)
                    for n in range(2):
                        act.wait_ge(rest_ready, 2 * last + n + 1)
                        nc.scalar.activation(parts[n][:, 1, :], rest[n][:], ACT.Copy).then_inc(mid_ready, 1)

        @block.vector
        def _(dve):
            links = [0]

            def link(ins):
                links[0] += 1
                ins.then_inc(chain, 1)
                dve.wait_ge(chain, links[0])

            nc.vector.memset(kb[2 * HD:2 * HD + 1, :, :], 1.0)
            ln.vector_part(dve)
            link(nc.vector.tensor_tensor(rms[:], k.rstd[:], k.rstd[:], ALU.mult))
            link(nc.vector.tensor_tensor(rms[:], rms[:], k.var[:], ALU.mult))
            nc.vector.tensor_scalar(rms[:], rms[:], 1e-6, None, ALU.add).then_inc(scaled, 1)
            dve.wait_ge(rms_ready, 1)
            link(nc.vector.reciprocal(rms[:], rms[:]))
            nc.vector.tensor_tensor(h_scale[:], k.rstd[:], rms[:], ALU.mult)
            link(nc.vector.tensor_tensor(h_shift[:], k.shift[:], rms[:], ALU.mult))
            for c in range(NG + 1):
                if c < NG:
                    if c:
                        dve.wait_ge(tr_done, c)
                    for j in range(G):
                        at = c * G + j
                        ins = nc.vector.tensor_scalar(xn[:, j, :], x[:, at, :], h_scale[:, at:at + 1], h_shift[:, at:at + 1],
                                                      ALU.mult, ALU.add)
                    ins.then_inc(xn_ready, 1)
                if c:
                    last = c - 1
                    dve.wait_ge(tables_in[last % 2], 32 * (last // 2 + 1))
                    if last:
                        dve.wait_ge(parts_ready, 2 * last)
                    for n, (w, mul) in enumerate(((P, scale), (KW, 1.0))):
                        dve.wait_ge(f_done, 2 * last + n + 1)
                        nc.vector.scalar_tensor_tensor(out=full[n][:], in0=f_ps[n][0:w, 0, :], scalar=mul,
                                                       in1=cos[last % 2][0:w, :], op0=ALU.mult, op1=ALU.mult)
                        nc.vector.scalar_tensor_tensor(out=rest[n][:], in0=f_ps[n][0:w, 1, :], scalar=mul,
                                                       in1=sin[last % 2][0:w, :], op0=ALU.mult, op1=ALU.mult).then_inc(rotated, 1)
                        dve.wait_ge(rotated, 4 * last + 2 * n + 1)
                        nc.vector.tensor_tensor(full[n][:], full[n][:], rest[n][:], ALU.add).then_inc(rotated, 1)
                    for n in range(2):
                        dve.wait_ge(high_ready, 2 * last + n + 1)
                        dve.wait_ge(rotated, 4 * last + 2 * n + 2)
                        nc.vector.tensor_tensor(rest[n][:], full[n][:], parts[n][:, 0, :], ALU.subtract).then_inc(rest_ready, 1)
                    dve.wait_ge(v_done, last + 1)
                    nc.vector.tensor_copy(v[:, last * G:(last + 1) * G, :, 0:HD],
                                          v_ps[last % 2][:, 0:G * KW].rearrange("p (t h e) -> p t h e", t=G, e=HD)).then_inc(v_taken, 1)
                    for n in range(2):
                        dve.wait_ge(rest_ready, 2 * last + n + 1)
                        dve.wait_ge(mid_ready, 2 * last + n + 1)
                        nc.vector.tensor_tensor(parts[n][:, 2, :], rest[n][:], parts[n][:, 1, :], ALU.subtract).then_inc(parts_ready, 1)


def attention_attend(k, kept, q_parts, dram_r):
    nc, x, d, ka, kb, v = k.nc, k.x, k.dram, kept["ka"], kept["kb"], kept["v"]
    with stage(k), ExitStack() as ctx:
        sb = lambda shape, dt=F32: k.work.cut(shape, dt)
        sem = lambda n: nc.alloc_semaphore(f"at_{n}")
        ps = lambda shape: k.banks.cut(shape, align=512)
        SCANS, UNITS = G * NH, G * NKV
        w_o = sb([P, D])
        constants = sb([P, 4, P], BF16)
        ident16, tri16, triT16, zeros = (constants[:, n, :] for n in range(4))
        qa, qb = [sb([P, NH, GW], BF16) for u in range(2)], [sb([2 * HD + 1, NH, GW], BF16) for u in range(2)]
        tops = sb([P, G, NH, NG])
        top, top_row = sb([P, G * NH]), sb([G * NH, P], BF16)
        p = [sb([P, 2, GW]) for u in range(2)]
        sums = [sb([P, GW]) for kv in range(NKV)]
        inv = sb([P, NKV, 2, G])
        y = sums[0][:].rearrange("p (b h e) -> p b h e", b=G, h=NH)
        v_now = sb([P, G, NKV, HV])
        yT, r = sb([P, GW]), sb([P, G, D])
        tri, triT = r[:, 0, :], r[:, 1, :]
        s_ps = [ps([P, 2, GW]) for u in range(2)]
        acc = ps([P, NKV, GW])
        scan_ps = [ps([P, GW]) for u in range(2)]
        sums_q = [s_ps[kv][:, 1, :].rearrange("p (b h e) -> p h b e", b=G, h=2) for kv in range(NKV)]

        weights_in, q_in = sem("weights_in"), [sem(f"q_in{u}") for u in range(2)]
        constants_ready, tops_set = sem("constants_ready"), sem("tops_set")
        scan_done, scan_taken, top_ready = sem("scan_done"), sem("scan_taken"), sem("top_ready")
        top_done, top_copied, top_in = sem("top_done"), sem("top_copied"), sem("top_in")
        s_done, p_ready, p_used, chain = sem("s_done"), sem("p_ready"), sem("p_used"), sem("chain")
        v_copied, v_passed = sem("v_copied"), sem("v_passed")
        sums_copied, sums_tr_done = sem("sums_copied"), sem("sums_tr_done")
        y_ready, y_tr_done, yT_ready, o_done, o_taken, r_ready, r_out = (
            sem(n) for n in ("y_ready", "y_tr_done", "yT_ready", "o_done", "o_taken", "r_ready", "r_out"))
        block = ctx.enter_context(nc.Block())
        loads = [(w_o[:], d["at_w_o"]), (tri[:], d["at_tri"]), (triT[:], d["at_triT"])]

        def scans_before(c):
            return SCANS * c * (c + 1) // 2

        def units_before(c):
            return UNITS * c * (c + 1) // 2

        @block.sync
        def _(sp):
            def load_q(c):
                cols, u = slice(c * GW, (c + 1) * GW), c % 2
                for row, part in enumerate((0, 0, 0, 1)):
                    sp.dma_start(qa[u][row * HD:(row + 1) * HD, :, :],
                                 q_parts[part][:, cols].rearrange("(h r) t -> r h t", r=HD)).then_inc(q_in[u], 16)
                for row, part in enumerate((2, 1)):
                    sp.dma_start(qb[u][row * HD:(row + 1) * HD, :, :],
                                 q_parts[part][:, cols].rearrange("(h r) t -> r h t", r=HD)).then_inc(q_in[u], 16)

            def store_top(c):
                sp.wait_ge(top_copied, c + 1)
                sp.dma_start(qb[c % 2][2 * HD:2 * HD + 1, :, :], top_row[:]).then_inc(top_in, 16)

            load_q(0)
            for out, src in loads:
                sp.dma_start(out, src).then_inc(weights_in, 16)
            load_q(1)
            store_top(0)
            for c in range(NG):
                if c + 2 < NG:
                    sp.wait_ge(s_done, units_before(c + 1))
                    load_q(c + 2)
                if c + 1 < NG:
                    store_top(c + 1)
                sp.wait_ge(r_ready, c + 1)
                sp.dma_start(dram_r[c * GW:(c + 1) * GW, :].rearrange("(t p) d -> p t d", p=P), r[:]).then_inc(r_out, 16)
            sp.wait_ge(r_out, 16 * NG)

        @block.gpsimd
        def _(pool):
            nc.gpsimd.memset(zeros, 0.0).then_inc(constants_ready, 1)

            def copy_values(c, sc):
                for j in range(G):
                    at = units_before(c) + sc * UNITS + j * NKV
                    if is_later(at - UNITS + NKV):
                        pool.wait_ge(p_used, at - UNITS + NKV)
                    nc.gpsimd.tensor_copy(v_now[:, j, :, :], v[:, bass.ds(sc * G + j, 1), :, :]).then_inc(v_copied, 1)

            for c in range(NG):
                if c:
                    with pool.Fori(0, c) as sc:
                        copy_values(c, sc)
                copy_values(c, c)

        @block.tensor
        def _(pe):
            def scan(c, sc, n, diagonal=False):
                b, head = n // NH, n % NH
                at, width = scans_before(c) + sc * SCANS + n, (b + 1) * P if diagonal else GW
                if is_later(at - 1):
                    pe.wait_ge(scan_taken, at - 1)
                out = scan_ps[n % 2]
                ins = nc.tensor.matmul(out[:, 0:width], qa[c % 2][:, head, b * P:(b + 1) * P],
                                       ka[:, head // 2, bass.ds(sc * GW, width)], start=True, stop=not diagonal)
                if diagonal:
                    ins = nc.tensor.matmul(out[:, b * P:width], ident16, tri16, start=False, stop=True)
                ins.then_inc(scan_done, 1)

            def scores(c, sc, n, diagonal=False):
                j, kv = n // NKV, n % NKV
                at, lo = units_before(c) + sc * UNITS + n, j * P if diagonal else 0
                if is_later(at - 1):
                    pe.wait_ge(p_ready, at - 1)
                for h in range(2):
                    keys, head, out = bass.ds(sc * GW + j * P, P), kv * 2 + h, s_ps[kv][:, h, lo:GW]
                    nc.tensor.matmul(out, ka[:, kv, keys], qa[c % 2][:, head, lo:GW], start=True, stop=False)
                    ins = nc.tensor.matmul(out, kb[:, kv, keys], qb[c % 2][:, head, lo:GW], start=False, stop=not diagonal)
                    if diagonal:
                        ins = nc.tensor.matmul(s_ps[kv][:, h, lo:lo + P], ident16, triT16, start=False, stop=True)
                ins.then_inc(s_done, 1)

            def values(c, sc, n, diagonal=False):
                j, kv = n // NKV, n % NKV
                pe.wait_ge(p_ready, units_before(c) + sc * UNITS + n + 1)
                if kv == 0:
                    wait_apart(pe, v_copied, (units_before(c) + sc * UNITS) // NKV + j + 1, v_passed)
                lo = j * P if diagonal else 0
                for h in range(2):
                    ins = nc.tensor.matmul(acc[64 * h:64 * h + HV, kv, lo:GW], v_now[:, j, kv, :],
                                           p[kv][:, h, lo:GW], start=False, stop=diagonal and j == G - 1,
                                           skip_group_check=True)
                ins.then_inc(p_used, 1)

            def both_passes(c, sc, diagonal=False):
                for n in range(UNITS):
                    scores(c, sc, n, diagonal)
                    if c + 1 < NG:
                        scan(c + 1, sc, 2 * n)
                        scan(c + 1, sc, 2 * n + 1)
                    if n:
                        values(c, sc, n - 1, diagonal)
                values(c, sc, UNITS - 1, diagonal)

            pe.wait_ge(q_in[0], 16 * 6)
            pe.wait_ge(constants_ready, 4)
            for n in range(SCANS):
                scan(0, 0, n, diagonal=True)
            pe.wait_ge(top_ready, 1)
            nc.tensor.transpose(s_ps[0][0:G * NH, 1, 0:P], top[:], k.ident[:]).then_inc(top_done, 1)
            for c in range(NG):
                if c:
                    pe.wait_ge(sums_copied, NKV * c)
                for kv in range(NKV):
                    nc.tensor.matmul(acc[:, kv, :], zeros, constants[:].rearrange("p n t -> p (n t)"), start=True, stop=False,
                                     skip_group_check=True)
                pe.wait_ge(top_in, 16 * (c + 1))
                if c:
                    pe.wait_ge(o_taken, c)
                if c + 1 < NG:
                    pe.wait_ge(q_in[(c + 1) % 2], 16 * 6 * ((c + 1) // 2 + 1))
                if c:
                    with pe.Fori(0, c) as sc:
                        both_passes(c, sc)
                both_passes(c, c, diagonal=True)
                for n in range(SCANS):
                    if n == 2:
                        pe.wait_ge(sums_copied, NKV * (c + 1))
                        for kv in range(NKV):
                            for b in range(G):
                                ins = nc.tensor.transpose(s_ps[kv][:, 1, b * P:(b + 1) * P], sums[kv][:, b * P:(b + 1) * P],
                                                          k.ident[:])
                        ins.then_inc(sums_tr_done, 1)
                    if n == 8:
                        pe.wait_ge(y_ready, c + 1)
                        for b in range(G):
                            ins = nc.tensor.transpose(s_ps[0][:, 0, b * P:(b + 1) * P],
                                                      y[:, b, :, :].rearrange("p h e -> p (h e)"), k.ident[:])
                        ins.then_inc(y_tr_done, 1)
                    if c + 1 < NG:
                        scan(c + 1, c + 1, n, diagonal=True)
                if c + 1 < NG:
                    pe.wait_ge(top_ready, c + 2)
                    nc.tensor.transpose(s_ps[0][0:G * NH, 1, 0:P], top[:], k.ident[:]).then_inc(top_done, 1)
                pe.wait_ge(yT_ready, c + 1)
                for b in range(G):
                    ins = nc.tensor.matmul(s_ps[1][:, 0, b * P:(b + 1) * P], yT[:, b * P:(b + 1) * P], w_o[:],
                                           start=True, stop=True)
                ins.then_inc(o_done, 1)

        @block.scalar
        def _(act):
            def exps(c, sc, n, diagonal=False):
                j, kv = n // NKV, n % NKV
                at, lo = units_before(c) + sc * UNITS + n, j * P if diagonal else 0
                act.wait_ge(s_done, at + 1)
                if is_later(at - 1):
                    act.wait_ge(p_used, at - 1)
                nc.scalar.activation(p[kv][:, :, lo:GW], s_ps[kv][:, :, lo:GW], ACT.Exp).then_inc(p_ready, 1)

            def copy_top(c):
                act.wait_ge(top_done, c + 1)
                if c:
                    act.wait_ge(top_in, 16 * c)
                nc.scalar.activation(top_row[:], s_ps[0][0:G * NH, 1, 0:P], ACT.Copy, scale=-1.0).then_inc(top_copied, 1)

            act.wait_ge(weights_in, 16 * len(loads))
            nc.scalar.activation(ident16, k.ident[:], ACT.Copy).then_inc(constants_ready, 1)
            nc.scalar.activation(tri16, tri[:], ACT.Copy).then_inc(constants_ready, 1)
            nc.scalar.activation(triT16, triT[:], ACT.Copy).then_inc(constants_ready, 1)
            copy_top(0)
            for c in range(NG):
                if c:
                    with act.Fori(0, c) as sc:
                        for n in range(UNITS):
                            exps(c, sc, n)
                for n in range(UNITS):
                    exps(c, c, n, diagonal=True)
                act.wait_ge(p_used, units_before(c + 1))
                for kv in range(NKV):
                    nc.scalar.activation(sums[kv][:], acc[:, kv, :], ACT.Copy).then_inc(sums_copied, 1)
                act.wait_ge(y_tr_done, c + 1)
                nc.scalar.activation(yT[:], s_ps[0][:, 0, :], ACT.Copy).then_inc(yT_ready, 1)
                if c + 1 < NG:
                    copy_top(c + 1)

        @block.vector
        def _(dve):
            links = [0]

            def link(ins):
                links[0] += 1
                ins.then_inc(chain, 1)
                dve.wait_ge(chain, links[0])

            def greatest(c, sc, n, diagonal=False):
                b, head = n // NH, n % NH
                dve.wait_ge(scan_done, scans_before(c) + sc * SCANS + n + 1)
                nc.vector.tensor_reduce(tops[:, b, head, bass.ds(sc, 1)], scan_ps[n % 2][:, 0:(b + 1) * P if diagonal else GW],
                                        AX.X, ALU.max).then_inc(scan_taken, 1)

            def greatest_of_all(c):
                dve.wait_ge(scan_taken, scans_before(c + 1))
                if c:
                    dve.wait_ge(top_done, c)
                nc.vector.tensor_reduce(top[:].rearrange("p (h b) -> p b h", h=NH), tops[:], AX.X, ALU.max).then_inc(top_ready, 1)

            nc.vector.memset(tops[:], -1e30).then_inc(tops_set, 1)
            dve.wait_ge(tops_set, 1)
            for n in range(SCANS):
                greatest(0, 0, n, diagonal=True)
            greatest_of_all(0)
            for c in range(NG):
                if c + 1 < NG:
                    dve.wait_ge(top_ready, c + 1)
                    if c:
                        with dve.Fori(0, c) as sc:
                            for n in range(SCANS):
                                greatest(c + 1, sc, n)
                    for n in range(SCANS):
                        greatest(c + 1, c, n)
                for n in range(SCANS):
                    if n == 2:
                        dve.wait_ge(sums_tr_done, c + 1)
                        for kv in range(NKV):
                            ins = nc.vector.reciprocal(inv[:, kv, :, :], sums_q[kv][:, :, :, HD])
                        link(ins)
                        for kv in range(NKV):
                            for h in range(2):
                                ins = nc.vector.tensor_tensor(y[:, :, kv * 2 + h, :], sums_q[kv][:, h, :, 0:HD],
                                                              inv[:, kv, h, :, None].to_broadcast([P, G, HD]), ALU.mult)
                        ins.then_inc(y_ready, 1)
                    if c + 1 < NG:
                        greatest(c + 1, c + 1, n, diagonal=True)
                if c + 1 < NG:
                    greatest_of_all(c + 1)
                if c:
                    dve.wait_ge(r_out, 16 * c)
                for j in range(G):
                    at = c * G + j
                    ins = nc.vector.tensor_scalar(r[:, j, :], x[:, at, :], k.rstd[:, at:at + 1], k.shift[:, at:at + 1],
                                                  ALU.mult, ALU.add)
                link(ins)
                dve.wait_ge(o_done, c + 1)
                link(nc.vector.tensor_tensor(r[:], r[:], s_ps[1][:, 0, :].rearrange("p (b d) -> p b d", b=G), ALU.add))
                dve.sem_inc(o_taken, 1)
                dve.sem_inc(r_ready, 1)
                xc = x[:, c * G:(c + 1) * G, :]
                nc.vector.tensor_tensor(xc, xc, r[:], ALU.add)




def load_all(k):
    nc, parts = k.nc, 4
    with stage(k), ExitStack() as ctx:
        x_in = [nc.alloc_semaphore(f"x_in{n}") for n in range(parts)]
        ident_in = nc.alloc_semaphore("ident_in")
        block = ctx.enter_context(nc.Block())
        tiles = T // parts

        @block.sync
        def _(sp):
            for n in range(parts):
                at = slice(n * tiles, (n + 1) * tiles)
                sp.dma_start(k.x[:, at, :], k.dram["x"][n * tiles * P:(n + 1) * tiles * P, :].rearrange(
                    "(t p) d -> p t d", p=P)).then_inc(x_in[n], 16)
            sp.dma_start(k.ident[:], k.dram["ident"]).then_inc(ident_in, 16)
            sp.wait_ge(ident_in, 16)

        @block.vector
        def _(dve):
            nc.vector.memset(k.ones[:], 1.0)
            for n in range(parts):
                dve.wait_ge(x_in[n], 16)
                with dve.Fori(0, tiles // 4) as i:
                    for u in range(4):
                        tile_stats(k, bass.ds(i * 4 + (n * tiles + u), 1))


def store_all(k):
    nc = k.nc
    with ExitStack() as ctx:
        x_out = ctx.enter_context(nc.semaphore("x_out"))
        block = ctx.enter_context(nc.Block())

        @block.sync
        def _(sp):
            sp.dma_start(k.out.rearrange("(t p) d -> p t d", p=P), k.x[:]).then_inc(x_out, 16)
            sp.wait_ge(x_out, 16)


def program(nc, dram, out, first=0, last=8):
    with ExitStack() as ctx:
        k = Kernel(nc, dram)
        k.out = out
        sb = lambda n, shape, dt=F32: ctx.enter_context(nc.sbuf_tensor(n, shape, dt))
        k.mask = sb("mask", [P, T, N], U8)
        k.x = sb("x_sb", [P, T, D])
        k.ident, k.ones = sb("ident_sb", [P, P]), sb("ones_sb", [P, P])
        k.rstd, k.shift, k.var = sb("rstd", [P, T]), sb("shift", [P, T]), sb("var", [P, T])
        k.stats = sb("stats", [P, T, 6])
        k.work = Workspace(sb("work", [P, WORK]), WORK)
        k.banks = Workspace(ctx.enter_context(nc.psum_tensor("banks", [P, BANKS * 512], F32)), BANKS * 512)
        load_all(k)
        loaded = False
        for s in range(first, last):
            if s in (0, 2, 4, 6):
                gnn_layer(k, f"L{s // 2}g", {0: "elu", 2: "leaky", 4: "tanh", 6: "leaky"}[s], load_adj=not loaded)
                loaded = True
            elif s == 1:
                ffn0_layer(k)
            else:
                ffn_layer(k, s // 2)
        store_all(k)


def lay_out(w):
    c = np.ascontiguousarray
    a = {"x": w["x"], "adjT": c(w["adj"].T), "ident": np.eye(P, dtype=np.float32)}
    for n, W, vec in ((0, w["L0_gnn_W"], w["L0_gnn_a"]), (1, w["L1_gnn_W_w"], w["L1_gnn_a"]),
                      (3, w["L3_gnn_W"].T, w["L3_gnn_a_vec"])):
        a[f"L{n}g_W"], a[f"L{n}g_WT"] = c(W), c(W.T)
        a[f"L{n}g_a2"] = c(vec.reshape(2, D).T)
    a["L2g_W"], a["L2g_a_row"] = w["L2_gnn_W"], c(w["L2_gnn_a"].reshape(D))
    for n, b in ((1, w["L1_gnn_W_b"]), (2, w["L2_gnn_b"]), (3, w["L3_gnn_b_W"])):
        a[f"L{n}g_b_row"] = b
    for n, b in ((1, w["L1_gnn_W_b"]), (3, w["L3_gnn_b_W"])):
        a[f"L{n}g_b_col"] = c(b.reshape(D, 1))
    a["L3g_ba"] = w["L3_gnn_b_a"]
    def inward(W):
        return c(W.transpose(1, 0, 2))

    def outward(W):
        e, h, d = W.shape
        tiles = -(-h // P)
        return c(np.pad(W, ((0, 0), (0, tiles * P - h), (0, 0))).reshape(e, tiles, P, d).transpose(2, 0, 1, 3))

    def by_hidden(b):
        return c(b.reshape(b.shape[0], -1, P).transpose(2, 0, 1))

    a["L0f_w_in"], a["L0f_w_up"] = (c(w[f"L0_ffn_{n}"].transpose(2, 0, 1)) for n in ("w1", "w3"))
    a["L0f_w_out"] = outward(w["L0_ffn_w2"].transpose(0, 2, 1))
    a["L0f_r_w"], a["L0f_ln2"] = c(w["L0_ffn_router_w"].T), c(w["L0_ffn_ln2_w"].reshape(D, 1))
    halves = np.concatenate([np.arange(HD // 2, HD), np.arange(HD // 2)])

    def rotated(W):
        return c(W.reshape(-1, HD, D)[:, halves].reshape(-1, D).T)

    for n, W in (("q", w["L0_ffn_wq"]), ("k", w["L0_ffn_wk"])):
        a[f"at_w_{n}"], a[f"at_w_{n}r"] = c(W.T), rotated(W)
    a["at_w_v"], a["at_w_o"] = c(w["L0_ffn_wv"].T), c(w["L0_ffn_wo"].T)
    a["at_ln1"] = c(w["L0_ffn_ln1_w"].reshape(D, 1))
    inv_freq = 1.0 / 10000.0 ** (np.arange(0, HD, 2, dtype=np.float32) / HD)
    angle = np.outer(np.arange(N, dtype=np.float32), inv_freq)
    angle = np.concatenate([angle, angle], axis=-1)
    sign = np.where(np.arange(HD) < HD // 2, -1.0, 1.0).astype(np.float32)
    a["at_cos"] = c(np.tile(np.cos(angle).T, (NH, 1)).astype(np.float32))
    a["at_sin"] = c(np.tile((np.sin(angle) * sign).T, (NH, 1)).astype(np.float32))
    a["at_tri"] = np.where(np.arange(P)[None, :] <= np.arange(P)[:, None], 0.0, -1e30).astype(np.float32)
    a["at_triT"] = c(a["at_tri"].T)
    a["L1f_w_in"], a["L1f_w_mid"] = inward(w["L1_ffn_expert_w1"]), inward(w["L1_ffn_expert_w2"])
    a["L1f_w_out"] = outward(w["L1_ffn_expert_w3"])
    a["L1f_b_in"], a["L1f_b_mid"] = by_hidden(w["L1_ffn_expert_b1"]), c(w["L1_ffn_expert_b2"].T)
    a["L1f_b_out"] = w["L1_ffn_expert_b3"]
    a["L1f_r_w"], a["L1f_r_b"] = w["L1_ffn_router_w2"], w["L1_ffn_router_b2"]
    a["L1f_r_w1"], a["L1f_r_b1"] = w["L1_ffn_router_w1"], c(w["L1_ffn_router_b1"].reshape(-1, 1))
    for n in (2, 3):
        a[f"L{n}f_w_in"], a[f"L{n}f_w_out"] = inward(w[f"L{n}_ffn_W1"]), outward(w[f"L{n}_ffn_W2"])
        a[f"L{n}f_b_in"], a[f"L{n}f_b_out"] = by_hidden(w[f"L{n}_ffn_b1"]), w[f"L{n}_ffn_b2"]
        a[f"L{n}f_r_w"], a[f"L{n}f_r_b"] = w[f"L{n}_ffn_Wg"], w[f"L{n}_ffn_bg"]
    a["L2f_r_b2"] = w["L2_ffn_bias"]
    return a


def kernel(**inputs):
    import concourse.bacc as bacc
    from concourse.bass_utils import run_bass_kernel_spmd
    nc = bacc.Bacc("TRN2", target_bir_lowering=False, num_devices=1, dynamic_dma_scratch_size=1024)
    arrays, dram = {}, {}
    for name, a in lay_out({n: np.asarray(v) for n, v in inputs.items()}).items():
        arrays[f"in_{name}_dram"] = a
        dram[name] = nc.dram_tensor(f"in_{name}_dram", a.shape, mybir.dt.from_np(a.dtype), kind="ExternalInput").ap()
    out = nc.dram_tensor("out_0_dram", (N, D), F32, kind="ExternalOutput").ap()
    program(nc, dram, out)
    return run_bass_kernel_spmd(nc, [arrays], core_ids=[0]).results[0]["out_0_dram"]
```

```python
from contextlib import ExitStack, contextmanager

import numpy as np

import concourse.bass as bass
from concourse import mybir

ALU = mybir.AluOpType
ACT = mybir.ActivationFunctionType
AX = mybir.AxisListType
F32 = mybir.dt.float32
BF16 = mybir.dt.bfloat16
U8 = mybir.dt.uint8
I32 = mybir.dt.int32
RMAX = bass.bass_isa.ReduceOp.max

P = 128
N = 4096
D = 128
T = N // P
G = 4
NG = T // G
GW = G * P
IC = 1024
NI = N // IC
NB = IC // P
VW = D + 1
ROW_MAX = 70.0
EPS = 1e-5
PARTS = 3
WORK = 19638
BANKS = 8


class Workspace:

    def __init__(self, tensor, width):
        self.tensor, self.width, self.used = tensor, width, 0

    def cut(self, shape, dt=F32, align=1):
        size = {F32: 4, I32: 4, BF16: 2, U8: 1}[dt]
        n = int(np.prod(shape[1:]))
        columns = -(-n * size // 4)
        start = -(-self.used // align) * align
        assert start + columns <= self.width, (shape, start, self.width)
        self.used = start + columns
        flat = self.tensor[0:shape[0], start:start + columns]
        if dt != F32:
            flat = flat.bitcast(dt)[:, 0:n]
        names = [f"d{i}" for i in range(len(shape) - 1)]
        if len(names) > 1:
            flat = flat.rearrange(f"p ({' '.join(names)}) -> p {' '.join(names)}", **dict(zip(names, shape[1:])))
        return flat


@contextmanager
def stage(k):
    marks = k.work.used, k.banks.used
    yield
    k.work.used, k.banks.used = marks


@contextmanager
def sublayer(k):
    before = k.nc.snapshot_sems()
    with stage(k):
        yield
    k.nc.clear_and_free_semaphores(k.nc.allocated_since(before))
    k.nc.all_engine_barrier()


class Kernel:

    def __init__(self, nc, dram):
        self.nc, self.dram = nc, dram


def is_later(count):
    return not isinstance(count, int) or count > 0


def wait_apart(engine, sem, value, passed):
    engine.wait_ge(sem, value).then_inc(passed, 1)




def tile_stats(k, at):
    return k.nc.vector.bn_stats(k.stats[:, at, :], k.x[:, at, :])


class LayerNorm:

    def __init__(self, k, name):
        self.k = k
        self.mean2, self.diff, self.m2, self.std = (k.work.cut([P, T]) for _ in range(4))
        self.step_done, self.var_ready, self.std_ready = (
            k.nc.alloc_semaphore(f"{name}_ln_{n}") for n in ("step_done", "var_ready", "std_ready"))

    def vector_part(self, dve):
        k, nc, mean2, diff, m2, step_done = self.k, self.k.nc, self.mean2, self.diff, self.m2, self.step_done
        even_mean, even_m2, odd_mean, odd_m2 = (k.stats[:, :, n] for n in (1, 2, 4, 5))
        nc.vector.tensor_tensor(mean2[:], even_mean, odd_mean, ALU.add)
        nc.vector.tensor_tensor(m2[:], even_m2, odd_m2, ALU.add)
        nc.vector.tensor_tensor(diff[:], even_mean, odd_mean, ALU.subtract).then_inc(step_done, 1)
        dve.wait_ge(step_done, 1)
        nc.vector.scalar_tensor_tensor(out=diff[:], in0=diff[:], scalar=0.25, in1=diff[:],
                                       op0=ALU.mult, op1=ALU.mult).then_inc(step_done, 1)
        dve.wait_ge(step_done, 2)
        nc.vector.scalar_tensor_tensor(out=k.var[:], in0=m2[:], scalar=1.0 / D, in1=diff[:],
                                       op0=ALU.mult, op1=ALU.add).then_inc(step_done, 1)
        dve.wait_ge(step_done, 3)
        nc.vector.tensor_scalar(m2[:], k.var[:], EPS, None, ALU.add).then_inc(self.var_ready, 1)
        dve.wait_ge(self.std_ready, 1)
        nc.vector.reciprocal(k.rstd[:], self.std[:]).then_inc(step_done, 1)
        dve.wait_ge(step_done, 4)
        nc.vector.scalar_tensor_tensor(out=k.shift[:], in0=mean2[:], scalar=-0.5, in1=k.rstd[:],
                                       op0=ALU.mult, op1=ALU.mult).then_inc(step_done, 1)
        dve.wait_ge(step_done, 5)

    def scalar_part(self, act):
        act.wait_ge(self.var_ready, 1)
        self.k.nc.scalar.activation(self.std[:], self.m2[:], ACT.Sqrt).then_inc(self.std_ready, 1)




def gnn_layer(k, name, kind, load_adj=False):
    nc, d = k.nc, k.dram
    with sublayer(k), ExitStack() as ctx:
        sb = lambda shape, dt=F32: k.work.cut(shape, dt)
        t = {
            "V": sb([P, T, VW]),
            "a_row": sb([P, N]) if kind != "tanh" else None,
            "b_col": sb([P, T]),
            "b_exp": sb([P, T]),
            "all_sum": sb([P, D]),
            "V_parts": sb([P, T, PARTS, VW], BF16) if kind == "tanh" else None,
        }
        gnn_project(k, name, kind, t)
        gnn_attend(k, name, kind, t, load_adj)


def gnn_project(k, name, kind, t):
    nc, x = k.nc, k.x
    V, a_row, b_col, b_exp = t["V"], t["a_row"], t["b_col"], t["b_exp"]
    tanh = kind == "tanh"
    bias = k.dram.get(f"{name}_b_row")
    with stage(k), ExitStack() as ctx:
        sb = lambda shape, dt=F32: k.work.cut(shape, dt)
        sem = lambda n: nc.alloc_semaphore(f"{name}_{n}")
        ps = lambda shape: k.banks.cut(shape, align=512)
        W_b, WT = sb([P, VW]), sb([P, D])
        W = W_b[:, 0:D]
        a2 = sb([P, 2])
        wa = sb([P, 2])
        wa_wide = sb([P, P])
        b_row, b_wide, bc = sb([P, D]), sb([P, P]), sb([P, 1])
        ba = sb([P, 1])
        aw_row = sb([P, D])
        const2 = sb([P, 2])
        xn = [sb([P, G, D]) for u in range(2)]
        xT = [sb([P, GW]) for u in range(2)]
        h = [sb([P, G, D]) for u in range(2)] if tanh else None
        h_sum = sb([P, T]) if tanh else None
        b_top, b_all = sb([P, 1]), sb([P, 1])
        v_sum, v_part = sb([P, D]), sb([P, NG, D])
        limit = sb([P, 1])
        xT_ps = [ps([P, GW]) for u in range(2)]
        v_ps = [ps([P, G, 256]) for u in range(2)]
        a_ps = [ps([P, GW]) for u in range(2)]
        s_ps = a_ps[1]
        wa_ps, c_ps, sum_ps = s_ps[:, 64:66], s_ps[:, 68:70], s_ps[:, 128:128 + D]

        weights_in, ones_set = sem("weights_in"), sem("ones_set")
        wa_done, wa_ready, const_ready, wide_ready = (sem(n) for n in ("wa_done", "wa_ready", "const_ready", "wide_ready"))
        xn_ready, tr_done, xT_ready = sem("xn_ready"), sem("tr_done"), sem("xT_ready")
        v_done, v_taken, a_taken = sem("v_done"), sem("v_taken"), sem("a_taken")
        h_ready, h_tanh, h_summed, h_scaled, h_taken = (
            sem(n) for n in ("h_ready", "h_tanh", "h_summed", "h_scaled", "h_taken"))
        chain, top_ready, top_all, shifted, exp_ready = (
            sem(n) for n in ("chain", "top_ready", "top_all", "shifted", "exp_ready"))
        b_taken, v_summed = sem("b_taken"), sem("v_summed")
        weight_ready, high_ready, rest_ready, mid_ready = (
            sem(n) for n in ("weight_ready", "high_ready", "rest_ready", "mid_ready"))
        V_parts, SPLITS = t["V_parts"], 4
        vsum_ready, sum_done = sem("vsum_ready"), sem("sum_done")
        block = ctx.enter_context(nc.Block())
        ln = LayerNorm(k, name)
        dr = k.dram
        loads = [(W, dr[f"{name}_W"])]
        if tanh:
            loads += [(aw_row[:], dr[f"{name}_a_row"].partition_broadcast(P))]
        else:
            loads += [(WT[:], dr[f"{name}_WT"]), (a2[:], dr[f"{name}_a2"])]
        if bias is not None:
            loads += [(b_row[:], bias.partition_broadcast(P))]
            if not tanh:
                loads += [(bc[:], dr[f"{name}_b_col"])]
        has_ba = f"{name}_ba" in dr
        if has_ba:
            loads += [(ba[:], dr[f"{name}_ba"].partition_broadcast(P))]

        @block.sync
        def _(sp):
            for out, src in loads:
                sp.dma_start(out, src).then_inc(weights_in, 16)

        @block.gpsimd
        def _(pool):
            nc.gpsimd.memset(V[:, :, D:VW], 1.0).then_inc(ones_set, 1)
            pool.wait_ge(top_ready, 1)
            nc.gpsimd.partition_all_reduce(b_all[:], b_top[:], P, RMAX).then_inc(top_all, 1)

        @block.tensor
        def _(pe):
            def transposes(g, u):
                pe.wait_ge(xn_ready, g + 1)
                if is_later(g - 1):
                    pe.wait_ge(xT_ready, g - 1)
                for j in range(G):
                    last = nc.tensor.transpose(xT_ps[u][:, j * P:(j + 1) * P], xn[u][:, j, :], k.ident[:])
                last.then_inc(tr_done, 1)

            def project(g, u):
                pe.wait_ge(xT_ready, g + 1)
                if is_later(g - 1):
                    pe.wait_ge(v_taken, g - 1)
                    if not tanh:
                        pe.wait_ge(b_taken, g - 1)
                width = D if tanh else VW
                for j in range(G):
                    last = nc.tensor.matmul(v_ps[u][:, j, 0:width], xT[u][:, j * P:(j + 1) * P], W_b[:, 0:width],
                                            start=True, stop=True)
                if not tanh:
                    if is_later(g - 1):
                        pe.wait_ge(a_taken, g - 1)
                    last = nc.tensor.matmul(a_ps[u][:], wa_wide[:], xT[u][:], start=True, stop=True)
                last.then_inc(v_done, 1)

            for u in range(2):
                transposes(u, u)
            pe.wait_ge(weights_in, 16 * len(loads))
            if not tanh:
                nc.tensor.matmul(wa_ps, WT[:], a2[:], start=True, stop=True).then_inc(wa_done, 1)
                if bias is not None:
                    pe.wait_ge(wide_ready, 1)
                    nc.tensor.matmul(c_ps, b_wide[:], a2[:], start=True, stop=True).then_inc(wa_done, 1)
                pe.wait_ge(wa_ready, 1)
                pe.wait_ge(const_ready, 1)
            for u in range(2):
                transposes(2 + u, u)
            for u in range(2):
                project(u, u)
            with pe.Fori(1, NG // 2 - 1) as i:
                for u in range(2):
                    transposes(i * 2 + (2 + u), u)
                for u in range(2):
                    project(i * 2 + u, u)
            for u in range(2):
                project(NG - 2 + u, u)
            if not tanh:
                pe.wait_ge(vsum_ready, 1)
                pe.wait_ge(a_taken, NG)
                nc.tensor.matmul(sum_ps, k.ones[:], v_sum[:], start=True, stop=True).then_inc(sum_done, 1)

        @block.scalar
        def _(act):
            def copy_T(g, u):
                act.wait_ge(tr_done, g + 1)
                if is_later(g - 1):
                    act.wait_ge(v_done, g - 1)
                nc.scalar.activation(xT[u][:], xT_ps[u][:], ACT.Copy).then_inc(xT_ready, 1)

            def take(g, u):
                if tanh:
                    act.wait_ge(h_ready, g + 1)
                    nc.scalar.activation(h[u][:], h[u][:], ACT.Tanh).then_inc(h_tanh, 1)
                else:
                    act.wait_ge(v_done, g + 1)
                    nc.scalar.activation(a_row[:, bass.ds(g * GW, GW)], a_ps[u][:], ACT.Identity,
                                         bias=const2[:, 0:1]).then_inc(a_taken, 1)

            ln.scalar_part(act)
            for u in range(2):
                copy_T(u, u)
            for u in range(2):
                copy_T(2 + u, u)
            if not tanh:
                act.wait_ge(const_ready, 1)
            for u in range(2):
                take(u, u)
            with act.Fori(1, NG // 2 - 1) as i:
                for u in range(2):
                    copy_T(i * 2 + (2 + u), u)
                for u in range(2):
                    take(i * 2 + u, u)
            for u in range(2):
                take(NG - 2 + u, u)
            act.wait_ge(shifted, 1)
            nc.scalar.activation(b_exp[:], b_exp[:], ACT.Exp, scale=1.0 if tanh else 0.2).then_inc(exp_ready, 1)
            if tanh:
                act.wait_ge(weight_ready, 1)
                act.wait_ge(ones_set, 1)
                act.wait_ge(v_taken, NG)
                for n in range(SPLITS + 1):
                    if n < SPLITS:
                        for at in range(n * T // SPLITS, (n + 1) * T // SPLITS):
                            ins = nc.scalar.activation(V_parts[:, at, 0, :], V[:, at, :], ACT.Copy, scale=b_exp[:, at:at + 1])
                        ins.then_inc(high_ready, 1)
                    if n:
                        tiles = slice((n - 1) * T // SPLITS, n * T // SPLITS)
                        act.wait_ge(rest_ready, n)
                        nc.scalar.activation(V_parts[:, tiles, 1, :], V[:, tiles, :], ACT.Copy).then_inc(mid_ready, 1)

        @block.vector
        def _(dve):
            links = [0]

            def link(ins):
                links[0] += 1
                ins.then_inc(chain, 1)
                dve.wait_ge(chain, links[0])

            def normalise(g, u):
                if is_later(g - 1):
                    dve.wait_ge(tr_done, g - 1)
                for j in range(G):
                    at = bass.ds(g * G + j, 1)
                    last = nc.vector.tensor_scalar(xn[u][:, j:j + 1, :], x[:, at, :], k.rstd[:, at], k.shift[:, at],
                                                   ALU.mult, ALU.add)
                last.then_inc(xn_ready, 1)

            def take(g, u):
                dve.wait_ge(v_done, g + 1)
                at = bass.ds(g * G, G)
                if tanh:
                    if is_later(g - 1):
                        dve.wait_ge(h_taken, g - 1)
                    nc.vector.tensor_tensor(h[u][:], v_ps[u][:, :, 0:D], b_row[:, None, :].to_broadcast([P, G, D]),
                                            ALU.add).then_inc(h_ready, 1)
                    nc.vector.tensor_copy(V[:, at, 0:D], v_ps[u][:, :, 0:D]).then_inc(v_taken, 1)
                elif bias is not None:
                    nc.vector.tensor_tensor(V[:, at, 0:D], v_ps[u][:, :, 0:D], b_row[:, None, :].to_broadcast([P, G, D]),
                                            ALU.add).then_inc(v_taken, 1)
                else:
                    nc.vector.tensor_copy(V[:, at, 0:D], v_ps[u][:, :, 0:D]).then_inc(v_taken, 1)
                if not tanh:
                    nc.vector.tensor_copy(b_col[:, at], v_ps[u][:, :, D]).then_inc(b_taken, 1)
                    dve.wait_ge(v_taken, g + 1)
                    nc.vector.tensor_reduce(v_part[:, bass.ds(g, 1), :], V[:, at, 0:D].rearrange("p t d -> p d t"),
                                            AX.X, ALU.add).then_inc(v_summed, 1)

            def reduce_h(g, u):
                at = bass.ds(g * G, G)
                dve.wait_ge(h_tanh, g + 1)
                nc.vector.tensor_reduce(h_sum[:, at], h[u][:], AX.X, ALU.add).then_inc(h_summed, 1)
                dve.wait_ge(h_summed, g + 1)
                nc.vector.tensor_tensor(h[u][:], h[u][:], aw_row[:, None, :].to_broadcast([P, G, D]),
                                        ALU.mult).then_inc(h_scaled, 1)
                dve.wait_ge(h_scaled, g + 1)
                nc.vector.tensor_reduce(b_col[:, at], h[u][:], AX.X, ALU.add).then_inc(h_taken, 1)

            ln.vector_part(dve)
            for u in range(2):
                normalise(u, u)
            def low_part(dve, n):
                tiles = slice(n * T // SPLITS, (n + 1) * T // SPLITS)
                dve.wait_ge(rest_ready, n + 1)
                dve.wait_ge(mid_ready, n + 1)
                nc.vector.tensor_tensor(V_parts[:, tiles, 2, :], V[:, tiles, :], V_parts[:, tiles, 1, :], ALU.subtract)

            dve.wait_ge(weights_in, 16 * len(loads))
            if not tanh:
                if bias is not None:
                    nc.vector.tensor_copy(b_wide[:], bc[:, 0:1].to_broadcast([P, P])).then_inc(wide_ready, 1)
                dve.wait_ge(wa_done, 1 if bias is None else 2)
                link(nc.vector.tensor_copy(wa[:], wa_ps))
                nc.vector.tensor_copy(W_b[:, D:VW], wa[:, 1:2])
                nc.vector.tensor_copy(wa_wide[:], wa[:, 0:1].to_broadcast([P, P])).then_inc(wa_ready, 1)
                if bias is not None:
                    if has_ba:
                        link(nc.vector.tensor_copy(const2[:], c_ps))
                        nc.vector.tensor_tensor(const2[:, 0:1], const2[:, 0:1], ba[:], ALU.add).then_inc(const_ready, 1)
                    else:
                        nc.vector.tensor_copy(const2[:], c_ps).then_inc(const_ready, 1)
                else:
                    nc.vector.memset(const2[:], 0.0).then_inc(const_ready, 1)
            for u in range(2):
                normalise(2 + u, u)
            for u in range(2):
                take(u, u)
            if tanh:
                for u in range(2):
                    reduce_h(u, u)
            with dve.Fori(1, NG // 2 - 1) as i:
                for u in range(2):
                    normalise(i * 2 + (2 + u), u)
                for u in range(2):
                    take(i * 2 + u, u)
                if tanh:
                    for u in range(2):
                        reduce_h(i * 2 + u, u)
            for u in range(2):
                take(NG - 2 + u, u)
            if tanh:
                for u in range(2):
                    reduce_h(NG - 2 + u, u)
                dve.wait_ge(h_taken, NG)
            else:
                dve.wait_ge(b_taken, NG)
                link(nc.vector.tensor_scalar(b_col[:], b_col[:], const2[:, 1:2], None, ALU.add))
            nc.vector.tensor_reduce(b_top[:], b_col[:], AX.X, ALU.max).then_inc(top_ready, 1)
            if not tanh:
                dve.wait_ge(v_summed, NG)
                nc.vector.tensor_reduce(v_sum[:], v_part[:].rearrange("p t d -> p d t"), AX.X, ALU.add).then_inc(vsum_ready, 1)
            dve.wait_ge(top_all, 1)
            if not tanh:
                link(nc.vector.tensor_scalar(limit[:], b_all[:], -1.0, ROW_MAX / 0.8, ALU.mult, ALU.add))
                nc.vector.tensor_scalar(b_exp[:], b_col[:], b_all[:], None, ALU.subtract).then_inc(shifted, 1)
                link(nc.vector.tensor_scalar(b_all[:], b_all[:], 0.2, None, ALU.mult))
                nc.vector.tensor_scalar(b_col[:], b_col[:], b_all[:], None, ALU.subtract)
                dve.wait_ge(a_taken, NG)
                nc.vector.tensor_scalar(a_row[:], a_row[:], limit[:], None, ALU.min)
                dve.wait_ge(sum_done, 1)
                nc.vector.tensor_copy(t["all_sum"][:], sum_ps)
            else:
                nc.vector.tensor_scalar(b_exp[:], b_col[:], b_all[:], None, ALU.subtract).then_inc(shifted, 1)
                dve.wait_ge(exp_ready, 1)
                link(nc.vector.tensor_scalar(h_sum[:], h_sum[:], 0.0, None, ALU.not_equal))
                nc.vector.tensor_tensor(b_exp[:], b_exp[:], h_sum[:], ALU.mult).then_inc(weight_ready, 1)
                dve.wait_ge(weight_ready, 1)
                dve.wait_ge(ones_set, 1)
                dve.wait_ge(v_taken, NG)
                for n in range(SPLITS):
                    dve.wait_ge(high_ready, n + 1)
                    for at in range(n * T // SPLITS, (n + 1) * T // SPLITS):
                        ins = nc.vector.scalar_tensor_tensor(out=V[:, at, :], in0=V[:, at, :], scalar=b_exp[:, at:at + 1],
                                                             in1=V_parts[:, at, 0, :], op0=ALU.mult, op1=ALU.subtract)
                    ins.then_inc(rest_ready, 1)
                    if n:
                        low_part(dve, n - 1)
                low_part(dve, SPLITS - 1)


def gnn_attend(k, name, kind, t, load_adj):
    nc, x, mask = k.nc, k.x, k.mask
    V, a_row, b_col, b_exp, all_sum = t["V"], t["a_row"], t["b_col"], t["b_exp"], t["all_sum"]
    tanh, elu = kind == "tanh", kind == "elu"
    STEPS = 8
    PE_STEPS = 14
    RING = 4
    with stage(k), ExitStack() as ctx:
        sb = lambda shape, dt=F32: k.work.cut(shape, dt)
        sem = lambda n: nc.alloc_semaphore(f"{name}_m_{n}")
        p = [sb([P, IC], BF16 if tanh else F32) for u in range(2)]
        e = [sb([P, IC]) for u in range(2)] if not tanh else None
        num = sb([P, NB, VW])
        den, lone, inv, lone_inv = (sb([P, NB]) for _ in range(4))
        low = sb([P, NB, D]) if elu else None
        adj = [sb([P, IC], I32) for u in range(RING)] if load_adj else None
        V_parts = t["V_parts"]
        acc_width = 512 if tanh else 256
        acc = k.banks.cut([P, NB, acc_width], align=512)
        per_bank, used = 512 // acc_width, PARTS * VW if tanh else VW
        num_parts = V[:].rearrange("p t d -> p (t d)")[:, 0:NB * used].rearrange("p (b n d) -> p b n d", b=NB, d=VW) if tanh else None
        AH = NB // 2
        half_taken, parts_added = sem("half_taken"), sem("parts_added")
        e_ready, p_ready, p_used, acc_taken = (sem(n) for n in ("e_ready", "p_ready", "p_used", "acc_taken"))
        chain, low_ready, low_exp, x_added = (sem(n) for n in ("chain", "low_ready", "low_exp", "x_added"))
        adj_in = [sem(f"adj_in{u}") for u in range(RING)]
        mask_ready, act_passed = sem("mask_ready"), sem("act_passed")
        block = ctx.enter_context(nc.Block())

        if load_adj:
            @block.sync
            def _(sp):
                def load(s, jt, ic, u):
                    if is_later(s - (RING - 1)):
                        sp.wait_ge(mask_ready, s - (RING - 1))
                    sp.dma_start(adj[u][:], k.dram["adjT"][bass.ds(jt * P, P), bass.ds(ic * IC, IC)]).then_inc(adj_in[u], 16)

                for u in range(RING):
                    load(u, u, 0, u)
                with sp.Fori(1, T // RING) as i:
                    for u in range(RING):
                        load(i * RING + u, i * RING + u, 0, u)
                with sp.Fori(1, NI) as ic:
                    with sp.Fori(0, T // RING) as i:
                        for u in range(RING):
                            load(ic * T + i * RING + u, i * RING + u, ic, u)

        @block.scalar
        def _(act):
            def exps(ic, i, u):
                s = ic * T + i * STEPS + u
                if is_later(s - 1):
                    wait_apart(act, p_ready, s - 1, act_passed)
                nc.scalar.activation(e[u % 2][:], a_row[:, bass.ds(ic * IC, IC)], ACT.Exp, scale=0.8,
                                     bias=b_col[:, bass.ds(i * STEPS + u, 1)]).then_inc(e_ready, 1)

            def take(ic):
                act.wait_ge(p_used, ic * T + T)
                if is_later(ic):
                    act.wait_ge(x_added, ic)
                if tanh:
                    nc.scalar.activation(num_parts[:, 0:AH, :, :].rearrange("p b n d -> p b (n d)"), acc[:, 0:AH, 0:used],
                                         ACT.Copy).then_inc(acc_taken, 1)
                else:
                    nc.scalar.activation(num[:], acc[:, :, 0:VW], ACT.Copy).then_inc(acc_taken, 1)

            def low_half(ic):
                if elu:
                    act.wait_ge(low_ready, ic + 1)
                    nc.scalar.activation(low[:], low[:], ACT.Exp).then_inc(low_exp, 1)

            if tanh:
                take(0)
                with act.Fori(1, NI) as ic:
                    take(ic)
            else:
                for u in range(STEPS):
                    exps(0, 0, u)
                with act.Fori(1, T // STEPS) as i:
                    for u in range(STEPS):
                        exps(0, i, u)
                with act.Fori(1, NI) as ic:
                    for u in range(2):
                        exps(ic, 0, u)
                    take(ic - 1)
                    for u in range(2, STEPS):
                        exps(ic, 0, u)
                    for u in range(2):
                        exps(ic, 1, u)
                    low_half(ic - 1)
                    for u in range(2, STEPS):
                        exps(ic, 1, u)
                    with act.Fori(2, T // STEPS) as i:
                        for u in range(STEPS):
                            exps(ic, i, u)
                take(NI - 1)
                low_half(NI - 1)

        @block.vector
        def _(dve):
            def weights(ic, i, u):
                cols = bass.ds(ic * IC, IC)
                if load_adj:
                    for v in (u, u + 1):
                        dve.wait_ge(adj_in[v % RING], (ic * (T // RING) + i * (STEPS // RING)) * 16 + (v // RING + 1) * 16)
                        nc.vector.tensor_scalar(mask[:, bass.ds(i * STEPS + v, 1), cols], adj[v % RING][:, None, :], 0.0, None,
                                                ALU.is_gt).then_inc(mask_ready, 1)
                for v in (u, u + 1):
                    s, at = ic * T + i * STEPS + v, bass.ds(i * STEPS + v, 1)
                    if load_adj:
                        dve.wait_ge(mask_ready, s + 1)
                    if is_later(s - 1):
                        dve.wait_ge(p_used, s - 1)
                    if tanh:
                        nc.vector.tensor_copy(p[v % 2][:, None, :], mask[:, at, cols]).then_inc(p_ready, 1)
                    else:
                        dve.wait_ge(e_ready, s + 1)
                        nc.vector.scalar_tensor_tensor(out=p[v % 2][:, None, :], in0=e[v % 2][:, None, :],
                                                       scalar=b_exp[:, at], in1=mask[:, at, cols],
                                                       op0=ALU.max, op1=ALU.mult).then_inc(p_ready, 1)

            def link(n, ins):
                ins.then_inc(chain, 1)
                dve.wait_ge(chain, n)

            def finish_denominators(ic, links):
                if tanh:
                    dve.wait_ge(p_used, ic * T + T)
                    nc.vector.tensor_copy(num_parts[:, AH:NB, :, :].rearrange("p b n d -> p b (n d)"),
                                          acc[:, AH:NB, 0:used]).then_inc(half_taken, 1)
                    dve.wait_ge(half_taken, ic + 1)
                dve.wait_ge(acc_taken, ic + 1)
                if tanh:
                    nc.vector.tensor_tensor(num[:], num_parts[:, :, 1, :], num_parts[:, :, 2, :], ALU.add).then_inc(parts_added, 1)
                    dve.wait_ge(parts_added, ic * 2 + 1)
                    nc.vector.tensor_tensor(num[:], num[:], num_parts[:, :, 0, :], ALU.add).then_inc(parts_added, 1)
                    dve.wait_ge(parts_added, ic * 2 + 2)
                    link(links + 1, nc.vector.tensor_scalar(den[:], num[:, :, D], 1e-37, None, ALU.max))
                    link(links + 2, nc.vector.reciprocal(inv[:], den[:]))
                else:
                    link(links + 1, nc.vector.tensor_scalar(lone[:], num[:, :, D], 0.0, None, ALU.is_equal))
                    link(links + 2, nc.vector.scalar_tensor_tensor(out=den[:], in0=lone[:], scalar=float(N), in1=num[:, :, D],
                                                                   op0=ALU.mult, op1=ALU.add))
                    link(links + 3, nc.vector.reciprocal(inv[:], den[:]))

            def finish_lone(ic, links, blocks):
                if not tanh:
                    for b in blocks:
                        ins = nc.vector.scalar_tensor_tensor(out=num[:, b, 0:D], in0=all_sum[:], scalar=lone[:, b:b + 1],
                                                             in1=num[:, b, 0:D], op0=ALU.mult, op1=ALU.add)
                    link(links + 3 + blocks.stop // (NB // 2), ins)

            def finish_quotients(ic, links):
                before = links + (2 if tanh else 5)
                link(before + 1, nc.vector.tensor_tensor(num[:, :, 0:D], num[:, :, 0:D],
                                                         inv[:, :, None].to_broadcast([P, NB, D]), ALU.mult))
                if elu:
                    nc.vector.tensor_scalar(low[:], num[:, :, 0:D], 0.0, None, ALU.min).then_inc(low_ready, 1)
                    link(before + 2, nc.vector.tensor_scalar(num[:, :, 0:D], num[:, :, 0:D], 0.0, -1.0, ALU.max, ALU.add))

            def finish_x(ic, links):
                tiles = bass.ds(ic * NB, NB)
                if elu:
                    dve.wait_ge(low_exp, ic + 1)
                    link(links + 8, nc.vector.tensor_tensor(num[:, :, 0:D], num[:, :, 0:D], low[:], ALU.add))
                nc.vector.tensor_tensor(x[:, tiles, :], x[:, tiles, :], num[:, :, 0:D], ALU.add).then_inc(x_added, 1)
                dve.wait_ge(x_added, ic + 1)

            def finish_stats(ic, blocks):
                for b in blocks:
                    tile_stats(k, bass.ds(ic * NB + b, 1))

            halves = range(0, NB // 2), range(NB // 2, NB)
            n_links = 3 if tanh else 8 if elu else 6
            for u in range(0, STEPS, 2):
                weights(0, 0, u)
            with dve.Fori(1, T // STEPS) as i:
                for u in range(0, STEPS, 2):
                    weights(0, i, u)
            with dve.Fori(1, NI) as ic:
                last = ic - 1, (ic - 1) * n_links
                weights(ic, 0, 0)
                finish_denominators(*last)
                weights(ic, 0, 2)
                finish_lone(*last, halves[0])
                weights(ic, 0, 4)
                finish_lone(*last, halves[1])
                weights(ic, 0, 6)
                finish_quotients(*last)
                weights(ic, 1, 0)
                finish_x(*last)
                weights(ic, 1, 2)
                finish_stats(ic - 1, halves[0])
                weights(ic, 1, 4)
                finish_stats(ic - 1, halves[1])
                weights(ic, 1, 6)
                with dve.Fori(2, T // STEPS) as i:
                    for u in range(0, STEPS, 2):
                        weights(ic, i, u)
            last = NI - 1, (NI - 1) * n_links
            finish_denominators(*last)
            for blocks in halves:
                finish_lone(*last, blocks)
            finish_quotients(*last)
            finish_x(*last)
            for blocks in halves:
                finish_stats(NI - 1, blocks)

        @block.tensor
        def _(pe):
            def step(ic, jt, u, first=False, last=False):
                pe.wait_ge(p_ready, ic * T + jt + 1)
                at = bass.ds(jt, 1)
                for b in range(NB):
                    ins = nc.tensor.matmul(acc[:, b, 0:used], p[u][:, b * P:(b + 1) * P], V_parts[:, at, :, :] if tanh else V[:, at, :],
                                           start=first and b % per_bank == 0, stop=last, skip_group_check=True)
                ins.then_inc(p_used, 1)

            def chunk(ic):
                if is_later(ic):
                    pe.wait_ge(acc_taken, ic)
                    if tanh:
                        pe.wait_ge(half_taken, ic)
                step(ic, 0, 0, first=True)
                step(ic, 1, 1)
                with pe.Fori(0, (T - 4) // PE_STEPS) as i:
                    for u in range(PE_STEPS):
                        step(ic, i * PE_STEPS + (2 + u), u % 2)
                step(ic, T - 2, 0)
                step(ic, T - 1, 1, last=True)

            chunk(0)
            with pe.Fori(1, NI) as ic:
                chunk(ic)




def ffn_spec(s):
    return {
        0: dict(E=8, hidden=[128, 128, 85], kind="gated", router="softmax_norm"),
        1: dict(E=6, hidden=[128], kind="deep", router="softmax_twice"),
        2: dict(E=8, hidden=[128, 128], kind="relu", router="softmax"),
        3: dict(E=8, hidden=[128, 128], kind="gelu", router="mask"),
    }[s]


def ffn_layer(k, s):
    nc, name, spec = k.nc, f"L{s}f", ffn_spec(s)
    with sublayer(k), ExitStack() as ctx:
        sb = lambda shape, dt=F32: k.work.cut(shape, dt)
        t = {"xT": sb([P, N]), "logits": sb([P, T, spec["E"]]),
             "gates": sb([P, T, spec["E"]])}
        w = ExpertWeights(k, name, spec)
        ffn_transpose(k, name, spec, t, load_experts=w.load)
        ffn_route(k, name, spec, t)
        ffn_experts(k, name, spec, t, w)


class ExpertWeights:

    def __init__(self, k, name, spec):
        sb = k.work.cut
        E, M, H = spec["E"], len(spec["hidden"]), sum(spec["hidden"])
        gated, deep, bias = spec["kind"] == "gated", spec["kind"] == "deep", spec["kind"] != "gated"
        self.w_in = sb([P, E, H])
        self.w_up = sb([P, E, H]) if gated else None
        self.w_mid = sb([P, E, D]) if deep else None
        self.w_out = sb([P, E, M, D])
        self.b_in = sb([P, E, M]) if bias else None
        self.b_mid = sb([P, E]) if deep else None
        self.b_out = sb([P, E, D]) if bias else None
        self.loaded = k.nc.alloc_semaphore(f"{name}_experts_loaded")
        dr = k.dram
        self.loads = [(self.w_in[:], dr[f"{name}_w_in"]), (self.w_out[:], dr[f"{name}_w_out"])]
        if gated:
            self.loads += [(self.w_up[:], dr[f"{name}_w_up"])]
        if deep:
            self.loads += [(self.w_mid[:], dr[f"{name}_w_mid"]), (self.b_mid[:], dr[f"{name}_b_mid"])]
        if bias:
            self.loads += [(self.b_in[:], dr[f"{name}_b_in"]), (self.b_out[:], dr[f"{name}_b_out"].partition_broadcast(P))]

    def load(self, sp):
        for out, src in self.loads:
            sp.dma_start(out, src).then_inc(self.loaded, 16)


def ffn_transpose(k, name, spec, t, src=None, load_experts=None):
    nc, x, E = k.nc, k.x if src is None else src, spec["E"]
    deep, gated = spec["kind"] == "deep", spec["kind"] == "gated"
    RH = D // 2
    with stage(k), ExitStack() as ctx:
        sb = lambda shape, dt=F32: k.work.cut(shape, dt)
        sem = lambda n: nc.alloc_semaphore(f"{name}_t_{n}")
        ps = lambda shape: k.banks.cut(shape, align=512)
        r_w = sb([RH if deep else P, E])
        r_b = sb([P, E]) if not gated else None
        ln2 = sb([P, 1]) if gated else None
        r_w1, r_b1 = (sb([P, RH]), sb([RH, 1])) if deep else (None, None)
        r_b2 = sb([P, E]) if spec["router"] == "softmax" else None
        xn = [sb([P, G, D]) for u in range(2)]
        xs = [sb([P, GW]) for u in range(2)]
        rh = [sb([RH, GW]) for u in range(2)] if deep else None
        xT_ps = [ps([P, GW]) for u in range(2)]
        rh_ps = [ps([RH, GW]) for u in range(2)] if deep else None
        lg_ps = ps([P, 512])
        weights_in, xn_ready, tr_done, xs_ready, xT_ready = (
            sem(n) for n in ("weights_in", "xn_ready", "tr_done", "xs_ready", "xT_ready"))
        ln = LayerNorm(k, name) if not gated else None
        rh_done, rh_ready, lg_done, bias_ready = (sem(n) for n in ("rh_done", "rh_ready", "lg_done", "bias_ready"))
        block = ctx.enter_context(nc.Block())
        dr = k.dram
        loads = [(r_w[:], dr[f"{name}_r_w"])]
        loads += [(ln2[:], dr[f"{name}_ln2"])] if gated else [(r_b[:], dr[f"{name}_r_b"].partition_broadcast(P))]
        if deep:
            loads += [(r_w1[:], dr[f"{name}_r_w1"]), (r_b1[:], dr[f"{name}_r_b1"])]
        if r_b2 is not None:
            loads += [(r_b2[:], dr[f"{name}_r_b2"].partition_broadcast(P))]

        @block.sync
        def _(sp):
            for out, src in loads:
                sp.dma_start(out, src).then_inc(weights_in, 16)
            if load_experts is not None:
                load_experts(sp)

        @block.vector
        def _(dve):
            def normalise(g, u):
                if is_later(g - 1):
                    dve.wait_ge(tr_done, g - 1)
                for j in range(G):
                    at = bass.ds(g * G + j, 1)
                    last = nc.vector.tensor_scalar(xn[u][:, j:j + 1, :], x[:, at, :], k.rstd[:, at], k.shift[:, at],
                                                   ALU.mult, ALU.add)
                last.then_inc(xn_ready, 1)

            def keep(g, u):
                dve.wait_ge(xs_ready, g + 1)
                nc.vector.tensor_copy(t["xT"][:, bass.ds(g * GW, GW)], xs[u][:]).then_inc(xT_ready, 1)

            if ln is not None:
                ln.vector_part(dve)
            for u in range(2):
                normalise(u, u)
            with dve.Fori(0, NG // 2 - 1) as i:
                for u in range(2):
                    normalise(i * 2 + (2 + u), u)
                for u in range(2):
                    keep(i * 2 + u, u)
            for u in range(2):
                keep(NG - 2 + u, u)
            dve.wait_ge(lg_done, NG)
            dve.wait_ge(weights_in, 16 * len(loads))
            if r_b2 is not None:
                nc.vector.tensor_tensor(r_b[:], r_b[:], r_b2[:], ALU.add).then_inc(bias_ready, 1)
                dve.wait_ge(bias_ready, 1)
            all_logits = lg_ps[:, 0:T * E].rearrange("p (t e) -> p t e", e=E)
            if gated:
                nc.vector.tensor_copy(t["logits"][:], all_logits)
            else:
                nc.vector.tensor_tensor(t["logits"][:], all_logits, r_b[:, None, :].to_broadcast([P, T, E]), ALU.add)

        @block.scalar
        def _(act):
            def copy_T(g, u):
                act.wait_ge(tr_done, g + 1)
                if is_later(g - 1):
                    act.wait_ge(rh_done if deep else lg_done, g - 1)
                    act.wait_ge(xT_ready, g - 1)
                nc.scalar.activation(xs[u][:], xT_ps[u][:], ACT.Copy, scale=ln2[:] if gated else 1.0).then_inc(xs_ready, 1)

            def relu(g, u):
                act.wait_ge(rh_done, g + 1)
                if is_later(g - 1):
                    act.wait_ge(lg_done, g - 1)
                nc.scalar.activation(rh[u][:], rh_ps[u][:], ACT.Relu, bias=r_b1[:]).then_inc(rh_ready, 1)

            if ln is not None:
                ln.scalar_part(act)
            act.wait_ge(weights_in, 16 * len(loads))
            for u in range(2):
                copy_T(u, u)
            for u in range(2):
                copy_T(2 + u, u)
            if deep:
                for u in range(2):
                    relu(u, u)
            with act.Fori(1, NG // 2 - 1) as i:
                for u in range(2):
                    copy_T(i * 2 + (2 + u), u)
                if deep:
                    for u in range(2):
                        relu(i * 2 + u, u)
            if deep:
                for u in range(2):
                    relu(NG - 2 + u, u)

        @block.tensor
        def _(pe):
            def transposes(g, u):
                pe.wait_ge(xn_ready, g + 1)
                if is_later(g - 1):
                    pe.wait_ge(xs_ready, g - 1)
                for j in range(G):
                    last = nc.tensor.transpose(xT_ps[u][:, j * P:(j + 1) * P], xn[u][:, j, :], k.ident[:])
                last.then_inc(tr_done, 1)

            def hidden(g, u):
                if deep:
                    pe.wait_ge(xs_ready, g + 1)
                    if is_later(g - 1):
                        pe.wait_ge(rh_ready, g - 1)
                    nc.tensor.matmul(rh_ps[u][:], r_w1[:], xs[u][:], start=True, stop=True).then_inc(rh_done, 1)

            def logits(g, u):
                if deep:
                    pe.wait_ge(rh_ready, g + 1)
                else:
                    pe.wait_ge(xs_ready, g + 1)
                src = rh[u] if deep else xs[u]
                for j in range(G):
                    last = nc.tensor.matmul(lg_ps[:, bass.ds((g * G + j) * E, E)], src[:, j * P:(j + 1) * P], r_w[:],
                                            start=True, stop=True)
                last.then_inc(lg_done, 1)

            def route(i):
                for u in range(2):
                    hidden(i * 2 + u, u)
                for u in range(2):
                    logits(i * 2 + u, u)

            pe.wait_ge(weights_in, 16 * len(loads))
            for u in range(2):
                transposes(u, u)
            for u in range(2):
                transposes(2 + u, u)
            route(0)
            with pe.Fori(1, NG // 2 - 1) as i:
                for u in range(2):
                    transposes(i * 2 + (2 + u), u)
                route(i)
            route(NG // 2 - 1)


def ffn_route(k, name, spec, t, load_experts=None):
    nc, E, router = k.nc, spec["E"], spec["router"]
    logits, gates = t["logits"], t["gates"]
    with stage(k), ExitStack() as ctx:
        sb = lambda shape, dt=F32: k.work.cut(shape, dt)
        sem = lambda n: nc.alloc_semaphore(f"{name}_r_{n}")
        first = sb([P, E])
        sel = [sb([P, T, E]) for n in range(2)]
        rank, score = sb([P, T, E]), sb([P, T, E])
        top = [sb([P, T]) for n in range(2)]
        top_rank, one, two = sb([P, T]), sb([P, T]), sb([P, T])
        total = sb([P, T])
        chain, to_exp, exp_done = sem("chain"), sem("to_exp"), sem("exp_done")
        block = ctx.enter_context(nc.Block())
        wide = lambda a: a[:, :, None].to_broadcast([P, T, E])
        softmax = router in ("softmax_norm", "softmax_twice")

        if load_experts is not None:
            @block.sync
            def _(sp):
                load_experts(sp)

        @block.scalar
        def _(act):
            if softmax:
                act.wait_ge(to_exp, 1)
                nc.scalar.activation(score[:], score[:], ACT.Exp).then_inc(exp_done, 1)
            if router in ("softmax", "softmax_twice"):
                act.wait_ge(to_exp, 2 if softmax else 1)
                nc.scalar.activation(two[:], two[:], ACT.Exp).then_inc(exp_done, 1)

        @block.vector
        def _(dve):
            links = [0]

            def link(ins):
                links[0] += 1
                ins.then_inc(chain, 1)
                dve.wait_ge(chain, links[0])

            def tt(out, a, b, op):
                link(nc.vector.tensor_tensor(out, a, b, op))

            def reduce(out, a, op):
                link(nc.vector.tensor_reduce(out, a, AX.X, op))

            for e in range(E):
                nc.vector.memset(first[:, e:e + 1], float(E - e))
            if softmax:
                reduce(top[0][:], logits[:], ALU.max)
                nc.vector.tensor_tensor(score[:], logits[:], wide(top[0]), ALU.subtract).then_inc(to_exp, 1)
                dve.wait_ge(exp_done, 1)
                reduce(total[:], score[:], ALU.add)
                link(nc.vector.reciprocal(total[:], total[:]))
                tt(score[:], score[:], wide(total), ALU.mult)
            else:
                link(nc.vector.tensor_copy(score[:], logits[:]))
            for n in range(2):
                reduce(top[n][:], score[:], ALU.max)
                tt(rank[:], score[:], wide(top[n]), ALU.is_equal)
                tt(rank[:], rank[:], first[:, None, :].to_broadcast([P, T, E]), ALU.mult)
                reduce(top_rank[:], rank[:], ALU.max)
                tt(sel[n][:], rank[:], wide(top_rank), ALU.is_equal)
                if n == 0:
                    link(nc.vector.scalar_tensor_tensor(out=score[:], in0=sel[0][:], scalar=-1e30, in1=score[:],
                                                        op0=ALU.mult, op1=ALU.add))
            if router in ("mask", "softmax_norm"):
                tt(gates[:], sel[0][:], sel[1][:], ALU.add)
            if router == "softmax_norm":
                tt(one[:], top[0][:], top[1][:], ALU.add)
                link(nc.vector.tensor_scalar(one[:], one[:], 1e-9, None, ALU.add))
                link(nc.vector.reciprocal(one[:], one[:]))
                tt(two[:], top[1][:], one[:], ALU.mult)
                tt(one[:], top[0][:], one[:], ALU.mult)
            elif router != "mask":
                nc.vector.tensor_tensor(two[:], top[1][:], top[0][:], ALU.subtract).then_inc(to_exp, 1)
                dve.wait_ge(exp_done, 2 if softmax else 1)
                link(nc.vector.tensor_scalar(one[:], two[:], 1.0, None, ALU.add))
                link(nc.vector.reciprocal(one[:], one[:]))
                tt(two[:], two[:], one[:], ALU.mult)
            if router != "mask":
                tt(sel[0][:], sel[0][:], wide(one), ALU.mult)
                tt(sel[1][:], sel[1][:], wide(two), ALU.mult)
                tt(gates[:], sel[0][:], sel[1][:], ALU.add)


def ffn_experts(k, name, spec, t, w):
    nc, x, E, kind, hidden = k.nc, k.x, spec["E"], spec["kind"], spec["hidden"]
    xT, gates = t["xT"], t["gates"]
    M = len(hidden)
    H = sum(hidden)
    units = [(e, m) for e in range(E) for m in range(M)]
    U = len(units)
    gated, deep = kind == "gated", kind == "deep"
    HS = 3 if gated else 2
    bias = not gated
    with stage(k), ExitStack() as ctx:
        sb = lambda shape, dt=F32: k.work.cut(shape, dt)
        sem = lambda n: nc.alloc_semaphore(f"{name}_e_{n}")
        ps = lambda shape: k.banks.cut(shape, align=512)
        w_in, w_up, w_mid, w_out, b_in, b_mid, b_out = w.w_in, w.w_up, w.w_mid, w.w_out, w.b_in, w.b_mid, w.b_out
        experts_loaded, n_loads = w.loaded, len(w.loads)
        act_out = [sb([P, GW]) for u in range(2)] if gated or deep else None
        hid = [sb([P, GW]) for u in range(HS)]
        in_ps = [ps([P, GW]) for u in range(HS)]
        up_ps = [ps([P, GW]) for u in range(HS)] if gated else None
        mid_ps = [ps([P, GW]) for u in range(2)] if deep else None
        y_ps = [ps([P, G, D]) for u in range(2)]
        in_done, in_taken, mid_done = sem("in_done"), sem("in_taken"), sem("mid_done")
        hid_ready, out_done, y_taken, x_chain = sem("hid_ready"), sem("out_done"), sem("y_taken"), sem("x_chain")
        block = ctx.enter_context(nc.Block())

        @block.tensor
        def _(pe):
            def first_product(c, n):
                e, m = units[n]
                lo, w = sum(hidden[:m]), hidden[m]
                at = c * U + n
                u = n % HS
                if deep:
                    pe.wait_ge(in_taken, at + 1)
                else:
                    pe.wait_ge(hid_ready, at + 1)
                cols = xT[:, bass.ds(c * GW, GW)]
                ins = nc.tensor.matmul(in_ps[u][0:w, :], w_in[:, e, lo:lo + w], cols, start=True, stop=True)
                if gated:
                    ins = nc.tensor.matmul(up_ps[u][0:w, :], w_up[:, e, lo:lo + w], cols, start=True, stop=True)
                ins.then_inc(in_done, 1)

            def mid_product(c, n):
                e, at, u = units[n][0], c * U + n, n % 2
                pe.wait_ge(in_taken, at + 3)
                pe.wait_ge(hid_ready, at + 1)
                nc.tensor.matmul(mid_ps[u][:], w_mid[:, e, :], act_out[u][:], start=True, stop=True).then_inc(mid_done, 1)

            def out_product(c, n):
                e, m = units[n]
                w, at, u = hidden[m], c * U + n, n % HS
                pe.wait_ge(hid_ready, at + HS + 1)
                if m == 0:
                    pe.wait_ge(y_taken, c * E + e + 1)
                for b in range(G):
                    ins = nc.tensor.matmul(y_ps[e % 2][:, b, :], hid[u][0:w, b * P:(b + 1) * P], w_out[0:w, e, m, :],
                                           start=m == 0 and b == 0, stop=m == M - 1, skip_group_check=True)
                ins.then_inc(out_done, 1)

            def unit(c, n, last=False):
                ahead = 2 if deep or gated else 1
                for step, product in ((ahead, first_product),) + (((1, mid_product),) if deep else ()):
                    if n + step < U:
                        product(c, n + step)
                    elif not last:
                        product(c + 1, n + step - U)
                out_product(c, n)

            pe.sem_inc(out_done, HS)
            pe.wait_ge(experts_loaded, 16 * n_loads)
            first_product(0, 0)
            if deep or gated:
                first_product(0, 1)
            if deep:
                mid_product(0, 0)
            with pe.Fori(0, NG - 1) as c:
                for n in range(U):
                    unit(c, n)
            for n in range(U):
                unit(NG - 1, n, last=True)

        @block.scalar
        def _(act):
            def unit(c, n):
                e, m = units[n]
                w, at, u = hidden[m], c * U + n, n % HS
                act.wait_ge(in_done, at + 1)
                if gated:
                    act.wait_ge(hid_ready, at + HS - 1)
                    nc.scalar.activation(act_out[n % 2][0:w, :], in_ps[u][0:w, :], ACT.Silu).then_inc(in_taken, 1)
                elif deep:
                    act.wait_ge(mid_done, at + 1)
                    nc.scalar.activation(act_out[u][:], in_ps[u][:], ACT.Relu, bias=b_in[:, e, m:m + 1]).then_inc(in_taken, 1)
                else:
                    act.wait_ge(out_done, at + 1)
                    nc.scalar.activation(hid[u][0:w, :], in_ps[u][0:w, :], ACT.Gelu if kind == "gelu" else ACT.Relu,
                                         bias=b_in[:, e, m:m + 1]).then_inc(hid_ready, 1)

            def mid_unit(c, n):
                e, at, u = units[n][0], c * U + n, n % HS
                act.wait_ge(mid_done, at + 3)
                act.wait_ge(out_done, at + 1)
                nc.scalar.activation(hid[u][:], mid_ps[u][:], ACT.Relu, bias=b_mid[:, e:e + 1]).then_inc(hid_ready, 1)

            if not gated:
                act.sem_inc(hid_ready, HS)
            if deep:
                act.sem_inc(in_taken, 2)
            act.wait_ge(experts_loaded, 16 * n_loads)
            if deep:
                unit(0, 0)
                with act.Fori(0, NG - 1) as c:
                    for n in range(U):
                        unit(c, n + 1) if n + 1 < U else unit(c + 1, 0)
                        mid_unit(c, n)
                for n in range(U):
                    if n + 1 < U:
                        unit(NG - 1, n + 1)
                    mid_unit(NG - 1, n)
            else:
                with act.Fori(0, NG) as c:
                    for n in range(U):
                        unit(c, n)

        @block.vector
        def _(dve):
            def product(c, n):
                e, m = units[n]
                w, at, u = hidden[m], c * U + n, n % HS
                dve.wait_ge(in_taken, at + 1)
                dve.wait_ge(out_done, at + 1)
                nc.vector.tensor_tensor(hid[u][0:w, :], act_out[n % 2][0:w, :], up_ps[u][0:w, :], ALU.mult).then_inc(hid_ready, 1)

            n_chain = 2 if bias else 1

            def add(c, e):
                done = (c * E + e) * n_chain
                dve.wait_ge(out_done, (c * E + e) * M + M + HS)
                for b in range(G):
                    at = bass.ds(c * G + b, 1)
                    ins = nc.vector.scalar_tensor_tensor(out=x[:, at, :], in0=y_ps[e % 2][:, b:b + 1, :], scalar=gates[:, at, e:e + 1],
                                                         in1=x[:, at, :], op0=ALU.mult, op1=ALU.add)
                ins.then_inc(y_taken, 1)
                dve.wait_ge(y_taken, c * E + e + 3)
                if bias:
                    for b in range(G):
                        at = bass.ds(c * G + b, 1)
                        ins = nc.vector.scalar_tensor_tensor(out=x[:, at, :], in0=b_out[:, e:e + 1, :], scalar=gates[:, at, e:e + 1],
                                                             in1=x[:, at, :], op0=ALU.mult, op1=ALU.add)
                    ins.then_inc(x_chain, 1)
                    dve.wait_ge(x_chain, c * E + e + 1)

            dve.sem_inc(y_taken, 2)
            if gated:
                dve.sem_inc(hid_ready, HS)
            if deep:
                dve.sem_inc(mid_done, 2)
            dve.wait_ge(experts_loaded, 16 * n_loads)
            with dve.Fori(0, NG) as c:
                for n, (e, m) in enumerate(units):
                    if gated:
                        product(c, n)
                        if m == 0 and e > 0:
                            add(c, e - 1)
                    else:
                        if m == M - 1:
                            add(c, e)
                if gated:
                    add(c, E - 1)
                for b in range(G):
                    tile_stats(k, bass.ds(c * G + b, 1))




def ffn0_layer(k):
    nc, name, spec = k.nc, "L0f", ffn_spec(0)
    with sublayer(k), ExitStack() as ctx:
        sb = lambda shape, dt=F32: k.work.cut(shape, dt)
        dram_r = nc.dram_tensor("r_scratch", (N, D), F32, kind="Internal").ap()
        causal_attention(k, dram_r)
        t = {"xT": sb([P, N]), "logits": sb([P, T, spec["E"]]),
             "gates": sb([P, T, spec["E"]])}
        with stage(k):
            r = sb([P, T, D])
            rms_norm_scale(k, r, dram_r)
            ffn_transpose(k, name, spec, t, src=r)
        w = ExpertWeights(k, name, spec)
        ffn_route(k, name, spec, t, load_experts=w.load)
        ffn_experts(k, name, spec, t, w)


def rms_norm_scale(k, r, dram_r):
    nc = k.nc
    with stage(k), ExitStack() as ctx:
        sem = lambda n: nc.alloc_semaphore(f"rms_{n}")
        even2, odd2 = k.work.cut([P, T]), k.work.cut([P, T])
        r_in, chain, mean_ready, root_ready = sem("r_in"), sem("chain"), sem("mean_ready"), sem("root_ready")
        block = ctx.enter_context(nc.Block())

        @block.sync
        def _(sp):
            for g in range(NG):
                sp.dma_start(r[:, g * G:(g + 1) * G, :],
                             dram_r[g * GW:(g + 1) * GW, :].rearrange("(t p) d -> p t d", p=P)).then_inc(r_in, 16)
            sp.wait_ge(r_in, 16 * NG)

        @block.scalar
        def _(act):
            act.wait_ge(mean_ready, 1)
            nc.scalar.activation(k.rstd[:], k.rstd[:], ACT.Sqrt).then_inc(root_ready, 1)

        @block.vector
        def _(dve):
            even_mean, even_m2, odd_mean, odd_m2 = (k.stats[:, :, n] for n in (1, 2, 4, 5))
            nc.vector.memset(k.shift[:], 0.0)
            nc.vector.tensor_tensor(even2[:], even_mean, even_mean, ALU.mult)
            nc.vector.tensor_tensor(odd2[:], odd_mean, odd_mean, ALU.mult)
            nc.vector.tensor_tensor(k.rstd[:], even_m2, odd_m2, ALU.add).then_inc(chain, 1)
            dve.wait_ge(chain, 1)
            nc.vector.tensor_tensor(even2[:], even2[:], odd2[:], ALU.add).then_inc(chain, 1)
            nc.vector.tensor_scalar(k.rstd[:], k.rstd[:], 1.0 / D, 1e-6, ALU.mult, ALU.add).then_inc(chain, 1)
            dve.wait_ge(chain, 3)
            nc.vector.scalar_tensor_tensor(out=k.rstd[:], in0=even2[:], scalar=0.5, in1=k.rstd[:],
                                           op0=ALU.mult, op1=ALU.add).then_inc(mean_ready, 1)
            dve.wait_ge(root_ready, 1)
            nc.vector.reciprocal(k.rstd[:], k.rstd[:])


NH, NKV, HD = 4, 2, 32
HV = HD + 1


def causal_attention(k, dram_r):
    with stage(k):
        kept = {"ka": k.work.cut([P, NKV, N], BF16), "kb": k.work.cut([2 * HD + 1, NKV, N], BF16),
                "v": k.work.cut([P, T, NKV, HV])}
        q_parts = k.nc.dram_tensor("q_parts", (PARTS, P, N), BF16, kind="Internal").ap()
        k_parts = k.nc.dram_tensor("k_parts", (PARTS, NKV * HD, N), BF16, kind="Internal").ap()
        attention_project(k, kept, q_parts, k_parts)
        attention_attend(k, kept, q_parts, dram_r)


def attention_project(k, kept, q_parts, k_parts):
    nc, x, d, ka, kb, v = k.nc, k.x, k.dram, kept["ka"], kept["kb"], kept["v"]
    scale = 1.0 / float(np.sqrt(np.float32(HD)))
    with stage(k), ExitStack() as ctx:
        sb = lambda shape, dt=F32: k.work.cut(shape, dt)
        sem = lambda n: nc.alloc_semaphore(f"ap_{n}")
        ps = lambda shape: k.banks.cut(shape, align=512)
        KW = NKV * HD
        w_q, w_qr = sb([P, D]), sb([P, D])
        w_k, w_kr, w_v = sb([P, KW]), sb([P, KW]), sb([P, KW])
        ln1 = sb([P, 1])
        rms, h_scale, h_shift = sb([P, T]), sb([P, T]), sb([P, T])
        cos, sin = [sb([P, GW]) for u in range(2)], [sb([P, GW]) for u in range(2)]
        xn = sb([P, G, D])
        xs = [sb([P, GW]) for u in range(2)]
        full = [sb([P, GW]), sb([KW, GW])]
        rest = [sb([P, GW]), sb([KW, GW])]
        parts = [sb([P, PARTS, GW], BF16), sb([KW, PARTS, GW], BF16)]
        xT_ps = [ps([P, GW]) for u in range(2)]
        ln = LayerNorm(k, "ap")
        f_ps = [ps([P, 2, GW]), ps([P, 2, GW])]
        v_ps = [ps([P, GW]) for u in range(2)]

        weights_in = sem("weights_in")
        tables_in = [sem(f"tables_in{u}") for u in range(2)]
        scaled, rms_ready, ones_set, chain = sem("scaled"), sem("rms_ready"), sem("ones_set"), sem("chain")
        xn_ready, tr_done, xs_ready = sem("xn_ready"), sem("tr_done"), sem("xs_ready")
        f_done, v_done, v_taken = sem("f_done"), sem("v_done"), sem("v_taken")
        rotated, high_ready, rest_ready, mid_ready, parts_ready = (
            sem(n) for n in ("rotated", "high_ready", "rest_ready", "mid_ready", "parts_ready"))
        parts_out, parts_in = [sem("q_out"), sem("k_out")], sem("parts_in")
        block = ctx.enter_context(nc.Block())
        loads = [(w_q[:], d["at_w_q"]), (w_qr[:], d["at_w_qr"]), (w_k[:], d["at_w_k"]), (w_kr[:], d["at_w_kr"]),
                 (w_v[:], d["at_w_v"]), (ln1[:], d["at_ln1"])]

        def tables(sp, c):
            cols = slice(c * GW, (c + 1) * GW)
            if c >= 2:
                sp.wait_ge(rotated, 4 * (c - 1))
            sp.dma_start(cos[c % 2][:], d["at_cos"][:, cols]).then_inc(tables_in[c % 2], 16)
            sp.dma_start(sin[c % 2][:], d["at_sin"][:, cols]).then_inc(tables_in[c % 2], 16)

        @block.sync
        def _(sp):
            for out, src in loads:
                sp.dma_start(out, src).then_inc(weights_in, 16)
            tables(sp, 0)
            tables(sp, 1)
            for c in range(NG):
                cols = slice(c * GW, (c + 1) * GW)
                sp.wait_ge(parts_ready, 2 * c + 1)
                sp.dma_start(q_parts[:, :, cols].rearrange("n p t -> p n t"), parts[0][:]).then_inc(parts_out[0], 16)
                sp.wait_ge(parts_ready, 2 * c + 2)
                sp.dma_start(k_parts[:, :, cols].rearrange("n p t -> p n t"), parts[1][:]).then_inc(parts_out[1], 16)
                if c + 2 < NG:
                    tables(sp, c + 2)
                if c % 2:
                    cols = slice((c - 1) * GW, (c + 1) * GW)
                    sp.wait_ge(parts_out[1], 16 * c + 16)
                    for row, part in enumerate((0, 1, 2, 0)):
                        sp.dma_start(ka[row * HD:(row + 1) * HD, :, cols],
                                     k_parts[part][:, cols].rearrange("(h r) t -> r h t", r=HD)).then_inc(parts_in, 16)
                    for row, part in enumerate((0, 1)):
                        sp.dma_start(kb[row * HD:(row + 1) * HD, :, cols],
                                     k_parts[part][:, cols].rearrange("(h r) t -> r h t", r=HD)).then_inc(parts_in, 16)
            sp.wait_ge(parts_in, 16 * 6 * NG // 2)
            sp.wait_ge(parts_out[0], 16 * NG)

        @block.gpsimd
        def _(pool):
            nc.gpsimd.memset(v[:, :, :, HD:HV], 1.0)

        @block.tensor
        def _(pe):
            pe.wait_ge(weights_in, 16 * len(loads))
            for c in range(NG + 1):
                if c < NG:
                    pe.wait_ge(xn_ready, c + 1)
                    if c >= 2:
                        pe.wait_ge(xs_ready, c - 1)
                    for j in range(G):
                        ins = nc.tensor.transpose(xT_ps[c % 2][:, j * P:(j + 1) * P], xn[:, j, :], k.ident[:])
                    ins.then_inc(tr_done, 1)
                if c:
                    last, xT = c - 1, xs[(c - 1) % 2]
                    pe.wait_ge(xs_ready, c)
                    for n, (w, width) in enumerate((((w_q, w_qr), P), ((w_k, w_kr), KW))):
                        if last:
                            pe.wait_ge(rotated, 4 * last - 4 + 2 * n + 1)
                        nc.tensor.matmul(f_ps[n][0:width, 0, :], w[0][:], xT[:], start=True, stop=True)
                        nc.tensor.matmul(f_ps[n][0:width, 1, :], w[1][:], xT[:], start=True, stop=True).then_inc(f_done, 1)
                    if last >= 2:
                        pe.wait_ge(v_taken, last - 1)
                    for j in range(G):
                        ins = nc.tensor.matmul(v_ps[last % 2][:, j * KW:(j + 1) * KW], xT[:, j * P:(j + 1) * P], w_v[:],
                                               start=True, stop=True)
                    ins.then_inc(v_done, 1)

        @block.scalar
        def _(act):
            ln.scalar_part(act)
            act.wait_ge(scaled, 1)
            nc.scalar.activation(rms[:], rms[:], ACT.Sqrt).then_inc(rms_ready, 1)
            act.wait_ge(weights_in, 16 * len(loads))
            for c in range(NG + 1):
                if c < NG:
                    act.wait_ge(tr_done, c + 1)
                    if c >= 2:
                        act.wait_ge(v_done, c - 1)
                    nc.scalar.activation(xs[c % 2][:], xT_ps[c % 2][:], ACT.Copy, scale=ln1[:]).then_inc(xs_ready, 1)
                if c:
                    last = c - 1
                    for n in range(2):
                        act.wait_ge(rotated, 4 * last + 2 * n + 2)
                        if last:
                            act.wait_ge(parts_out[n], 16 * last)
                        nc.scalar.activation(parts[n][:, 0, :], full[n][:], ACT.Copy).then_inc(high_ready, 1)
                    for n in range(2):
                        act.wait_ge(rest_ready, 2 * last + n + 1)
                        nc.scalar.activation(parts[n][:, 1, :], rest[n][:], ACT.Copy).then_inc(mid_ready, 1)

        @block.vector
        def _(dve):
            links = [0]

            def link(ins):
                links[0] += 1
                ins.then_inc(chain, 1)
                dve.wait_ge(chain, links[0])

            nc.vector.memset(kb[2 * HD:2 * HD + 1, :, :], 1.0)
            ln.vector_part(dve)
            link(nc.vector.tensor_tensor(rms[:], k.rstd[:], k.rstd[:], ALU.mult))
            link(nc.vector.tensor_tensor(rms[:], rms[:], k.var[:], ALU.mult))
            nc.vector.tensor_scalar(rms[:], rms[:], 1e-6, None, ALU.add).then_inc(scaled, 1)
            dve.wait_ge(rms_ready, 1)
            link(nc.vector.reciprocal(rms[:], rms[:]))
            nc.vector.tensor_tensor(h_scale[:], k.rstd[:], rms[:], ALU.mult)
            link(nc.vector.tensor_tensor(h_shift[:], k.shift[:], rms[:], ALU.mult))

            def normalise(c):
                if c:
                    dve.wait_ge(tr_done, c)
                for j in range(G):
                    at = c * G + j
                    ins = nc.vector.tensor_scalar(xn[:, j, :], x[:, at, :], h_scale[:, at:at + 1], h_shift[:, at:at + 1],
                                                  ALU.mult, ALU.add)
                ins.then_inc(xn_ready, 1)

            for c in range(NG + 1):
                if c == 0:
                    normalise(0)
                    normalise(1)
                else:
                    last = c - 1
                    dve.wait_ge(tables_in[last % 2], 32 * (last // 2 + 1))
                    if last:
                        dve.wait_ge(parts_ready, 2 * last)
                    for n, (w, mul) in enumerate(((P, scale), (KW, 1.0))):
                        dve.wait_ge(f_done, 2 * last + n + 1)
                        nc.vector.scalar_tensor_tensor(out=full[n][:], in0=f_ps[n][0:w, 0, :], scalar=mul,
                                                       in1=cos[last % 2][0:w, :], op0=ALU.mult, op1=ALU.mult)
                        nc.vector.scalar_tensor_tensor(out=rest[n][:], in0=f_ps[n][0:w, 1, :], scalar=mul,
                                                       in1=sin[last % 2][0:w, :], op0=ALU.mult, op1=ALU.mult).then_inc(rotated, 1)
                        dve.wait_ge(rotated, 4 * last + 2 * n + 1)
                        nc.vector.tensor_tensor(full[n][:], full[n][:], rest[n][:], ALU.add).then_inc(rotated, 1)
                    if c + 1 < NG:
                        normalise(c + 1)
                    for n in range(2):
                        dve.wait_ge(high_ready, 2 * last + n + 1)
                        dve.wait_ge(rotated, 4 * last + 2 * n + 2)
                        nc.vector.tensor_tensor(rest[n][:], full[n][:], parts[n][:, 0, :], ALU.subtract).then_inc(rest_ready, 1)
                    dve.wait_ge(v_done, last + 1)
                    nc.vector.tensor_copy(v[:, last * G:(last + 1) * G, :, 0:HD],
                                          v_ps[last % 2][:, 0:G * KW].rearrange("p (t h e) -> p t h e", t=G, e=HD)).then_inc(v_taken, 1)
                    for n in range(2):
                        dve.wait_ge(rest_ready, 2 * last + n + 1)
                        dve.wait_ge(mid_ready, 2 * last + n + 1)
                        nc.vector.tensor_tensor(parts[n][:, 2, :], rest[n][:], parts[n][:, 1, :], ALU.subtract).then_inc(parts_ready, 1)


def attention_attend(k, kept, q_parts, dram_r):
    nc, x, d, ka, kb, v = k.nc, k.x, k.dram, kept["ka"], kept["kb"], kept["v"]
    with stage(k), ExitStack() as ctx:
        sb = lambda shape, dt=F32: k.work.cut(shape, dt)
        sem = lambda n: nc.alloc_semaphore(f"at_{n}")
        ps = lambda shape: k.banks.cut(shape, align=512)
        SCANS, UNITS = G * NH, G * NKV
        EARLY = SCANS // 2
        w_o = sb([P, D])
        constants = sb([P, 4, P], BF16)
        ident16, tri16, triT16, zeros = (constants[:, n, :] for n in range(4))
        qa, qb = [sb([P, NH, GW], BF16) for u in range(2)], [sb([2 * HD + 1, NH, GW], BF16) for u in range(2)]
        tops = sb([P, G, NH, NG])
        top, top_row = sb([P, G * NH]), sb([G * NH, P], BF16)
        p = [sb([P, 2, GW]) for u in range(2)]
        sums = [sb([P, GW]) for kv in range(NKV)]
        inv = sb([P, NKV, 2, G])
        y = sums[0][:].rearrange("p (b h e) -> p b h e", b=G, h=NH)
        v_now = sb([P, G, NKV, HV])
        yT, r = sb([P, GW]), sb([P, G, D])
        tri, triT = r[:, 0, :], r[:, 1, :]
        s_ps = [ps([P, 2, GW]) for u in range(2)]
        acc = ps([P, NKV, GW])
        scan_ps = [ps([P, GW]) for u in range(2)]
        sums_q = [s_ps[kv][:, 1, :].rearrange("p (b h e) -> p h b e", b=G, h=2) for kv in range(NKV)]

        weights_in, q_in = sem("weights_in"), [sem(f"q_in{u}") for u in range(2)]
        constants_ready, tops_set = sem("constants_ready"), sem("tops_set")
        scan_done, scan_taken, top_ready = sem("scan_done"), sem("scan_taken"), sem("top_ready")
        top_done, top_copied, top_in = sem("top_done"), sem("top_copied"), sem("top_in")
        s_done, p_ready, p_used, chain = sem("s_done"), sem("p_ready"), sem("p_used"), sem("chain")
        v_copied, v_passed = sem("v_copied"), sem("v_passed")
        sums_copied, sums_tr_done = sem("sums_copied"), sem("sums_tr_done")
        y_ready, y_tr_done, yT_ready, o_done, o_taken, r_ready, r_out = (
            sem(n) for n in ("y_ready", "y_tr_done", "yT_ready", "o_done", "o_taken", "r_ready", "r_out"))
        block = ctx.enter_context(nc.Block())
        loads = [(w_o[:], d["at_w_o"]), (tri[:], d["at_tri"]), (triT[:], d["at_triT"])]

        def scans_before(c):
            return SCANS * c * (c + 1) // 2

        def units_before(c):
            return UNITS * c * (c + 1) // 2

        @block.sync
        def _(sp):
            def load_q(c):
                cols, u = slice(c * GW, (c + 1) * GW), c % 2
                for row, part in enumerate((0, 0, 0, 1)):
                    sp.dma_start(qa[u][row * HD:(row + 1) * HD, :, :],
                                 q_parts[part][:, cols].rearrange("(h r) t -> r h t", r=HD)).then_inc(q_in[u], 16)
                for row, part in enumerate((2, 1)):
                    sp.dma_start(qb[u][row * HD:(row + 1) * HD, :, :],
                                 q_parts[part][:, cols].rearrange("(h r) t -> r h t", r=HD)).then_inc(q_in[u], 16)

            def store_top(c):
                sp.wait_ge(top_copied, c + 1)
                sp.dma_start(qb[c % 2][2 * HD:2 * HD + 1, :, :], top_row[:]).then_inc(top_in, 16)

            load_q(0)
            for out, src in loads:
                sp.dma_start(out, src).then_inc(weights_in, 16)
            load_q(1)
            store_top(0)
            for c in range(NG):
                if c + 2 < NG:
                    sp.wait_ge(s_done, units_before(c + 1))
                    load_q(c + 2)
                if c + 1 < NG:
                    store_top(c + 1)
                sp.wait_ge(r_ready, c + 1)
                sp.dma_start(dram_r[c * GW:(c + 1) * GW, :].rearrange("(t p) d -> p t d", p=P), r[:]).then_inc(r_out, 16)
            sp.wait_ge(r_out, 16 * NG)

        @block.gpsimd
        def _(pool):
            nc.gpsimd.memset(zeros, 0.0).then_inc(constants_ready, 1)

            def copy_values(c, sc):
                for j in range(G):
                    at = units_before(c) + sc * UNITS + j * NKV
                    if is_later(at - UNITS + NKV):
                        pool.wait_ge(p_used, at - UNITS + NKV)
                    nc.gpsimd.tensor_copy(v_now[:, j, :, :], v[:, bass.ds(sc * G + j, 1), :, :]).then_inc(v_copied, 1)

            for c in range(NG):
                if c:
                    with pool.Fori(0, c) as sc:
                        copy_values(c, sc)
                copy_values(c, c)

        @block.tensor
        def _(pe):
            def scan(c, sc, n, diagonal=False):
                b, head = n // NH, n % NH
                at, width = scans_before(c) + sc * SCANS + n, (b + 1) * P if diagonal else GW
                if is_later(at - 1):
                    pe.wait_ge(scan_taken, at - 1)
                out = scan_ps[n % 2]
                ins = nc.tensor.matmul(out[:, 0:width], qa[c % 2][:, head, b * P:(b + 1) * P],
                                       ka[:, head // 2, bass.ds(sc * GW, width)], start=True, stop=not diagonal)
                if diagonal:
                    ins = nc.tensor.matmul(out[:, b * P:width], ident16, tri16, start=False, stop=True)
                ins.then_inc(scan_done, 1)

            def scores(c, sc, n, diagonal=False):
                j, kv = n // NKV, n % NKV
                at, lo = units_before(c) + sc * UNITS + n, j * P if diagonal else 0
                if is_later(at - 1):
                    pe.wait_ge(p_ready, at - 1)
                for h in range(2):
                    keys, head, out = bass.ds(sc * GW + j * P, P), kv * 2 + h, s_ps[kv][:, h, lo:GW]
                    nc.tensor.matmul(out, ka[:, kv, keys], qa[c % 2][:, head, lo:GW], start=True, stop=False)
                    ins = nc.tensor.matmul(out, kb[:, kv, keys], qb[c % 2][:, head, lo:GW], start=False, stop=not diagonal)
                    if diagonal:
                        ins = nc.tensor.matmul(s_ps[kv][:, h, lo:lo + P], ident16, triT16, start=False, stop=True)
                ins.then_inc(s_done, 1)

            def values(c, sc, n, diagonal=False):
                j, kv = n // NKV, n % NKV
                pe.wait_ge(p_ready, units_before(c) + sc * UNITS + n + 1)
                if kv == 0:
                    wait_apart(pe, v_copied, (units_before(c) + sc * UNITS) // NKV + j + 1, v_passed)
                lo = j * P if diagonal else 0
                for h in range(2):
                    ins = nc.tensor.matmul(acc[64 * h:64 * h + HV, kv, lo:GW], v_now[:, j, kv, :],
                                           p[kv][:, h, lo:GW], start=False, stop=diagonal and j == G - 1,
                                           skip_group_check=True)
                ins.then_inc(p_used, 1)

            def both_passes(c, sc, diagonal=False):
                def scans(first, count):
                    if c + 1 < NG:
                        for m in range(first, first + count):
                            scan(c + 1, sc + m // SCANS, m % SCANS, diagonal=m >= SCANS)

                per_unit = (SCANS + EARLY) // UNITS if diagonal else 2
                for n in range(UNITS):
                    scores(c, sc, n, diagonal)
                    scans(per_unit * n, 2)
                    if n:
                        values(c, sc, n - 1, diagonal)
                    scans(per_unit * n + 2, per_unit - 2)
                values(c, sc, UNITS - 1, diagonal)

            pe.wait_ge(q_in[0], 16 * 6)
            pe.wait_ge(constants_ready, 4)
            for n in range(SCANS):
                scan(0, 0, n, diagonal=True)
            pe.wait_ge(top_ready, 1)
            nc.tensor.transpose(s_ps[0][0:G * NH, 1, 0:P], top[:], k.ident[:]).then_inc(top_done, 1)
            for c in range(NG):
                if c:
                    pe.wait_ge(sums_copied, NKV * c)
                for kv in range(NKV):
                    nc.tensor.matmul(acc[:, kv, :], zeros, constants[:].rearrange("p n t -> p (n t)"), start=True, stop=False,
                                     skip_group_check=True)
                pe.wait_ge(top_in, 16 * (c + 1))
                if c:
                    pe.wait_ge(o_taken, c)
                if c + 1 < NG:
                    pe.wait_ge(q_in[(c + 1) % 2], 16 * 6 * ((c + 1) // 2 + 1))
                if c:
                    with pe.Fori(0, c) as sc:
                        both_passes(c, sc)
                both_passes(c, c, diagonal=True)
                for n in range(EARLY, SCANS):
                    if n == EARLY + 2:
                        pe.wait_ge(sums_copied, NKV * (c + 1))
                        for kv in range(NKV):
                            for b in range(G):
                                ins = nc.tensor.transpose(s_ps[kv][:, 1, b * P:(b + 1) * P], sums[kv][:, b * P:(b + 1) * P],
                                                          k.ident[:])
                        ins.then_inc(sums_tr_done, 1)
                    if n == EARLY + 4:
                        pe.wait_ge(y_ready, c + 1)
                        for b in range(G):
                            ins = nc.tensor.transpose(s_ps[0][:, 0, b * P:(b + 1) * P],
                                                      y[:, b, :, :].rearrange("p h e -> p (h e)"), k.ident[:])
                        ins.then_inc(y_tr_done, 1)
                    if c + 1 < NG:
                        scan(c + 1, c + 1, n, diagonal=True)
                if c + 1 < NG:
                    pe.wait_ge(top_ready, c + 2)
                    nc.tensor.transpose(s_ps[0][0:G * NH, 1, 0:P], top[:], k.ident[:]).then_inc(top_done, 1)
                pe.wait_ge(yT_ready, c + 1)
                for b in range(G):
                    ins = nc.tensor.matmul(s_ps[1][:, 0, b * P:(b + 1) * P], yT[:, b * P:(b + 1) * P], w_o[:],
                                           start=True, stop=True)
                ins.then_inc(o_done, 1)

        @block.scalar
        def _(act):
            def exps(c, sc, n, diagonal=False):
                j, kv = n // NKV, n % NKV
                at, lo = units_before(c) + sc * UNITS + n, j * P if diagonal else 0
                act.wait_ge(s_done, at + 1)
                if is_later(at - 1):
                    act.wait_ge(p_used, at - 1)
                nc.scalar.activation(p[kv][:, :, lo:GW], s_ps[kv][:, :, lo:GW], ACT.Exp).then_inc(p_ready, 1)

            def copy_top(c):
                act.wait_ge(top_done, c + 1)
                if c:
                    act.wait_ge(top_in, 16 * c)
                nc.scalar.activation(top_row[:], s_ps[0][0:G * NH, 1, 0:P], ACT.Copy, scale=-1.0).then_inc(top_copied, 1)

            act.wait_ge(weights_in, 16 * len(loads))
            nc.scalar.activation(ident16, k.ident[:], ACT.Copy).then_inc(constants_ready, 1)
            nc.scalar.activation(tri16, tri[:], ACT.Copy).then_inc(constants_ready, 1)
            nc.scalar.activation(triT16, triT[:], ACT.Copy).then_inc(constants_ready, 1)
            copy_top(0)
            for c in range(NG):
                if c:
                    with act.Fori(0, c) as sc:
                        for n in range(UNITS):
                            exps(c, sc, n)
                for n in range(UNITS):
                    exps(c, c, n, diagonal=True)
                act.wait_ge(p_used, units_before(c + 1))
                for kv in range(NKV):
                    nc.scalar.activation(sums[kv][:], acc[:, kv, :], ACT.Copy).then_inc(sums_copied, 1)
                act.wait_ge(y_tr_done, c + 1)
                nc.scalar.activation(yT[:], s_ps[0][:, 0, :], ACT.Copy).then_inc(yT_ready, 1)
                if c + 1 < NG:
                    copy_top(c + 1)

        @block.vector
        def _(dve):
            links = [0]

            def link(ins):
                links[0] += 1
                ins.then_inc(chain, 1)
                dve.wait_ge(chain, links[0])

            def greatest(c, sc, n, diagonal=False):
                b, head = n // NH, n % NH
                dve.wait_ge(scan_done, scans_before(c) + sc * SCANS + n + 1)
                nc.vector.tensor_reduce(tops[:, b, head, bass.ds(sc, 1)], scan_ps[n % 2][:, 0:(b + 1) * P if diagonal else GW],
                                        AX.X, ALU.max).then_inc(scan_taken, 1)

            def greatest_of_all(c):
                dve.wait_ge(scan_taken, scans_before(c + 1))
                if c:
                    dve.wait_ge(top_done, c)
                nc.vector.tensor_reduce(top[:].rearrange("p (h b) -> p b h", h=NH), tops[:], AX.X, ALU.max).then_inc(top_ready, 1)

            nc.vector.memset(tops[:], -1e30).then_inc(tops_set, 1)
            dve.wait_ge(tops_set, 1)
            for n in range(SCANS):
                greatest(0, 0, n, diagonal=True)
            greatest_of_all(0)
            for c in range(NG):
                if c + 1 < NG:
                    dve.wait_ge(top_ready, c + 1)
                    if c:
                        with dve.Fori(0, c) as sc:
                            for n in range(SCANS):
                                greatest(c + 1, sc, n)
                    for n in range(SCANS):
                        greatest(c + 1, c, n)
                for n in range(EARLY):
                    if c + 1 < NG:
                        greatest(c + 1, c + 1, n, diagonal=True)
                for n in range(EARLY, SCANS):
                    if n == EARLY + 2:
                        dve.wait_ge(sums_tr_done, c + 1)
                        for kv in range(NKV):
                            ins = nc.vector.reciprocal(inv[:, kv, :, :], sums_q[kv][:, :, :, HD])
                        link(ins)
                        for kv in range(NKV):
                            for h in range(2):
                                ins = nc.vector.tensor_tensor(y[:, :, kv * 2 + h, :], sums_q[kv][:, h, :, 0:HD],
                                                              inv[:, kv, h, :, None].to_broadcast([P, G, HD]), ALU.mult)
                        ins.then_inc(y_ready, 1)
                    if c + 1 < NG:
                        greatest(c + 1, c + 1, n, diagonal=True)
                if c + 1 < NG:
                    greatest_of_all(c + 1)
                if c:
                    dve.wait_ge(r_out, 16 * c)
                for j in range(G):
                    at = c * G + j
                    ins = nc.vector.tensor_scalar(r[:, j, :], x[:, at, :], k.rstd[:, at:at + 1], k.shift[:, at:at + 1],
                                                  ALU.mult, ALU.add)
                link(ins)
                dve.wait_ge(o_done, c + 1)
                link(nc.vector.tensor_tensor(r[:], r[:], s_ps[1][:, 0, :].rearrange("p (b d) -> p b d", b=G), ALU.add))
                dve.sem_inc(o_taken, 1)
                dve.sem_inc(r_ready, 1)
                xc = x[:, c * G:(c + 1) * G, :]
                nc.vector.tensor_tensor(xc, xc, r[:], ALU.add)
                for j in range(G):
                    nc.vector.bn_stats(k.stats[:, c * G + j:c * G + j + 1, :], r[:, j:j + 1, :])




def load_all(k):
    nc, parts = k.nc, 4
    with sublayer(k), ExitStack() as ctx:
        x_in = [nc.alloc_semaphore(f"x_in{n}") for n in range(parts)]
        ident_in = nc.alloc_semaphore("ident_in")
        block = ctx.enter_context(nc.Block())
        tiles = T // parts

        @block.sync
        def _(sp):
            for n in range(parts):
                at = slice(n * tiles, (n + 1) * tiles)
                sp.dma_start(k.x[:, at, :], k.dram["x"][n * tiles * P:(n + 1) * tiles * P, :].rearrange(
                    "(t p) d -> p t d", p=P)).then_inc(x_in[n], 16)
            sp.dma_start(k.ident[:], k.dram["ident"]).then_inc(ident_in, 16)
            sp.wait_ge(ident_in, 16)

        @block.vector
        def _(dve):
            nc.vector.memset(k.ones[:], 1.0)
            for n in range(parts):
                dve.wait_ge(x_in[n], 16)
                for at in range(n * tiles, (n + 1) * tiles):
                    tile_stats(k, slice(at, at + 1))


def store_all(k):
    nc = k.nc
    with ExitStack() as ctx:
        x_out = ctx.enter_context(nc.semaphore("x_out"))
        block = ctx.enter_context(nc.Block())

        @block.sync
        def _(sp):
            sp.dma_start(k.out.rearrange("(t p) d -> p t d", p=P), k.x[:]).then_inc(x_out, 16)
            sp.wait_ge(x_out, 16)


def program(nc, dram, out, first=0, last=8):
    with ExitStack() as ctx:
        k = Kernel(nc, dram)
        k.out = out
        sb = lambda n, shape, dt=F32: ctx.enter_context(nc.sbuf_tensor(n, shape, dt))
        k.mask = sb("mask", [P, T, N], U8)
        k.x = sb("x_sb", [P, T, D])
        k.ident, k.ones = sb("ident_sb", [P, P]), sb("ones_sb", [P, P])
        k.rstd, k.shift, k.var = sb("rstd", [P, T]), sb("shift", [P, T]), sb("var", [P, T])
        k.stats = sb("stats", [P, T, 6])
        k.work = Workspace(sb("work", [P, WORK]), WORK)
        k.banks = Workspace(ctx.enter_context(nc.psum_tensor("banks", [P, BANKS * 512], F32)), BANKS * 512)
        load_all(k)
        loaded = False
        for s in range(first, last):
            if s in (0, 2, 4, 6):
                gnn_layer(k, f"L{s // 2}g", {0: "elu", 2: "leaky", 4: "tanh", 6: "leaky"}[s], load_adj=not loaded)
                loaded = True
            elif s == 1:
                ffn0_layer(k)
            else:
                ffn_layer(k, s // 2)
        store_all(k)


def lay_out(w):
    c = np.ascontiguousarray
    a = {"x": w["x"], "adjT": c(w["adj"].T), "ident": np.eye(P, dtype=np.float32)}
    for n, W, vec in ((0, w["L0_gnn_W"], w["L0_gnn_a"]), (1, w["L1_gnn_W_w"], w["L1_gnn_a"]),
                      (3, w["L3_gnn_W"].T, w["L3_gnn_a_vec"])):
        a[f"L{n}g_W"], a[f"L{n}g_WT"] = c(W), c(W.T)
        a[f"L{n}g_a2"] = c(vec.reshape(2, D).T)
    a["L2g_W"], a["L2g_a_row"] = w["L2_gnn_W"], c(w["L2_gnn_a"].reshape(D))
    for n, b in ((1, w["L1_gnn_W_b"]), (2, w["L2_gnn_b"]), (3, w["L3_gnn_b_W"])):
        a[f"L{n}g_b_row"] = b
    for n, b in ((1, w["L1_gnn_W_b"]), (3, w["L3_gnn_b_W"])):
        a[f"L{n}g_b_col"] = c(b.reshape(D, 1))
    a["L3g_ba"] = w["L3_gnn_b_a"]
    def inward(W):
        return c(W.transpose(1, 0, 2))

    def outward(W):
        e, h, d = W.shape
        tiles = -(-h // P)
        return c(np.pad(W, ((0, 0), (0, tiles * P - h), (0, 0))).reshape(e, tiles, P, d).transpose(2, 0, 1, 3))

    def by_hidden(b):
        return c(b.reshape(b.shape[0], -1, P).transpose(2, 0, 1))

    a["L0f_w_in"], a["L0f_w_up"] = (c(w[f"L0_ffn_{n}"].transpose(2, 0, 1)) for n in ("w1", "w3"))
    a["L0f_w_out"] = outward(w["L0_ffn_w2"].transpose(0, 2, 1))
    a["L0f_r_w"], a["L0f_ln2"] = c(w["L0_ffn_router_w"].T), c(w["L0_ffn_ln2_w"].reshape(D, 1))
    halves = np.concatenate([np.arange(HD // 2, HD), np.arange(HD // 2)])

    def rotated(W):
        return c(W.reshape(-1, HD, D)[:, halves].reshape(-1, D).T)

    for n, W in (("q", w["L0_ffn_wq"]), ("k", w["L0_ffn_wk"])):
        a[f"at_w_{n}"], a[f"at_w_{n}r"] = c(W.T), rotated(W)
    a["at_w_v"], a["at_w_o"] = c(w["L0_ffn_wv"].T), c(w["L0_ffn_wo"].T)
    a["at_ln1"] = c(w["L0_ffn_ln1_w"].reshape(D, 1))
    inv_freq = 1.0 / 10000.0 ** (np.arange(0, HD, 2, dtype=np.float32) / HD)
    angle = np.outer(np.arange(N, dtype=np.float32), inv_freq)
    angle = np.concatenate([angle, angle], axis=-1)
    sign = np.where(np.arange(HD) < HD // 2, -1.0, 1.0).astype(np.float32)
    a["at_cos"] = c(np.tile(np.cos(angle).T, (NH, 1)).astype(np.float32))
    a["at_sin"] = c(np.tile((np.sin(angle) * sign).T, (NH, 1)).astype(np.float32))
    a["at_tri"] = np.where(np.arange(P)[None, :] <= np.arange(P)[:, None], 0.0, -1e30).astype(np.float32)
    a["at_triT"] = c(a["at_tri"].T)
    a["L1f_w_in"], a["L1f_w_mid"] = inward(w["L1_ffn_expert_w1"]), inward(w["L1_ffn_expert_w2"])
    a["L1f_w_out"] = outward(w["L1_ffn_expert_w3"])
    a["L1f_b_in"], a["L1f_b_mid"] = by_hidden(w["L1_ffn_expert_b1"]), c(w["L1_ffn_expert_b2"].T)
    a["L1f_b_out"] = w["L1_ffn_expert_b3"]
    a["L1f_r_w"], a["L1f_r_b"] = w["L1_ffn_router_w2"], w["L1_ffn_router_b2"]
    a["L1f_r_w1"], a["L1f_r_b1"] = w["L1_ffn_router_w1"], c(w["L1_ffn_router_b1"].reshape(-1, 1))
    for n in (2, 3):
        a[f"L{n}f_w_in"], a[f"L{n}f_w_out"] = inward(w[f"L{n}_ffn_W1"]), outward(w[f"L{n}_ffn_W2"])
        a[f"L{n}f_b_in"], a[f"L{n}f_b_out"] = by_hidden(w[f"L{n}_ffn_b1"]), w[f"L{n}_ffn_b2"]
        a[f"L{n}f_r_w"], a[f"L{n}f_r_b"] = w[f"L{n}_ffn_Wg"], w[f"L{n}_ffn_bg"]
    a["L2f_r_b2"] = w["L2_ffn_bias"]
    return a


def kernel(**inputs):
    import concourse.bacc as bacc
    from concourse.bass_utils import run_bass_kernel_spmd
    nc = bacc.Bacc("TRN2", target_bir_lowering=False, num_devices=1, dynamic_dma_scratch_size=1024)
    arrays, dram = {}, {}
    for name, a in lay_out({n: np.asarray(v) for n, v in inputs.items()}).items():
        arrays[f"in_{name}_dram"] = a
        dram[name] = nc.dram_tensor(f"in_{name}_dram", a.shape, mybir.dt.from_np(a.dtype), kind="ExternalInput").ap()
    out = nc.dram_tensor("out_0_dram", (N, D), F32, kind="ExternalOutput").ap()
    program(nc, dram, out)
    return run_bass_kernel_spmd(nc, [arrays], core_ids=[0]).results[0]["out_0_dram"]
```
